# Optimizing a Trainium2 kernel written in Bass

```python
import numpy as np
import jax
import jax.numpy as jnp

def _softmax(x, axis=-1):
    return jax.nn.softmax(x, axis=axis)

def _gelu(x):
    return jax.nn.gelu(x, approximate=True)

def _silu(x):
    return jax.nn.silu(x)

def _sigmoid(x):
    return jax.nn.sigmoid(x)

def _layernorm(x, axis=-1, eps=1e-05):
    m = jnp.mean(x, axis=axis, keepdims=True)
    v = jnp.var(x, axis=axis, keepdims=True)
    return (x - m) / jnp.sqrt(v + eps)

def _scatter_add(tgt, idx, src, axis=0):
    return tgt.at[idx].add(src)

def _segment_sum(src, seg, n):
    return jax.ops.segment_sum(src, seg, n)
kernel_name = 'mk_adaln_ffn_d4_seqx_r4_04f6e2'

def setup_inputs(seed: int=0):
    np.random.seed(seed)
    _w = jnp.asarray

    def _rec_inputs():
        import jax
        import jax.numpy as jnp
        _rk = jax.random.key(seed)
        x = -7.109e-05 + 0.9999 * jax.random.normal(jax.random.fold_in(_rk, 1), (2, 1024, 256), jnp.float32)
        _lenS = 1024 - jax.random.randint(jax.random.fold_in(_rk, 7), (2,), 0, max(1, 1024 // 4) + 1, jnp.int32)
        _lenS2 = 1024 - jax.random.randint(jax.random.fold_in(_rk, 8), (2,), 0, max(1, 1024 // 4) + 1, jnp.int32)
        itok_B_0_8 = jax.random.randint(jax.random.fold_in(_rk, 11), (2,), 0, 9, jnp.int32)
        itok_B_0_2 = jax.random.randint(jax.random.fold_in(_rk, 12), (2,), 0, 3, jnp.int32)
        itok_B_0_30 = jax.random.randint(jax.random.fold_in(_rk, 13), (2,), 0, 31, jnp.int32)
        itok_B_0_15 = jax.random.randint(jax.random.fold_in(_rk, 14), (2,), 0, 16, jnp.int32)
        return (x, itok_B_0_8, itok_B_0_2, itok_B_0_30, itok_B_0_15)
    x, itok_B_0_8, itok_B_0_2, itok_B_0_30, itok_B_0_15 = _rec_inputs()

    def _L0_cond_setup():
        import jax, jax.numpy as jnp
        import numpy as np
        LN_EPS = 1e-05
        key = jax.random.key(seed)
        ks = jax.random.split(key, 8)
        B, S, H, A, L = (32, 512, 256, 64, 10)
        return {'hidden_states': jax.random.normal(ks[0], (B, S, H), dtype=jnp.float32), 'language_ids': jax.random.randint(ks[1], (B,), 0, L, dtype=jnp.int64), 'W1': jax.random.normal(ks[2], (L, H, A), dtype=jnp.float32) * (1.0 / np.sqrt(H)), 'b1': jnp.zeros((L, A), dtype=jnp.float32), 'W2': jax.random.normal(ks[3], (L, A, H), dtype=jnp.float32) * (1.0 / np.sqrt(A)), 'b2': jnp.zeros((L, H), dtype=jnp.float32), 'gamma': jnp.ones((L, H), dtype=jnp.float32), 'beta': jnp.zeros((L, H), dtype=jnp.float32)}
    _L0_cond_all = _L0_cond_setup()
    _L0_cond_in = {k: v for k, v in _L0_cond_all.items() if k in ('W1', 'b1', 'W2', 'b2', 'gamma', 'beta')}
    del _L0_cond_all

    def _L0_ffn_setup():
        import jax, jax.numpy as jnp
        import numpy as np
        TOP_P = 0.8
        B, T, H, F, E = (2, 512, 256, 1024, 8)
        key = jax.random.key(seed)
        k0, k1, k2, k3 = jax.random.split(key, 4)
        x = jax.random.normal(k0, (B, T, H), jnp.float32)
        Wr = jax.random.normal(k1, (H, E), jnp.float32) * 0.02
        br = jnp.zeros((E,), jnp.float32)
        W1 = jax.random.normal(k2, (E, H, F), jnp.float32) * 0.02
        b1 = jnp.zeros((E, F), jnp.float32)
        W2 = jax.random.normal(k3, (E, F, H), jnp.float32) * 0.02
        b2 = jnp.zeros((E, H), jnp.float32)
        return {'x': x, 'Wr': Wr, 'br': br, 'W1': W1, 'b1': b1, 'W2': W2, 'b2': b2}
    _L0_ffn_all = _L0_ffn_setup()
    _L0_ffn_in = {k: v for k, v in _L0_ffn_all.items() if k in ('Wr', 'br', 'W1', 'b1', 'W2', 'b2')}
    del _L0_ffn_all

    def _L1_cond_setup():
        import jax, jax.numpy as jnp
        import numpy as np
        NEG_INF = -1e+30
        key = jax.random.key(seed)
        k1, k2, k3, k4, k5 = jax.random.split(key, 5)
        B, S, D, A = (16, 256, 256, 64)
        hidden = jax.random.normal(k1, (B, S, D), dtype=jnp.float32)
        W1 = jax.random.normal(k2, (D, A), dtype=jnp.float32) / np.sqrt(D)
        b1 = jax.random.normal(k3, (A,), dtype=jnp.float32) * 0.01
        v = jax.random.normal(k4, (A,), dtype=jnp.float32) / np.sqrt(A)
        prompt_type_ids = jax.random.randint(k5, (B,), 0, 3, dtype=jnp.int32)
        return {'hidden': hidden, 'W1': W1, 'b1': b1, 'v': v, 'prompt_type_ids': prompt_type_ids}
    _L1_cond_all = _L1_cond_setup()
    _L1_cond_in = {k: v for k, v in _L1_cond_all.items() if k in ('W1', 'b1', 'v')}
    del _L1_cond_all

    def _L1_ffn_setup():
        import jax, jax.numpy as jnp
        import numpy as np
        B, S, D, F, E = (4, 512, 256, 1024, 8)
        key = jax.random.key(seed)
        ks = jax.random.split(key, 7)
        s1 = 1.0 / np.sqrt(D)
        s2 = 1.0 / np.sqrt(F)
        x = jax.random.normal(ks[0], (B, S, D), dtype=jnp.float32)
        W1 = jax.random.uniform(ks[1], (E, D, F), jnp.float32, -s1, s1)
        b1 = jax.random.uniform(ks[2], (E, F), jnp.float32, -s1, s1)
        W2 = jax.random.uniform(ks[3], (E, F, D), jnp.float32, -s2, s2)
        b2 = jax.random.uniform(ks[4], (E, D), jnp.float32, -s2, s2)
        Wr = jax.random.uniform(ks[5], (D, E), jnp.float32, -s1, s1)
        br = jax.random.uniform(ks[6], (E,), jnp.float32, -s1, s1)
        return {'x': x, 'W1': W1, 'b1': b1, 'W2': W2, 'b2': b2, 'Wr': Wr, 'br': br}
    _L1_ffn_all = _L1_ffn_setup()
    _L1_ffn_in = {k: v for k, v in _L1_ffn_all.items() if k in ('W1', 'b1', 'W2', 'b2', 'Wr', 'br')}
    del _L1_ffn_all

    def _L2_cond_setup():
        import jax, jax.numpy as jnp
        import numpy as np
        C, I, O = (32, 256, 256)
        B, T = (64, 128)
        key = jax.random.key(seed)
        kx, kc, kw, kb = jax.random.split(key, 4)
        x = jax.random.normal(kx, (B, T, I), dtype=jnp.float32)
        cat_ids = jax.random.randint(kc, (B,), 0, C)
        W = 0.02 * jax.random.normal(kw, (C, I, O), dtype=jnp.float32)
        b = jnp.zeros((C, O), dtype=jnp.float32)
        return {'x': x, 'cat_ids': cat_ids, 'W': W, 'b': b}
    _L2_cond_all = _L2_cond_setup()
    _L2_cond_in = {k: v for k, v in _L2_cond_all.items() if k in ('W', 'b')}
    del _L2_cond_all

    def _L2_ffn_setup():
        import jax, jax.numpy as jnp
        import numpy as np
        B, T, E, C, H, G = (2, 512, 8, 256, 512, 16)
        key = jax.random.key(seed)
        ks = jax.random.split(key, 7)
        return {'hidden_states': jax.random.normal(ks[0], (B, T, C), jnp.float32), 'w_red': jax.random.normal(ks[1], (C, G), jnp.float32) * 0.02, 'wg': jax.random.normal(ks[2], (E, G), jnp.float32), 'W1': jax.random.normal(ks[3], (E, C, H), jnp.float32) * 0.02, 'b1': jax.random.normal(ks[4], (E, H), jnp.float32) * 0.02, 'W2': jax.random.normal(ks[5], (E, H, C), jnp.float32) * 0.02, 'b2': jax.random.normal(ks[6], (E, C), jnp.float32) * 0.02}
    _L2_ffn_all = _L2_ffn_setup()
    _L2_ffn_in = {k: v for k, v in _L2_ffn_all.items() if k in ('w_red', 'wg', 'W1', 'b1', 'W2', 'b2')}
    del _L2_ffn_all

    def _L3_cond_setup():
        import jax, jax.numpy as jnp
        import numpy as np
        INPUT_DIM = 256
        OUTPUT_DIM = 256
        NUM_CATEGORIES = 16
        B, S = (32, 128)
        key = jax.random.key(seed)
        kx, kw, kb, ki = jax.random.split(key, 4)
        k = 1.0 / np.sqrt(INPUT_DIM)
        x = jax.random.normal(kx, (B, S, INPUT_DIM), dtype=jnp.float32)
        weight = jax.random.uniform(kw, (NUM_CATEGORIES, INPUT_DIM, OUTPUT_DIM), dtype=jnp.float32, minval=-k, maxval=k)
        bias = jax.random.uniform(kb, (NUM_CATEGORIES, OUTPUT_DIM), dtype=jnp.float32, minval=-k, maxval=k)
        emb_ids = jax.random.randint(ki, (B,), 0, NUM_CATEGORIES, dtype=jnp.int64)
        return {'x': x, 'emb_ids': emb_ids, 'weight': weight, 'bias': bias}
    _L3_cond_all = _L3_cond_setup()
    _L3_cond_in = {k: v for k, v in _L3_cond_all.items() if k in ('weight', 'bias')}
    del _L3_cond_all

    def _L3_ffn_setup():
        import jax, jax.numpy as jnp
        import numpy as np
        H = 256
        E = 32
        I = 128
        TOP_K = 6
        IS = 256
        NORM_MIN = 1e-12
        B, S = (2, 256)
        key = jax.random.key(seed)
        ks = jax.random.split(key, 8)
        sc = 0.02
        return {'hidden_states': jax.random.normal(ks[0], (B, S, H), jnp.float32), 'router_weight': jax.random.normal(ks[1], (E, H), jnp.float32) * sc, 'e_score_bias': jnp.zeros((E,), jnp.float32), 'gate_up_proj': jax.random.normal(ks[2], (E, 2 * I, H), jnp.float32) * sc, 'down_proj': jax.random.normal(ks[3], (E, H, I), jnp.float32) * sc, 'shared_gate_w': jax.random.normal(ks[4], (IS, H), jnp.float32) * sc, 'shared_up_w': jax.random.normal(ks[5], (IS, H), jnp.float32) * sc, 'shared_down_w': jax.random.normal(ks[6], (H, IS), jnp.float32) * sc}
    _L3_ffn_all = _L3_ffn_setup()
    _L3_ffn_in = {k: v for k, v in _L3_ffn_all.items() if k in ('router_weight', 'e_score_bias', 'gate_up_proj', 'down_proj', 'shared_gate_w', 'shared_up_w', 'shared_down_w')}
    del _L3_ffn_all
    return {'x': x, 'itok_B_0_8': itok_B_0_8, 'itok_B_0_2': itok_B_0_2, 'itok_B_0_30': itok_B_0_30, 'itok_B_0_15': itok_B_0_15, 'L0_cond_W1': _L0_cond_in['W1'], 'L0_cond_b1': _L0_cond_in['b1'], 'L0_cond_W2': _L0_cond_in['W2'], 'L0_cond_b2': _L0_cond_in['b2'], 'L0_cond_gamma': _L0_cond_in['gamma'], 'L0_cond_beta': _L0_cond_in['beta'], 'L0_ffn_Wr': _L0_ffn_in['Wr'], 'L0_ffn_br': _L0_ffn_in['br'], 'L0_ffn_W1': _L0_ffn_in['W1'], 'L0_ffn_b1': _L0_ffn_in['b1'], 'L0_ffn_W2': _L0_ffn_in['W2'], 'L0_ffn_b2': _L0_ffn_in['b2'], 'L1_cond_W1': _L1_cond_in['W1'], 'L1_cond_b1': _L1_cond_in['b1'], 'L1_cond_v': _L1_cond_in['v'], 'L1_ffn_W1': _L1_ffn_in['W1'], 'L1_ffn_b1': _L1_ffn_in['b1'], 'L1_ffn_W2': _L1_ffn_in['W2'], 'L1_ffn_b2': _L1_ffn_in['b2'], 'L1_ffn_Wr': _L1_ffn_in['Wr'], 'L1_ffn_br': _L1_ffn_in['br'], 'L2_cond_W': _L2_cond_in['W'], 'L2_cond_b': _L2_cond_in['b'], 'L2_ffn_w_red': _L2_ffn_in['w_red'], 'L2_ffn_wg': _L2_ffn_in['wg'], 'L2_ffn_W1': _L2_ffn_in['W1'], 'L2_ffn_b1': _L2_ffn_in['b1'], 'L2_ffn_W2': _L2_ffn_in['W2'], 'L2_ffn_b2': _L2_ffn_in['b2'], 'L3_cond_weight': _L3_cond_in['weight'], 'L3_cond_bias': _L3_cond_in['bias'], 'L3_ffn_router_weight': _L3_ffn_in['router_weight'], 'L3_ffn_e_score_bias': _L3_ffn_in['e_score_bias'], 'L3_ffn_gate_up_proj': _L3_ffn_in['gate_up_proj'], 'L3_ffn_down_proj': _L3_ffn_in['down_proj'], 'L3_ffn_shared_gate_w': _L3_ffn_in['shared_gate_w'], 'L3_ffn_shared_up_w': _L3_ffn_in['shared_up_w'], 'L3_ffn_shared_down_w': _L3_ffn_in['shared_down_w']}

def reference(x, itok_B_0_8, itok_B_0_2, itok_B_0_30, itok_B_0_15, L0_cond_W1, L0_cond_b1, L0_cond_W2, L0_cond_b2, L0_cond_gamma, L0_cond_beta, L0_ffn_Wr, L0_ffn_br, L0_ffn_W1, L0_ffn_b1, L0_ffn_W2, L0_ffn_b2, L1_cond_W1, L1_cond_b1, L1_cond_v, L1_ffn_W1, L1_ffn_b1, L1_ffn_W2, L1_ffn_b2, L1_ffn_Wr, L1_ffn_br, L2_cond_W, L2_cond_b, L2_ffn_w_red, L2_ffn_wg, L2_ffn_W1, L2_ffn_b1, L2_ffn_W2, L2_ffn_b2, L3_cond_weight, L3_cond_bias, L3_ffn_router_weight, L3_ffn_e_score_bias, L3_ffn_gate_up_proj, L3_ffn_down_proj, L3_ffn_shared_gate_w, L3_ffn_shared_up_w, L3_ffn_shared_down_w):
    import jax
    import jax.numpy as jnp

    def _L0_cond_ref(hidden_states, language_ids, W1, b1, W2, b2, gamma, beta):
        import jax, jax.numpy as jnp
        import numpy as np
        LN_EPS = 1e-05
        w1 = W1[language_ids]
        w2 = W2[language_ids]
        h = jnp.einsum('bsh,bha->bsa', hidden_states, w1) + b1[language_ids][:, None, :]
        h = jax.nn.relu(h)
        adapted = jnp.einsum('bsa,bah->bsh', h, w2) + b2[language_ids][:, None, :]
        x = hidden_states + adapted
        mean = jnp.mean(x, axis=-1, keepdims=True)
        var = jnp.mean(jnp.square(x - mean), axis=-1, keepdims=True)
        normed = (x - mean) * jax.lax.rsqrt(var + LN_EPS)
        return normed * gamma[language_ids][:, None, :] + beta[language_ids][:, None, :]

    def _L0_ffn_ref(x, Wr, br, W1, b1, W2, b2):
        import jax, jax.numpy as jnp
        import numpy as np
        TOP_P = 0.8
        B, T, H, F, E = (2, 512, 256, 1024, 8)
        probs = jax.nn.softmax(x @ Wr + br, axis=-1)
        sorted_idx = jnp.argsort(-probs, axis=-1)
        sorted_probs = jnp.take_along_axis(probs, sorted_idx, axis=-1)
        cum = jnp.cumsum(sorted_probs, axis=-1)
        mask = cum < TOP_P
        mask = mask.at[..., 0].set(True)
        inv = jnp.argsort(sorted_idx, axis=-1)
        keep = jnp.take_along_axis(mask, inv, axis=-1)
        gate = probs * keep
        h = jax.nn.relu(jnp.einsum('bth,ehf->betf', x, W1) + b1[None, :, None, :])
        y = jnp.einsum('betf,efh->beth', h, W2) + b2[None, :, None, :]
        return jnp.einsum('bte,beth->bth', gate, y)

    def _L1_cond_ref(hidden, W1, b1, v, prompt_type_ids):
        import jax, jax.numpy as jnp
        import numpy as np
        NEG_INF = -1e+30
        B, S, D = hidden.shape
        attn_in = jnp.tanh(jnp.einsum('bsd,da->bsa', hidden, W1) + b1)
        scores = jnp.einsum('bsa,a->bs', attn_in, v)
        idx = jnp.arange(S)
        j = idx[:, None]
        l = idx[None, :]
        prefix_m = l <= j
        postfix_m = l >= j
        cloze_m = l != j
        pt = prompt_type_ids[:, None, None]
        mask = jnp.where(pt == 0, prefix_m[None], jnp.where(pt == 1, postfix_m[None], cloze_m[None]))
        masked_scores = jnp.where(mask, scores[:, None, :], NEG_INF)
        p = jax.nn.softmax(masked_scores, axis=-1)
        cnt = jnp.sum(mask, axis=-1).astype(hidden.dtype)
        pooled = jnp.einsum('bjl,bld->bjd', p, hidden) / cnt[..., None]
        return pooled

    def _L1_ffn_ref(x, W1, b1, W2, b2, Wr, br):
        import jax, jax.numpy as jnp
        import numpy as np
        B, S, D, F, E = (4, 512, 256, 1024, 8)
        b, s, d = x.shape
        e = Wr.shape[1]
        logits = x @ Wr + br
        idx = jnp.argmax(logits, axis=-1)
        probs = jax.nn.softmax(logits, axis=-1)
        gates = jnp.take_along_axis(probs, idx[..., None], axis=-1)[..., 0]
        xf = x.reshape(-1, d)
        idxf = idx.reshape(-1)
        gf = gates.reshape(-1)
        out = jnp.zeros_like(xf)
        for ei in range(e):
            h = jax.nn.gelu(xf @ W1[ei] + b1[ei], approximate=False)
            y = h @ W2[ei] + b2[ei]
            mask = (idxf == ei).astype(xf.dtype)
            out = out + y * (gf * mask)[:, None]
        return out.reshape(b, s, d)

    def _L2_cond_ref(x, cat_ids, W, b):
        import jax, jax.numpy as jnp
        import numpy as np
        C, I, O = (32, 256, 256)
        B, T = (64, 128)
        selected_W = W[cat_ids]
        selected_b = b[cat_ids]
        if x.ndim == 2:
            return jnp.einsum('bi,bio->bo', x, selected_W) + selected_b
        return jnp.einsum('bti,bio->bto', x, selected_W) + selected_b[:, None, :]

    def _L2_ffn_ref(hidden_states, w_red, wg, W1, b1, W2, b2):
        import jax, jax.numpy as jnp
        import numpy as np
        B, T, E, C, H, G = (2, 512, 8, 256, 512, 16)
        b, t, c = hidden_states.shape
        x = hidden_states.reshape(-1, c)
        x_red = x @ w_red
        wg_n = wg / jnp.maximum(jnp.linalg.norm(wg, axis=1, keepdims=True), 0.0001)
        logits = x_red @ wg_n.T
        gates = jax.nn.softmax(logits, axis=1)
        scores = jnp.max(gates, axis=1)
        idx = jnp.argmax(gates, axis=1)
        h = jnp.einsum('nc,ech->neh', x, W1) + b1[None]
        h = jnp.take_along_axis(h, idx[:, None, None], axis=1)[:, 0, :]
        h = jax.nn.gelu(h, approximate=False)
        o = jnp.einsum('nh,ehc->nec', h, W2) + b2[None]
        o = jnp.take_along_axis(o, idx[:, None, None], axis=1)[:, 0, :]
        o = o * scores[:, None]
        return o.reshape(b, t, c)

    def _L3_cond_ref(x, emb_ids, weight, bias):
        import jax, jax.numpy as jnp
        import numpy as np
        INPUT_DIM = 256
        OUTPUT_DIM = 256
        NUM_CATEGORIES = 16
        B, S = (32, 128)
        ids = emb_ids.reshape(-1).astype(jnp.int32)
        w = weight[ids]
        b = bias[ids]
        return jnp.einsum('bsi,bij->bsj', x, w) + b[:, None, :]

    def _L3_ffn_ref(hidden_states, router_weight, e_score_bias, gate_up_proj, down_proj, shared_gate_w, shared_up_w, shared_down_w):
        import jax, jax.numpy as jnp
        import numpy as np
        H = 256
        E = 32
        I = 128
        TOP_K = 6
        IS = 256
        NORM_MIN = 1e-12
        B, S = (2, 256)
        b, s, h = hidden_states.shape
        x = hidden_states.reshape(-1, h)
        T = x.shape[0]
        shared_out = jax.nn.silu(x @ shared_gate_w.T) * (x @ shared_up_w.T) @ shared_down_w.T
        xf = x.astype(jnp.float32)
        router_logits = xf @ router_weight.T
        routing_weights = jax.nn.softmax(router_logits, axis=-1)
        corrected = routing_weights + e_score_bias
        _, top_idx = jax.lax.top_k(corrected, TOP_K)
        top_w = jnp.take_along_axis(routing_weights, top_idx, axis=-1)
        top_w = top_w / jnp.clip(top_w.sum(axis=-1, keepdims=True), NORM_MIN)
        top_w = top_w.astype(x.dtype)
        combine = jnp.zeros((T, E), x.dtype).at[jnp.arange(T)[:, None], top_idx].add(top_w)
        gu = jnp.einsum('th,eih->tei', x, gate_up_proj)
        gate, up = jnp.split(gu, 2, axis=-1)
        hmid = jax.nn.silu(gate) * up
        y = jnp.einsum('tei,ehi->teh', hmid, down_proj)
        out = jnp.einsum('teh,te->th', y, combine) + shared_out
        return out.reshape(b, s, h)
    x = x + _L0_ffn_ref(_L0_cond_ref(x, itok_B_0_8, L0_cond_W1, L0_cond_b1, L0_cond_W2, L0_cond_b2, L0_cond_gamma, L0_cond_beta), L0_ffn_Wr, L0_ffn_br, L0_ffn_W1, L0_ffn_b1, L0_ffn_W2, L0_ffn_b2)
    x = x + _L1_ffn_ref(_L1_cond_ref(x, L1_cond_W1, L1_cond_b1, L1_cond_v, itok_B_0_2), L1_ffn_W1, L1_ffn_b1, L1_ffn_W2, L1_ffn_b2, L1_ffn_Wr, L1_ffn_br)
    x = x + _L2_ffn_ref(_L2_cond_ref(x, itok_B_0_30, L2_cond_W, L2_cond_b), L2_ffn_w_red, L2_ffn_wg, L2_ffn_W1, L2_ffn_b1, L2_ffn_W2, L2_ffn_b2)
    x = x + _L3_ffn_ref(_L3_cond_ref(x, itok_B_0_15, L3_cond_weight, L3_cond_bias), L3_ffn_router_weight, L3_ffn_e_score_bias, L3_ffn_gate_up_proj, L3_ffn_down_proj, L3_ffn_shared_gate_w, L3_ffn_shared_up_w, L3_ffn_shared_down_w)
    return x

_drawn_inputs = setup_inputs


def setup_inputs(seed=0):
    import zlib

    import numpy as np

    out = dict(_drawn_inputs(seed))
    spreads = {'L0_cond_b1': (0.0, 0.1),
     'L0_cond_b2': (0.0, 0.1),
     'L0_cond_gamma': (1.0, 0.2),
     'L0_cond_beta': (0.0, 0.1),
     'L0_ffn_br': (0.0, 0.1),
     'L0_ffn_b1': (0.0, 0.1),
     'L0_ffn_b2': (0.0, 0.1),
     'L2_cond_b': (0.0, 0.1),
     'L3_ffn_e_score_bias': (0.0, 0.1)}
    factors = {}
    for name, (base, spread) in spreads.items():
        noise = np.random.default_rng([zlib.crc32(name.encode()), seed]).standard_normal(out[name].shape)
        drawn = base * np.exp(spread * noise) if base else spread * noise
        out[name] = jnp.asarray(drawn.astype(out[name].dtype))
    for name, factor in factors.items():
        out[name] = (out[name] * factor).astype(out[name].dtype)
    return out
```

```python
import concourse.bass as bass
from concourse import mybir
from contextlib import ExitStack

F32 = mybir.dt.float32
F32R = mybir.dt.float32r
I32 = mybir.dt.int32
ALU = mybir.AluOpType
ACT = mybir.ActivationFunctionType
AX = mybir.AxisListType

P = 128
B, SEQ, D = 2, 1024, 256
NT = B * SEQ // P
TPB = SEQ // P
CH = 512
NC = B * SEQ // CH
TPC = CH // P
KD = D // P
A0 = 64
GR = 16
SUB = 512
FB = SUB // P
LN_EPS = 1e-5
TOP_P = 0.8
TOP_K = 6
NEG = -1e30
LAYERS = [(8, 1024, ACT.Relu), (8, 1024, ACT.Gelu), (8, 512, ACT.Gelu)]
E3 = 32
E3S = 34
PW = D + 2


def build(nc, t):
    with ExitStack() as ctx:
        def sb(name, shape, dt=F32):
            return ctx.enter_context(nc.sbuf_tensor(name, shape, dt))

        def sem(name):
            return ctx.enter_context(nc.semaphore(name))

        X = sb("x_tok", [P, NT, D])
        Z = sb("z_tok", [P, NT, D])
        TAh = sb("featA_hi", [P, KD, NT * P], F32R)
        TAl = sb("featA_lo", [P, KD, NT * P], F32R)
        TBh = sb("featB_hi", [P, NT * PW], F32R)
        TBl = sb("featB_lo", [P, NT * PW], F32R)
        TBhv = TBh[:, 0:KD * NT * P].rearrange("p (k n) -> p k n", k=KD)
        TBlv = TBl[:, 0:KD * NT * P].rearrange("p (k n) -> p k n", k=KD)
        XRh = TBh[:].rearrange("p (t w) -> p t w", t=NT)
        XRl = TBl[:].rearrange("p (t w) -> p t w", t=NT)
        W1r = sb("w1_raw", [P, KD * SUB])
        W2r = sb("w2_raw", [P, FB * D])
        W1h = sb("w1_hi", [P, 2, KD * SUB], F32R)
        W1l = sb("w1_lo", [P, 2, KD * SUB], F32R)
        W2h = sb("w2_hi", [P, 2, FB * D], F32R)
        W2l = sb("w2_lo", [P, 2, FB * D], F32R)
        HF = sb("hidden_f32", [P, FB, CH])
        HTh = sb("hidden_hi", [P, 2, FB, CH], F32R)
        HTl = sb("hidden_lo", [P, 2, FB, CH], F32R)
        SC = sb("scratch", [P, 8, CH])
        G = sb("gates", [P, NT, E3S + 1])
        IO = sb("iota_f32", [P, 64])
        IOi = sb("iota_int", [P, 64], I32)
        L3W = sb("list3_weights", [1, 64], I32)
        L3G = sb("list3_gates", [1, 64], I32)
        ident = sb("ident", [P, P])
        IDS = sb("ids", [1, 8], I32)
        MODEi = sb("mode_int", [P, B], I32)
        B1 = [sb(f"b1_{L}", [P, LAYERS[L][0] * LAYERS[L][1] // P]) for L in range(3)]
        BS = sb("b1_step", [P, 3 * FB])
        B2 = [sb(f"b2_{L}", [LAYERS[L][0], D]) for L in range(3)]
        BR = [sb("br_0", [P, 8]), sb("br_1", [P, 8]), None, sb("br_3", [P, E3])]
        CB0 = sb("cond0_b1", [A0, B])
        CB1 = sb("cond1_b1", [A0, 1])
        CB2 = sb("cond2_b", [P, B, KD])
        CB3 = sb("cond3_b", [P, B, KD])
        V1 = sb("cond1_v", [A0, 1])
        RW = [GR if L == 2 else 8 if L < 2 else E3 for L in range(4)]
        Rr = [sb(f"router_raw{L}", [P, KD, RW[L]]) for L in range(4)]
        Rh = [sb(f"router_hi{L}", [P, KD, RW[L]], F32R) for L in range(4)]
        Rl = [sb(f"router_lo{L}", [P, KD, RW[L]], F32R) for L in range(4)]
        WG = sb("wg", [8, 3 * GR])
        WGT = sb("wg_t", [GR, 8])
        ST = sb("stats", [P, 6])
        MV = sb("mean_var", [P, NT, 2])
        SM = sb("small", [P, 8, NT])
        JC = sb("j_col", [P, TPB])
        JCi = sb("j_col_int", [P, TPB], I32)
        MD = sb("mode", [P, B, 8])
        DM = sb("diag_mask", [P, B, P])
        TM = sb("tri", [P, 3, P])
        RS = sb("reset", [P, CH])
        ONE = sb("ones", [P, P])
        PS = ctx.enter_context(nc.psum_tensor("ps", [P, 8, CH], F32))

        s_x = [sem(f"x_in{c}") for c in range(NC)]
        s_ids = sem("ids_in")
        s_small = sem("small_in")
        N_SMALL = 22
        s_mode = sem("mode_in")
        s_rows = sem("rows_in")
        s_craw = [sem(f"cond_raw{L}") for L in range(4)]
        s_csplit = [sem(f"cond_split{L}") for L in range(4)]
        s_const0 = sem("const_fill")
        s_const = sem("const")
        s_rsplit = sem("router_split")
        s_dve = sem("dve_step")
        s_act = sem("act_step")
        s_pool = sem("pool_step")
        TR = ["x0", "z0", "x1", "z1", "x2", "x3"]
        s_tps = {n: sem(f"tr_ps_{n}") for n in TR}
        s_thi = {n: sem(f"tr_hi_{n}") for n in TR}
        s_tlo = {n: sem(f"tr_lo_{n}") for n in TR}
        s_ch = {L: sem(f"cond_h{L}") for L in range(4)}
        s_chf = {L: sem(f"cond_hf{L}") for L in range(4)}
        s_chi = {L: sem(f"cond_hi{L}") for L in range(4)}
        s_clo = {L: sem(f"cond_lo{L}") for L in range(4)}
        s_cy = sem("cond0_y")
        s_cyf = sem("cond0_y_used")
        s_var = sem("ln_var")
        s_std = sem("ln_std")
        s_norm = sem("ln_norm")
        s_z0 = sem("z0_tile")
        s_sc = sem("score_ps")
        s_sc_sb = sem("score_row")
        s_xr = sem("pool_rhs")
        s_arg = sem("pool_arg")
        s_pf = sem("pool_p")
        s_phi = sem("pool_hi")
        s_plo = sem("pool_lo")
        s_pmm = sem("pool_mm")
        s_den = sem("pool_den")
        s_z1 = sem("z1_tile")
        s_lg = [sem(f"logits{L}") for L in range(4)]
        s_sub = [sem(f"logits_shifted{L}") for L in range(4)]
        s_exp = [sem(f"logits_exp{L}") for L in range(4)]
        s_gate = [sem(f"gates{L}") for L in range(4)]
        s_gt = [sem(f"gates_t_ps{L}") for L in range(3)]
        s_gts = [sem(f"gates_t{L}") for L in range(3)]
        s_by = [sem(f"bias_y{L}") for L in range(3)]
        s_bu = [sem(f"bias_used{L}") for L in range(3)]
        s_red = sem("reduced_ps")
        s_reds = sem("reduced")
        s_wgn = sem("wg_norm")
        s_wgt = sem("wg_t_ps")
        s_wgs = sem("wg_t_sb")
        s_ss = sem("wg_sumsq")
        s_sq = sem("wg_root")
        s_wraw = [sem(f"w_raw{L}") for L in range(4)]
        s_wsplit = [sem(f"w_split{L}") for L in range(4)]
        s_whi = [sem(f"w_hi{L}") for L in range(4)]
        s_hps = [sem(f"h_ps{L}") for L in range(4)]
        s_b1 = [sem(f"b1_step{L}") for L in range(3)]
        s_hf3 = sem("silu3")
        s_hm3 = sem("hmid3")
        s_hhi = [sem(f"h_hi{L}") for L in range(4)]
        s_hlo = [sem(f"h_lo{L}") for L in range(4)]
        s_y = [sem(f"y_ps{L}") for L in range(4)]
        s_yfree = [sem(f"y_free{L}") for L in range(4)]
        s_cnt3 = sem("counts3_in")
        s_cnt3p = sem("counts3_ps")
        s_list3 = sem("list3")
        s_done3 = sem("layer3_done")
        s_out = sem("out_stored")

        NSUB = [LAYERS[L][0] * LAYERS[L][1] // SUB for L in range(3)]
        NSUB.append(E3S)
        FEAT = [(TBhv, TBlv), (TAh, TAl), (TAh, TAl), (TAh, TAl)]
        YC = 2 * TPC
        STEPS3 = E3S // 2
        UPI = 2 * NC

        block = ctx.enter_context(nc.Block())

        @block.sync
        def _(sp):
            sp.dma_start(IDS[0:1, 0:8], t["ids"]).then_inc(s_ids, 16)
            for c in range(NC):
                sp.dma_start(X[:, c * TPC:(c + 1) * TPC, :],
                             t["x"].rearrange("b (t p) d -> p (b t) d", p=P)[:, c * TPC:(c + 1) * TPC, :]
                             ).then_inc(s_x[c], 16)
            sp.wait_ge(s_ids, 16)
            lang = [sp.value_load(IDS[0:1, b:b + 1], min_val=0, max_val=9) for b in range(B)]
            for b in range(B):
                sp.dma_start(W1r[:, b * KD * A0:(b + 1) * KD * A0].rearrange("p (k a) -> p k a", k=KD),
                             t["L0_cond_W1"][bass.ds(lang[b], 1), :, :].rearrange("o (k p) a -> p (o k) a", p=P)
                             ).then_inc(s_craw[0], 16)
                sp.dma_start(W1r[0:A0, 256 + b * D:256 + (b + 1) * D],
                             t["L0_cond_W2"][bass.ds(lang[b], 1), :, :].rearrange("o a d -> a (o d)")
                             ).then_inc(s_craw[0], 16)
            for b in range(B):
                for n, name in enumerate(("L0_cond_b2", "L0_cond_gamma", "L0_cond_beta")):
                    sp.dma_start(HF[:, n, b * D:(b + 1) * D],
                                 t[name][bass.ds(lang[b], 1), :].broadcast_to([P, D])).then_inc(s_rows, 16)
                sp.dma_start(CB0[:, b:b + 1], t["L0_cond_b1"][bass.ds(lang[b], 1), :].rearrange("o a -> a o")).then_inc(s_small, 16)
            for L, name in enumerate(("L0_ffn_Wr", "L1_ffn_Wr", "L2_ffn_w_red", "L3_router_t")):
                sp.dma_start(Rr[L][:], t[name].rearrange("(k p) e -> p k e", p=P)).then_inc(s_small, 16)
            sp.dma_start(BR[0][:], t["L0_ffn_br"].unsqueeze(0).broadcast_to([P, 8])).then_inc(s_small, 16)
            sp.dma_start(BR[1][:], t["L1_ffn_br"].unsqueeze(0).broadcast_to([P, 8])).then_inc(s_small, 16)
            sp.dma_start(BR[3][:], t["L3_ffn_e_score_bias"].unsqueeze(0).broadcast_to([P, E3])).then_inc(s_small, 16)
            for L in range(3):
                sp.dma_start(B1[L][:], t[f"L{L}_b1_t"]).then_inc(s_small, 16)
                sp.dma_start(B2[L][:], t[f"L{L}_ffn_b2"]).then_inc(s_small, 16)
            sp.dma_start(CB1[:], t["L1_cond_b1"].unsqueeze(1)).then_inc(s_small, 16)
            sp.dma_start(V1[:], t["L1_cond_v"].unsqueeze(1)).then_inc(s_small, 16)
            sp.dma_start(WG[:, 0:GR], t["L2_ffn_wg"]).then_inc(s_small, 16)
            cat = [sp.value_load(IDS[0:1, 4 + b:5 + b], min_val=0, max_val=31) for b in range(B)]
            emb = [sp.value_load(IDS[0:1, 6 + b:7 + b], min_val=0, max_val=15) for b in range(B)]
            for b in range(B):
                sp.dma_start(CB2[:, b, :], t["L2_cond_b"][:, bass.ds(cat[b], 1), :].rearrange("p o k -> p (o k)")
                             ).then_inc(s_small, 16)
                sp.dma_start(CB3[:, b, :], t["L3_cond_b"][:, bass.ds(emb[b], 1), :].rearrange("p o k -> p (o k)")
                             ).then_inc(s_small, 16)

            def sub_weights(L, s):
                if L < 3:
                    sp.dma_start(W1r[:], t[f"L{L}_w1"][bass.ds(s, 1)].rearrange("o p f -> p (o f)")).then_inc(s_wraw[L], 16)
                    sp.dma_start(W2r[:], t[f"L{L}_w2"][bass.ds(s, 1)].rearrange("o p f -> p (o f)")).then_inc(s_wraw[L], 16)
                else:
                    sp.dma_start(W1r[:, 0:KD * D], t["L3_w1"][bass.ds(s, 1)].rearrange("o p f -> p (o f)")
                                 ).then_inc(s_wraw[L], 16)
                    sp.dma_start(W2r[:, 0:D], t["L3_w2"][bass.ds(s, 1)].rearrange("o p f -> p (o f)")
                                 ).then_inc(s_wraw[L], 16)

            for L in range(4):
                sp.wait_ge(s_csplit[L], 1)
                if L == 3:
                    sub_weights(3, E3)
                    sp.wait_ge(s_list3, 1)
                    steps = sp.value_load(L3G[0:1, 63:64], min_val=1, max_val=STEPS3)
                    with sp.Fori(1, E3S) as s:
                        with sp.If(s < steps * 2):
                            e = sp.value_load(L3W[0:1, bass.ds(s, 1)], min_val=0, max_val=E3S - 1)
                            sp.wait_ge(s_wsplit[3], s)
                            sub_weights(3, e)
                    break
                sub_weights(L, 0)
                with sp.Fori(1, NSUB[L]) as s:
                    sp.wait_ge(s_wsplit[L], s)
                    sub_weights(L, s)
                sp.wait_ge(s_wsplit[L], NSUB[L])
                if L == 0:
                    sp.dma_start(W1r[:, 0:KD * A0].rearrange("p (k a) -> p k a", k=KD),
                                 t["L1_cond_W1"].rearrange("(k p) a -> p k a", p=P)).then_inc(s_craw[1], 16)
                if L in (1, 2):
                    row = cat if L == 1 else emb
                    for b in range(B):
                        sp.dma_start(W1r[:, b * KD * D:(b + 1) * KD * D].rearrange("p (k d) -> p k d", k=KD),
                                     t["L2_cond_W" if L == 1 else "L3_cond_weight"][bass.ds(row[b], 1), :, :]
                                     .rearrange("o (k p) d -> p (o k) d", p=P)).then_inc(s_craw[L + 1], 16)
            sp.wait_ge(s_done3, 1)
            for c in range(NC):
                sp.dma_start(t["out"].rearrange("b (t p) d -> p (b t) d", p=P)[:, c * TPC:(c + 1) * TPC, :],
                             X[:, c * TPC:(c + 1) * TPC, :]).then_inc(s_out, 16)
            sp.wait_ge(s_out, 16 * NC)

        @block.gpsimd
        def _(gp):
            gp.dma_start(MODEi[:], t["L1_mode"].unsqueeze(0).broadcast_to([P, B])).then_inc(s_mode, 16)
            gp.memset(ident[:], 0.0).then_inc(s_const0, 1)
            gp.memset(TM[:], 1.0).then_inc(s_const0, 1)
            gp.memset(RS[:], 1.0).then_inc(s_const0, 1)
            gp.memset(ONE[:], 1.0).then_inc(s_const, 1)
            gp.iota(JCi[:], [[P, TPB]], base=0, channel_multiplier=1).then_inc(s_const, 1)
            gp.iota(IOi[:], [[1, 64]], base=0, channel_multiplier=0).then_inc(s_const, 1)
            gp.wait_ge(s_const0, 3)
            gp.affine_select(out=ident[:], in_=ident[:], compare_op=ALU.not_equal, fill=1.0, base=0,
                             pattern=[[-1, P]], channel_multiplier=1).then_inc(s_const, 1)
            gp.affine_select(out=TM[:, 0, :], in_=TM[:, 0, :], compare_op=ALU.is_ge, fill=0.0, base=0,
                             pattern=[[1, P]], channel_multiplier=-1).then_inc(s_const, 1)
            gp.affine_select(out=TM[:, 1, :], in_=TM[:, 1, :], compare_op=ALU.is_ge, fill=0.0, base=0,
                             pattern=[[-1, P]], channel_multiplier=1).then_inc(s_const, 1)
            gp.affine_select(out=TM[:, 2, :], in_=TM[:, 2, :], compare_op=ALU.not_equal, fill=0.0, base=0,
                             pattern=[[-1, P]], channel_multiplier=1).then_inc(s_const, 1)
            gp.wait_ge(s_rows, 16 * 3 * B)
            for n in range(NT):
                b = n // TPB
                gp.wait_ge(s_norm, n + 1)
                gp.tensor_tensor(Z[:, n, :], Z[:, n, :], HF[:, 1, b * D:(b + 1) * D], ALU.mult).then_inc(s_pool, 1)
                gp.wait_ge(s_pool, n + 1)
                gp.tensor_tensor(Z[:, n, :], Z[:, n, :], HF[:, 2, b * D:(b + 1) * D], ALU.add).then_inc(s_z0, 1)

        @block.tensor
        def _(pe):
            def mm3(out, lh, ll, rh, rl, first, last):
                nc.tensor.matmul(out, lh, rh, start=first, stop=False)
                nc.tensor.matmul(out, lh, rl, start=False, stop=False)
                return nc.tensor.matmul(out, ll, rh, start=False, stop=last)

            def transposes(n, src, ready):
                for c in range(NC):
                    ready(c)
                    for k in range(KD):
                        g = KD * c + k
                        if g >= 4:
                            pe.wait_ge(s_tlo[n], g - 3)
                        for j in range(TPC):
                            last = nc.tensor.transpose(PS[:, g % 4, j * P:(j + 1) * P],
                                                       src[:, c * TPC + j, k * P:(k + 1) * P], ident[:])
                        last.then_inc(s_tps[n], 1)

            def routing(L, wait_feat):
                fh, fl = FEAT[L]
                E = RW[L]
                for n in range(NT):
                    if n % TPC == 0:
                        wait_feat(n // TPC)
                    for k in range(KD):
                        last = mm3(PS[:, 4, n * E:(n + 1) * E], fh[:, k, n * P:(n + 1) * P],
                                   fl[:, k, n * P:(n + 1) * P], Rh[L][:, k, :], Rl[L][:, k, :], k == 0, k == KD - 1)
                last.then_inc(s_lg[L], 1)

            def bias(L):
                E = LAYERS[L][0]
                pe.wait_ge(s_gate[L], 1)
                for n in range(NT):
                    last = nc.tensor.transpose(PS[0:E, n // TPC, (n % TPC) * P:(n % TPC + 1) * P],
                                               G[:, n, 0:E], ident[:])
                last.then_inc(s_gt[L], 1)
                pe.wait_ge(s_gts[L], 1)
                for n in range(NT):
                    if n >= 4:
                        pe.wait_ge(s_bu[L], n - 3)
                    nc.tensor.matmul(PS[:, 4 + n % 4, 0:D], SC[0:E, 4 + n // TPC, (n % TPC) * P:(n % TPC + 1) * P],
                                     B2[L][:], start=True, stop=True).then_inc(s_by[L], 1)
                pe.wait_ge(s_bu[L], NT)

            def ffn(L):
                fh, fl = FEAT[L]

                def hidden(q, u):
                    s, c = (u // NC) % 2, u % NC
                    for f in range(FB):
                        if f == 0 and c == 0:
                            pe.wait_ge(s_wsplit[L], (q + NC) // NC if isinstance(q, int) else q[0] * 2 + u // NC + 1)
                        if not (isinstance(q, int) and q == 0):
                            pe.wait_ge(s_hhi[L], FB * (q[0] * UPI + u - 1) + f + 1)
                        for k in range(KD):
                            w = slice(k * SUB + f * P, k * SUB + (f + 1) * P)
                            last = mm3(PS[:, f, :], W1h[:, s, w], W1l[:, s, w],
                                       fh[:, k, c * CH:(c + 1) * CH], fl[:, k, c * CH:(c + 1) * CH],
                                       k == 0, k == KD - 1)
                        last.then_inc(s_hps[L], 1)

                def output(i, u):
                    s, c = u // NC, u % NC
                    pe.wait_ge(s_hlo[L], FB * (i * UPI + u + 1))
                    for j in range(TPC):
                        pe.wait_ge(s_yfree[L], TPC * (i * UPI + u) + j + 1)
                        for f in range(FB):
                            tok = slice(j * P, (j + 1) * P)
                            w = slice(f * D, (f + 1) * D)
                            last = mm3(PS[:, 4 + j, 0:D], HTh[:, u % 2, f, tok], HTl[:, u % 2, f, tok],
                                       W2h[:, s, w], W2l[:, s, w], f == 0, f == FB - 1)
                        last.then_inc(s_y[L], 1)

                def step(i, final):
                    for u in range(UPI):
                        if not (final and u == UPI - 1):
                            hidden((i,), u + 1)
                        output(i, u)

                hidden(0, 0)
                steps = NSUB[L] // 2
                with pe.Fori(0, steps - 1) as i:
                    step(i, False)
                step(steps - 1, True)

            def ffn3():
                fh, fl = FEAT[3]

                def hidden(i, u, first=False):
                    s, c = (u // NC) % 2, u % NC
                    if c == 0:
                        pe.wait_ge(s_wsplit[3], 1 if first else i * 2 + u // NC + 1)
                    for g in range(2):
                        if not first:
                            pe.wait_ge(s_hm3, i * UPI + u + 1)
                        for k in range(KD):
                            w = slice(k * D + g * P, k * D + (g + 1) * P)
                            last = mm3(PS[:, 2 * (u % 2) + g, :], W1h[:, s, w], W1l[:, s, w],
                                       fh[:, k, c * CH:(c + 1) * CH], fl[:, k, c * CH:(c + 1) * CH],
                                       k == 0, k == KD - 1)
                        last.then_inc(s_hps[3], 1)

                def output(i, u):
                    s = u // NC
                    pe.wait_ge(s_hlo[3], i * UPI + u + 1)
                    for j in range(TPC):
                        pe.wait_ge(s_yfree[3], YC + TPC * (i * UPI + u - 1) + j + 1)
                        tok = slice(j * P, (j + 1) * P)
                        mm3(PS[:, 4 + j, 0:D], HTh[:, u % 2, 0, tok], HTl[:, u % 2, 0, tok],
                            W2h[:, s, 0:D], W2l[:, s, 0:D], True, True).then_inc(s_y[3], 1)

                steps = pe.value_load(L3G[0:1, 63:64], min_val=1, max_val=STEPS3)
                hidden(0, 0, True)
                with pe.Fori(0, STEPS3) as i:
                    with pe.If(i < steps):
                        for u in range(UPI - 1):
                            hidden(i, u + 1)
                            output(i, u)
                        with pe.If(i + 1 < steps):
                            hidden(i, UPI)
                        output(i, UPI - 1)

            pe.wait_ge(s_const, 7)
            transposes("x0", X, lambda c: pe.wait_ge(s_x[c], 16))
            pe.wait_ge(s_csplit[0], 1)
            for c in range(NC):
                b = c // (NC // B)
                pe.wait_ge(s_tlo["x0"], KD * (c + 1))
                if c >= 2:
                    pe.wait_ge(s_chi[0], c - 1)
                for k in range(KD):
                    w = slice(b * KD * A0 + k * A0, b * KD * A0 + (k + 1) * A0)
                    last = mm3(PS[0:A0, 4 + c % 2, :], W1h[:, 1, w], W1l[:, 1, w], TAh[:, k, c * CH:(c + 1) * CH],
                               TAl[:, k, c * CH:(c + 1) * CH], k == 0, k == KD - 1)
                last.then_inc(s_ch[0], 1)
                pe.wait_ge(s_clo[0], c + 1)
                for j in range(TPC):
                    n = c * TPC + j
                    if n >= 2:
                        pe.wait_ge(s_cyf, n - 1)
                    w = slice(256 + b * D, 256 + (b + 1) * D)
                    mm3(PS[:, 6 + n % 2, 0:D], HTh[0:A0, c % 2, 0, j * P:(j + 1) * P],
                        HTl[0:A0, c % 2, 0, j * P:(j + 1) * P], W1h[0:A0, 1, w], W1l[0:A0, 1, w],
                        True, True).then_inc(s_cy, 1)
            transposes("z0", Z, lambda c: pe.wait_ge(s_z0, TPC * (c + 1)))
            pe.wait_ge(s_rsplit, 4)
            routing(0, lambda c: pe.wait_ge(s_tlo["z0"], KD * (c + 1)))
            bias(0)
            ffn(0)

            def tiles_done(L):
                return lambda c: pe.wait_ge(s_yfree[L], 4 + TPC * (NSUB[L] * NC - NC + c + 1))

            transposes("x1", X, tiles_done(0))
            pe.wait_ge(s_csplit[1], 1)
            for c in range(NC):
                pe.wait_ge(s_tlo["x1"], KD * (c + 1))
                if c >= 2:
                    pe.wait_ge(s_chf[1], c - 1)
                for k in range(KD):
                    w = slice(k * A0, (k + 1) * A0)
                    last = mm3(PS[0:A0, 4 + c % 2, :], W1h[:, 1, w], W1l[:, 1, w], TAh[:, k, c * CH:(c + 1) * CH],
                               TAl[:, k, c * CH:(c + 1) * CH], k == 0, k == KD - 1)
                last.then_inc(s_ch[1], 1)
            pe.wait_ge(s_chf[1], NC)
            pe.wait_ge(s_tlo["x1"], KD * NC)
            pe.wait_ge(s_clo[1], 1)
            for n in range(NT):
                nc.tensor.matmul(PS[:, 6, n:n + 1], HF[0:A0, n // TPC, (n % TPC) * P:(n % TPC + 1) * P], V1[:],
                                 start=True, stop=True)
            for c in range(NC):
                last = nc.tensor.matmul(PS[:, c, :], SC[0:A0, 7, 0:P], HF[0:A0, c, :], start=True, stop=True)
            last.then_inc(s_sc, 1)
            pe.wait_ge(s_sc_sb, 1)
            pe.wait_ge(s_xr, NT + 1)
            for b in range(B):
                if b:
                    pe.wait_ge(s_z1, TPB * b)
                for lb in range(TPB):
                    q = b * TPB + lb
                    pe.wait_ge(s_plo, q + 1)
                    for jt in range(TPB):
                        last = mm3(PS[:, jt, 0:PW], HTh[:, q % 2, jt // 4, (jt % 4) * P:(jt % 4 + 1) * P],
                                   HTl[:, q % 2, jt // 4, (jt % 4) * P:(jt % 4 + 1) * P],
                                   XRh[:, q, :], XRl[:, q, :], lb == 0, lb == TPB - 1)
                    last.then_inc(s_pmm, 1)
            pe.wait_ge(s_z1, NT)
            transposes("z1", Z, lambda c: None)
            routing(1, lambda c: pe.wait_ge(s_tlo["z1"], KD * (c + 1)))
            bias(1)
            ffn(1)

            def linear_cond(L):
                n = f"x{L}"
                transposes(n, X, tiles_done(L - 1))
                pe.wait_ge(s_csplit[L], 1)
                for c in range(NC):
                    b = c // (NC // B)
                    pe.wait_ge(s_tlo[n], KD * (c + 1))
                    for m in range(KD):
                        g = KD * c + m
                        if g >= 4:
                            pe.wait_ge(s_chi[L], g - 3)
                        for k in range(KD):
                            w = slice((b * KD + k) * D + m * P, (b * KD + k) * D + (m + 1) * P)
                            last = mm3(PS[:, 4 + g % 4, :], W1h[:, 1, w], W1l[:, 1, w],
                                       TBhv[:, k, c * CH:(c + 1) * CH], TBlv[:, k, c * CH:(c + 1) * CH],
                                       k == 0, k == KD - 1)
                        last.then_inc(s_ch[L], 1)
                pe.wait_ge(s_clo[L], KD * NC)

            linear_cond(2)
            for c in range(NC):
                for k in range(KD):
                    last = mm3(PS[0:GR, c, :], Rh[2][:, k, :], Rl[2][:, k, :], TAh[:, k, c * CH:(c + 1) * CH],
                               TAl[:, k, c * CH:(c + 1) * CH], k == 0, k == KD - 1)
            last.then_inc(s_red, 1)
            pe.wait_ge(s_wgn, 1)
            nc.tensor.transpose(PS[0:GR, 5, 0:8], WG[:, 2 * GR:3 * GR], ident[0:8, 0:8]).then_inc(s_wgt, 1)
            pe.wait_ge(s_wgs, 1)
            pe.wait_ge(s_reds, 1)
            for n in range(NT):
                last = nc.tensor.matmul(PS[:, 4, n * 8:(n + 1) * 8], HF[0:GR, n // TPC, (n % TPC) * P:(n % TPC + 1) * P],
                                        WGT[:], start=True, stop=True)
            last.then_inc(s_lg[2], 1)
            bias(2)
            ffn(2)

            linear_cond(3)
            routing(3, lambda c: None)
            pe.wait_ge(s_cnt3, 1)
            nc.tensor.matmul(PS[:, 5, 0:E3], ONE[:], SC[:, 6, 0:E3], start=True, stop=True).then_inc(s_cnt3p, 1)
            pe.wait_ge(s_list3, 1)
            ffn3()

        @block.scalar
        def _(act):
            def transposes(n, dst):
                for g in range(KD * NC):
                    c, k = g // KD, g % KD
                    act.wait_ge(s_tps[n], g + 1)
                    act.activation(dst[:, k, c * CH:(c + 1) * CH], PS[:, g % 4, :], ACT.Copy).then_inc(s_thi[n], 1)

            def exps(L, n):
                act.wait_ge(s_sub[L], 1)
                act.activation(SC[:, 1, 0:n], SC[:, 0, 0:n], ACT.Exp).then_inc(s_exp[L], 1)

            def gates_t(L):
                E = LAYERS[L][0]
                act.wait_ge(s_gt[L], 1)
                act.activation(SC[0:E, 4:8, :], PS[0:E, 0:4, :], ACT.Copy).then_inc(s_gts[L], 1)

            def ffn(L):
                func = LAYERS[L][2]
                BL = B1[L]

                def unit(i, u, first=False):
                    s, c = (u // NC), u % NC
                    for f in range(FB):
                        if first:
                            act.wait_ge(s_hps[L], f + 1)
                            b1 = BL[:, f:f + 1]
                        else:
                            act.wait_ge(s_hps[L], FB * (i * UPI + u) + f + 1)
                            act.wait_ge(s_hlo[L], FB * (i * UPI + u - 1) + f + 1)
                            act.wait_ge(s_yfree[L], TPC * (i * UPI + u))
                            b1 = BS[:, s * FB + f:s * FB + f + 1]
                        act.activation(HF[:, f, :], PS[:, f, :], func, bias=b1)
                        act.activation(HTh[:, u % 2, f, :], PS[:, f, :], func, bias=b1).then_inc(s_hhi[L], 1)

                def step(i, final):
                    n = (2 if final else 3) * FB
                    act.wait_ge(s_hhi[L], FB * (i * UPI + 1))
                    act.activation(BS[:, 0:n], BL[:, bass.ds(i * 2 * FB, n)], ACT.Copy).then_inc(s_b1[L], 1)
                    act.wait_ge(s_b1[L], i + 1)
                    for u in range(1, UPI + 1 - final):
                        unit(i, u)

                unit(0, 0, True)
                steps = NSUB[L] // 2
                with act.Fori(0, steps - 1) as i:
                    step(i, 0)
                step(steps - 1, 1)

            def ffn3():
                act.wait_ge(s_list3, 1)
                steps = act.value_load(L3G[0:1, 63:64], min_val=1, max_val=STEPS3)

                def unit(i, u):
                    act.wait_ge(s_hps[3], 2 * (i * UPI + u) + 1)
                    act.activation(HF[:, u % 2, :], PS[:, 2 * (u % 2), :], ACT.Silu).then_inc(s_hf3, 1)
                    act.wait_ge(s_hm3, 2 + i * UPI + u + 1)
                    act.wait_ge(s_yfree[3], YC + TPC * (i * UPI + u - 1))
                    act.activation(HTh[:, u % 2, 0, :], HF[:, 2 + u % 2, :], ACT.Copy).then_inc(s_hhi[3], 1)

                with act.Fori(0, STEPS3) as i:
                    with act.If(i < steps):
                        for u in range(UPI):
                            unit(i, u)

            transposes("x0", TAh)
            act.wait_ge(s_small, 16 * N_SMALL)
            for c in range(NC):
                b = c // (NC // B)
                act.wait_ge(s_ch[0], c + 1)
                if c >= 1:
                    act.wait_ge(s_clo[0], c)
                if c >= 2:
                    act.wait_ge(s_cy, TPC * (c - 1))
                act.activation(HF[0:A0, 3, :], PS[0:A0, 4 + c % 2, :], ACT.Relu, bias=CB0[:, b:b + 1])
                act.activation(HTh[0:A0, c % 2, 0, :], PS[0:A0, 4 + c % 2, :], ACT.Relu,
                               bias=CB0[:, b:b + 1]).then_inc(s_chi[0], 1)
            act.wait_ge(s_var, 1)
            act.activation(SM[:, 0, :], SM[:, 0, :], ACT.Sqrt).then_inc(s_std, 1)
            transposes("z0", TBhv)
            exps(0, NT * 8)
            gates_t(0)
            ffn(0)
            transposes("x1", TAh)
            for n in range(NT):
                act.activation(XRh[:, n, 0:D], X[:, n, :], ACT.Copy).then_inc(s_act, 1)
            for c in range(NC):
                act.wait_ge(s_ch[1], c + 1)
                act.activation(HF[0:A0, c, :], PS[0:A0, 4 + c % 2, :], ACT.Tanh, bias=CB1[:, 0:1]).then_inc(s_chf[1], 1)
            act.wait_ge(s_sc, 1)
            act.activation(SM[:, 0, :], PS[:, 6, 0:NT], ACT.Copy)
            act.activation(SC[:, 0:4, :], PS[:, 0:4, :], ACT.Copy).then_inc(s_sc_sb, 1)
            for q in range(NT):
                act.wait_ge(s_arg, q + 1)
                if q >= 2:
                    act.wait_ge(s_pmm, q - 1)
                    act.wait_ge(s_plo, q - 1)
                act.activation(HF[:, 2 * (q % 2):2 * (q % 2) + 2, :], SC[:, 4 + 2 * (q % 2):6 + 2 * (q % 2), :],
                               ACT.Exp).then_inc(s_pf, 1)
                act.activation(HTh[:, q % 2, 0:2, :], SC[:, 4 + 2 * (q % 2):6 + 2 * (q % 2), :],
                               ACT.Exp).then_inc(s_phi, 1)
                if q % TPB == TPB - 1:
                    b = q // TPB
                    act.wait_ge(s_den, b + 1)
                    for jt in range(TPB):
                        n = b * TPB + jt
                        act.activation(Z[:, n, :], PS[:, jt, 0:D], ACT.Copy, scale=SM[:, 2, n:n + 1]).then_inc(s_z1, 1)
            transposes("z1", TAh)
            exps(1, NT * 8)
            gates_t(1)
            ffn(1)

            def linear_cond(L):
                transposes(f"x{L}", TBhv)
                CB = CB2 if L == 2 else CB3
                for g in range(KD * NC):
                    c, m = g // KD, g % KD
                    act.wait_ge(s_ch[L], g + 1)
                    if g >= 4:
                        act.wait_ge(s_clo[L], g - 3)
                    act.activation(HF[:, g % 4, :], PS[:, 4 + g % 4, :], ACT.Identity, bias=CB[:, c // 2, m:m + 1])
                    act.activation(TAh[:, m, c * CH:(c + 1) * CH], PS[:, 4 + g % 4, :], ACT.Identity,
                                   bias=CB[:, c // 2, m:m + 1]).then_inc(s_chi[L], 1)

            linear_cond(2)
            act.wait_ge(s_clo[2], KD * NC)
            act.wait_ge(s_red, 1)
            act.activation(HF[0:GR, :, :], PS[0:GR, 0:4, :], ACT.Copy).then_inc(s_reds, 1)
            act.wait_ge(s_ss, 1)
            act.activation(SM[0:8, 4, 0:1], SM[0:8, 4, 0:1], ACT.Sqrt).then_inc(s_sq, 1)
            exps(2, NT * 8)
            gates_t(2)
            ffn(2)
            linear_cond(3)
            exps(3, NT * E3)
            ffn3()

        @block.vector
        def _(dve):
            steps_done = [0]

            def link(ins):
                steps_done[0] += 1
                ins.then_inc(s_dve, 1)
                dve.wait_ge(s_dve, steps_done[0])

            def lo(out, full, hi):
                return nc.vector.tensor_tensor(out, full, hi.bitcast(F32), ALU.subtract)

            def transposes(n, dh, dl):
                for g in range(KD * NC):
                    c, k = g // KD, g % KD
                    dve.wait_ge(s_thi[n], g + 1)
                    lo(dl[:, k, c * CH:(c + 1) * CH], PS[:, g % 4, :], dh[:, k, c * CH:(c + 1) * CH]).then_inc(s_tlo[n], 1)

            def cond_split(L, loads, parts):
                dve.wait_ge(s_craw[L], 16 * loads)
                for rows, cols in parts:
                    link(nc.vector.tensor_copy(W1h[0:rows, 1, cols], W1r[0:rows, cols]))
                    last = lo(W1l[0:rows, 1, cols], W1r[0:rows, cols], W1h[0:rows, 1, cols])
                    link(last)
                dve.sem_inc(s_csplit[L], 1)

            def split_into(L, buf, s, after):
                n1, n2 = (KD * SUB, FB * D) if L < 3 else (KD * D, D)
                dve.wait_ge(s_wraw[L], s * 32 + 32)
                if after is not None:
                    dve.wait_ge(s_yfree[L], TPC + after)
                nc.vector.tensor_copy(W1h[:, buf, 0:n1], W1r[:, 0:n1]).then_inc(s_whi[L], 1)
                nc.vector.tensor_copy(W2h[:, buf, 0:n2], W2r[:, 0:n2]).then_inc(s_whi[L], 1)
                dve.wait_ge(s_whi[L], s * 2 + 1)
                lo(W1l[:, buf, 0:n1], W1r[:, 0:n1], W1h[:, buf, 0:n1])
                dve.wait_ge(s_whi[L], s * 2 + 2)
                lo(W2l[:, buf, 0:n2], W2r[:, 0:n2], W2h[:, buf, 0:n2]).then_inc(s_wsplit[L], 1)

            def softmax(L, E):
                lg = SC[:, 0, 0:NT * E].rearrange("p (t e) -> p t e", e=E)
                pr = SC[:, 1, 0:NT * E].rearrange("p (t e) -> p t e", e=E)
                ps = PS[:, 4, 0:NT * E].rearrange("p (t e) -> p t e", e=E)
                dve.wait_ge(s_lg[L], 1)
                if L < 2:
                    link(nc.vector.tensor_tensor(lg, ps, BR[L][:].unsqueeze(1).broadcast_to([P, NT, E]), ALU.add))
                else:
                    link(nc.vector.tensor_copy(lg, ps))
                link(nc.vector.tensor_reduce(SM[:, 5, :], lg, axis=AX.X, op=ALU.max))
                nc.vector.tensor_tensor(lg, lg, SM[:, 5, :].unsqueeze(2).broadcast_to([P, NT, E]),
                                        ALU.subtract).then_inc(s_sub[L], 1)
                dve.wait_ge(s_exp[L], 1)
                link(nc.vector.tensor_reduce(SM[:, 6, :], pr, axis=AX.X, op=ALU.add))
                link(nc.vector.reciprocal(SM[:, 7, :], SM[:, 6, :]))
                return lg, pr

            def bc(col, E):
                return col.unsqueeze(2).broadcast_to([P, NT, E])

            def running(E):
                dve.wait_ge(s_const, 7)
                link(nc.vector.memset(RS[:].rearrange("p (t e) -> p t e", e=E)[:, :, 0:1], 0.0))
                link(nc.vector.tensor_tensor_scan(SC[:, 3, 0:NT * E], RS[:, 0:NT * E], SC[:, 2, 0:NT * E],
                                                  0.0, ALU.mult, ALU.add))

            def top1(L):
                lg, pr = softmax(L, 8)
                eq = SC[:, 2, 0:NT * 8].rearrange("p (t e) -> p t e", e=8)
                run = SC[:, 3, 0:NT * 8].rearrange("p (t e) -> p t e", e=8)
                link(nc.vector.tensor_single_scalar(eq, lg, 0.0, ALU.is_equal))
                running(8)
                link(nc.vector.scalar_tensor_tensor(run, run, 1.0, eq, ALU.is_equal, ALU.mult))
                link(nc.vector.tensor_tensor(pr, pr, bc(SM[:, 7, :], 8), ALU.mult))
                nc.vector.tensor_tensor(G[:, :, 0:8], run, pr, ALU.mult).then_inc(s_gate[L], 1)

            def bias(L):
                for n in range(NT):
                    dve.wait_ge(s_by[L], n + 1)
                    nc.vector.tensor_tensor(X[:, n, :], PS[:, 4 + n % 4, 0:D], X[:, n, :], ALU.add).then_inc(s_bu[L], 1)

            def ffn(L):
                def lows(i, u, first=False):
                    for f in range(FB):
                        dve.wait_ge(s_hhi[L], f + 1 if first else FB * (i * UPI + u) + f + 1)
                        lo(HTl[:, u % 2, f, :], HF[:, f, :], HTh[:, u % 2, f, :]).then_inc(s_hlo[L], 1)

                def gated(i, u):
                    c, s = u % NC, u // NC
                    e = (i if L < 2 else i * 2 + s)
                    for j in range(TPC):
                        n = c * TPC + j
                        dve.wait_ge(s_y[L], TPC * (i * UPI + u) + j + 1)
                        nc.vector.scalar_tensor_tensor(X[:, n, :], PS[:, 4 + j, 0:D], G[:, n, bass.ds(e, 1)],
                                                       X[:, n, :], ALU.mult, ALU.add).then_inc(s_yfree[L], 1)

                def step(i, final):
                    for u in range(UPI):
                        if not (final and u == UPI - 1):
                            lows(i, u + 1)
                        gated(i, u)
                        if u == 0:
                            split_into(L, 1, i * 2 + 1, TPC * UPI * i)
                        if u == 4 and not final:
                            split_into(L, 0, i * 2 + 2, TPC * (UPI * i + NC))

                split_into(L, 0, 0, None)
                dve.sem_inc(s_yfree[L], TPC)
                lows(0, 0, True)
                steps = NSUB[L] // 2
                with dve.Fori(0, steps - 1) as i:
                    step(i, False)
                step(steps - 1, True)

            def ffn3():
                def mid(i, u):
                    dve.wait_ge(s_hf3, i * UPI + u + 1)
                    dve.wait_ge(s_hps[3], 2 * (i * UPI + u) + 2)
                    nc.vector.tensor_tensor(HF[:, 2 + u % 2, :], HF[:, u % 2, :], PS[:, 2 * (u % 2) + 1, :],
                                            ALU.mult).then_inc(s_hm3, 1)
                    dve.wait_ge(s_hhi[3], i * UPI + u + 1)
                    lo(HTl[:, u % 2, 0, :], HF[:, 2 + u % 2, :], HTh[:, u % 2, 0, :]).then_inc(s_hlo[3], 1)

                steps = dve.value_load(L3G[0:1, 63:64], min_val=1, max_val=STEPS3)

                def gated(i, u, e):
                    c = u % NC
                    for j in range(TPC):
                        n = c * TPC + j
                        dve.wait_ge(s_y[3], TPC * (i * UPI + u) + j + 1)
                        nc.vector.scalar_tensor_tensor(X[:, n, :], PS[:, 4 + j, 0:D], G[:, n, bass.ds(e, 1)],
                                                       X[:, n, :], ALU.mult, ALU.add).then_inc(s_yfree[3], 1)

                split_into(3, 0, 0, None)
                dve.sem_inc(s_yfree[3], YC)
                dve.sem_inc(s_hm3, 2)
                mid(0, 0)
                with dve.Fori(0, STEPS3) as i:
                    with dve.If(i < steps):
                        for s in range(2):
                            e = dve.value_load(L3G[0:1, bass.ds(i * 2 + s, 1)], min_val=0, max_val=E3S)
                            for u in range(s * NC, (s + 1) * NC):
                                if u < UPI - 1:
                                    mid(i, u + 1)
                                else:
                                    with dve.If(i + 1 < steps):
                                        mid(i, UPI)
                                gated(i, u, e)
                                if u == 0:
                                    split_into(3, 1, i * 2 + 1, YC - TPC + TPC * UPI * i)
                                if u == NC:
                                    with dve.If(i + 1 < steps):
                                        split_into(3, 0, i * 2 + 2, YC - TPC + TPC * (UPI * i + NC))
                dve.drain().then_inc(s_done3, 1)

            dve.wait_ge(s_const, 7)
            link(nc.vector.tensor_copy(IO[:], IOi[:]))
            dve.wait_ge(s_small, 16 * N_SMALL)
            for L in range(4):
                link(nc.vector.tensor_copy(Rh[L][:], Rr[L][:]))
                lo(Rl[L][:], Rr[L][:], Rh[L][:]).then_inc(s_rsplit, 1)
            cond_split(0, 2 * B, [(P, slice(0, 256)), (A0, slice(256, 256 + B * D))])
            transposes("x0", TAh, TAl)
            for c in range(NC):
                b = c // (NC // B)
                dve.wait_ge(s_chi[0], c + 1)
                lo(HTl[0:A0, c % 2, 0, :], HF[0:A0, 3, :], HTh[0:A0, c % 2, 0, :]).then_inc(s_clo[0], 1)
                for j in range(TPC):
                    n = c * TPC + j
                    dve.wait_ge(s_cy, n + 1)
                    nc.vector.tensor_tensor(Z[:, n, :], PS[:, 6 + n % 2, 0:D], X[:, n, :], ALU.add).then_inc(s_cyf, 1)
                    if n == 0:
                        dve.wait_ge(s_rows, 16 * 3 * B)
                    dve.wait_ge(s_cyf, n + 1)
                    link(nc.vector.tensor_tensor(Z[:, n, :], Z[:, n, :], HF[:, 0, b * D:(b + 1) * D], ALU.add))
                    link(nc.vector.bn_stats(ST[:], Z[:, n, :]))
                    link(nc.vector.bn_aggr(MV[:, n, :], ST[:]))
            nc.vector.tensor_scalar(SM[:, 0, :], MV[:, :, 1], LN_EPS, None, ALU.add).then_inc(s_var, 1)
            dve.wait_ge(s_std, 1)
            link(nc.vector.reciprocal(SM[:, 1, :], SM[:, 0, :]))
            for n in range(NT):
                nc.vector.tensor_scalar(Z[:, n, :], Z[:, n, :], MV[:, n, 0:1], SM[:, 1, n:n + 1],
                                        ALU.subtract, ALU.mult).then_inc(s_norm, 1)
            transposes("z0", TBhv, TBlv)
            lg, pr = softmax(0, 8)
            link(nc.vector.tensor_tensor(pr, pr, bc(SM[:, 7, :], 8), ALU.mult))
            before = SC[:, 2, 0:NT * 8].rearrange("p (t e) -> p t e", e=8)
            term = SC[:, 3, 0:NT * 8].rearrange("p (t e) -> p t e", e=8)
            link(nc.vector.memset(before, 0.0))
            for j in range(8):
                pj = pr[:, :, j:j + 1]
                if j:
                    nc.vector.tensor_tensor(term[:, :, 0:j], pr[:, :, 0:j], pj.broadcast_to([P, NT, j]), ALU.is_lt)
                if j < 7:
                    nc.vector.tensor_tensor(term[:, :, j + 1:8], pr[:, :, j + 1:8],
                                            pj.broadcast_to([P, NT, 7 - j]), ALU.is_le)
                link(nc.vector.memset(term[:, :, j:j + 1], 0.0))
                link(nc.vector.tensor_tensor(term, term, pj.broadcast_to([P, NT, 8]), ALU.mult))
                link(nc.vector.tensor_tensor(before, before, term, ALU.add))
            link(nc.vector.tensor_tensor(term, before, pr, ALU.add))
            link(nc.vector.tensor_single_scalar(term, term, TOP_P, ALU.is_lt))
            link(nc.vector.scalar_tensor_tensor(term, before, 0.0, term, ALU.is_equal, ALU.max))
            nc.vector.tensor_tensor(G[:, :, 0:8], term, pr, ALU.mult).then_inc(s_gate[0], 1)
            bias(0)
            ffn(0)
            cond_split(1, 1, [(P, slice(0, KD * A0))])
            link(nc.vector.tensor_copy(SC[0:A0, 7, 0:P], V1[:].broadcast_to([A0, P])))
            dve.sem_inc(s_clo[1], 1)
            transposes("x1", TAh, TAl)
            for n in range(NT):
                dve.wait_ge(s_act, n + 1)
                lo(XRl[:, n, 0:D], X[:, n, :], XRh[:, n, 0:D]).then_inc(s_xr, 1)
            nc.vector.tensor_copy(XRh[:, :, D:D + 2], ONE[:, 0:2].unsqueeze(1).broadcast_to([P, NT, 2]))
            link(nc.vector.tensor_scalar(XRl[:, :, D:D + 2], ONE[:, 0:2].unsqueeze(1).broadcast_to([P, NT, 2]),
                                         0.0, None, ALU.mult))
            dve.sem_inc(s_xr, 1)
            dve.wait_ge(s_mode, 16)
            link(nc.vector.tensor_copy(MD[:, :, 7], MODEi[:]))
            nc.vector.tensor_single_scalar(MD[:, :, 0], MD[:, :, 7], 0.0, ALU.is_equal)
            link(nc.vector.tensor_single_scalar(MD[:, :, 1], MD[:, :, 7], 1.0, ALU.is_equal))
            link(nc.vector.tensor_tensor(MD[:, :, 6], MD[:, :, 0], MD[:, :, 1], ALU.add))
            link(nc.vector.tensor_scalar(MD[:, :, 2], MD[:, :, 6], -1.0, 1.0, ALU.mult, ALU.add))
            nc.vector.tensor_scalar(MD[:, :, 3], MD[:, :, 0], NEG, None, ALU.mult)
            link(nc.vector.tensor_scalar(MD[:, :, 4], MD[:, :, 1], NEG, None, ALU.mult))
            link(nc.vector.tensor_copy(JC[:], JCi[:]))
            for b in range(B):
                m = [MD[:, b, k:k + 1] for k in range(8)]
                link(nc.vector.tensor_scalar(DM[:, b, :], TM[:, 0, :], m[0], None, ALU.mult))
                link(nc.vector.scalar_tensor_tensor(DM[:, b, :], TM[:, 1, :], m[1], DM[:, b, :], ALU.mult, ALU.add))
                link(nc.vector.scalar_tensor_tensor(DM[:, b, :], TM[:, 2, :], m[2], DM[:, b, :], ALU.mult, ALU.add))
                link(nc.vector.tensor_scalar(DM[:, b, :], DM[:, b, :], -NEG, NEG, ALU.mult, ALU.add))
                cnt = SM[:, 3, b * TPB:(b + 1) * TPB]
                tmp = SM[:, 4, b * TPB:(b + 1) * TPB]
                link(nc.vector.tensor_scalar(tmp, JC[:], 1.0, None, ALU.add))
                link(nc.vector.tensor_scalar(cnt, tmp, m[0], None, ALU.mult))
                link(nc.vector.tensor_scalar(tmp, JC[:], -1.0, float(SEQ), ALU.mult, ALU.add))
                link(nc.vector.scalar_tensor_tensor(cnt, tmp, m[1], cnt, ALU.mult, ALU.add))
                link(nc.vector.memset(tmp, float(SEQ - 1)))
                link(nc.vector.scalar_tensor_tensor(cnt, tmp, m[2], cnt, ALU.mult, ALU.add))
            dve.wait_ge(s_sc_sb, 1)
            for b in range(B):
                m = [MD[:, b, k:k + 1] for k in range(8)]
                cols = SM[:, 0, b * TPB:(b + 1) * TPB]
                sl = SM[:, 5, b * TPB:(b + 1) * TPB]
                su = SM[:, 6, b * TPB:(b + 1) * TPB]
                nc.vector.tensor_scalar(sl, cols, m[3], None, ALU.add)
                nc.vector.tensor_scalar(su, cols, m[4], None, ALU.add)
                row = SC[:, 2 * b:2 * b + 2, :].rearrange("p a c -> p (a c)")
                pre, suf, oth = (Z[:, 4 * k:4 * k + 4, :].rearrange("p a c -> p (a c)") for k in range(3))
                link(nc.vector.tensor_tensor_scan(pre, row, row, -3e38, ALU.max, ALU.max))
                link(nc.vector.tensor_tensor_scan(suf[:, ::-1], row[:, ::-1], row[:, ::-1], -3e38, ALU.max, ALU.max))
                nc.vector.tensor_tensor(oth[:, 1:SEQ - 1], pre[:, 0:SEQ - 2], suf[:, 2:SEQ], ALU.max)
                nc.vector.tensor_copy(oth[:, 0:1], suf[:, 1:2])
                link(nc.vector.tensor_copy(oth[:, SEQ - 1:SEQ], pre[:, SEQ - 2:SEQ - 1]))
                link(nc.vector.tensor_scalar(row, pre, m[0], -1.0, ALU.mult, ALU.mult))
                link(nc.vector.tensor_scalar(pre, suf, m[1], -1.0, ALU.mult, ALU.mult))
                link(nc.vector.tensor_tensor(row, row, pre, ALU.add))
                link(nc.vector.tensor_scalar(pre, oth, m[2], -1.0, ALU.mult, ALU.mult))
                link(nc.vector.tensor_tensor(row, row, pre, ALU.add))
            for b in range(B):
                cols = SM[:, 0, b * TPB:(b + 1) * TPB]
                sl = SM[:, 5, b * TPB:(b + 1) * TPB]
                su = SM[:, 6, b * TPB:(b + 1) * TPB]
                row = SC[:, 2 * b:2 * b + 2, :].rearrange("p a c -> p (a c)")
                for lb in range(TPB):
                    q = b * TPB + lb
                    if q >= 2:
                        dve.wait_ge(s_phi, q - 1)
                    arg = SC[:, 4 + 2 * (q % 2):6 + 2 * (q % 2), :].rearrange("p a c -> p (a c)")
                    diag = slice(lb * P, (lb + 1) * P)
                    if lb:
                        nc.vector.tensor_scalar(arg[:, 0:lb * P], row[:, 0:lb * P], sl[:, lb:lb + 1], 0.0,
                                                ALU.add, ALU.min)
                    if lb < TPB - 1:
                        nc.vector.tensor_scalar(arg[:, (lb + 1) * P:], row[:, (lb + 1) * P:], su[:, lb:lb + 1], 0.0,
                                                ALU.add, ALU.min)
                    link(nc.vector.tensor_scalar(arg[:, diag], row[:, diag], cols[:, lb:lb + 1], 0.0,
                                                 ALU.add, ALU.min))
                    nc.vector.tensor_tensor(arg[:, diag], arg[:, diag], DM[:, b, :], ALU.add).then_inc(s_arg, 1)
                    if lb:
                        pooled_lo = q - 1
                        dve.wait_ge(s_phi, pooled_lo + 1)
                        lo(HTl[:, pooled_lo % 2, 0:2, :], HF[:, 2 * (pooled_lo % 2):2 * (pooled_lo % 2) + 2, :],
                           HTh[:, pooled_lo % 2, 0:2, :]).then_inc(s_plo, 1)
                q = b * TPB + TPB - 1
                dve.wait_ge(s_phi, q + 1)
                lo(HTl[:, q % 2, 0:2, :], HF[:, 2 * (q % 2):2 * (q % 2) + 2, :], HTh[:, q % 2, 0:2, :]).then_inc(s_plo, 1)
                dve.wait_ge(s_pmm, q + 1)
                bs = slice(b * TPB, (b + 1) * TPB)
                link(nc.vector.tensor_tensor(SM[:, 4, bs], PS[:, :, D], SM[:, 3, bs], ALU.mult))
                nc.vector.reciprocal(SM[:, 2, bs], SM[:, 4, bs]).then_inc(s_den, 1)
            transposes("z1", TAh, TAl)
            top1(1)
            bias(1)
            ffn(1)

            def linear_cond(L):
                cond_split(L, B, [(P, slice(0, B * KD * D))])
                transposes(f"x{L}", TBhv, TBlv)
                for g in range(KD * NC):
                    c, m = g // KD, g % KD
                    dve.wait_ge(s_chi[L], g + 1)
                    lo(TAl[:, m, c * CH:(c + 1) * CH], HF[:, g % 4, :], TAh[:, m, c * CH:(c + 1) * CH]).then_inc(s_clo[L], 1)

            link(nc.vector.tensor_tensor(WG[:, GR:2 * GR], WG[:, 0:GR], WG[:, 0:GR], ALU.mult))
            nc.vector.tensor_reduce(SM[0:8, 4, 0:1], WG[:, GR:2 * GR], axis=AX.X, op=ALU.add).then_inc(s_ss, 1)
            linear_cond(2)
            dve.wait_ge(s_sq, 1)
            link(nc.vector.tensor_scalar(SM[0:8, 4, 1:2], SM[0:8, 4, 0:1], 1e-4, None, ALU.max))
            link(nc.vector.reciprocal(SM[0:8, 4, 2:3], SM[0:8, 4, 1:2]))
            nc.vector.tensor_scalar(WG[:, 2 * GR:3 * GR], WG[:, 0:GR], SM[0:8, 4, 2:3], None, ALU.mult).then_inc(s_wgn, 1)
            dve.wait_ge(s_wgt, 1)
            nc.vector.tensor_copy(WGT[:], PS[0:GR, 5, 0:8]).then_inc(s_wgs, 1)
            top1(2)
            bias(2)
            ffn(2)
            linear_cond(3)
            lg, pr = softmax(3, E3)
            link(nc.vector.tensor_tensor(pr, pr, bc(SM[:, 7, :], E3), ALU.mult))
            link(nc.vector.tensor_tensor(lg, pr, BR[3][:].unsqueeze(1).broadcast_to([P, NT, E3]), ALU.add))
            for n in range(NT):
                last = nc.vector.max(SC[:, 4, n * 8:(n + 1) * 8], lg[:, n, :])
            link(last)
            bar = SC[:, 4, 0:NT * 8].rearrange("p (t e) -> p t e", e=8)[:, :, TOP_K - 1:TOP_K].broadcast_to([P, NT, E3])
            eq = SC[:, 2, :].rearrange("p (t e) -> p t e", e=E3)
            run = SC[:, 3, :].rearrange("p (t e) -> p t e", e=E3)
            gt = SC[:, 5, :].rearrange("p (t e) -> p t e", e=E3)
            nc.vector.tensor_tensor(gt, lg, bar, ALU.is_gt)
            link(nc.vector.tensor_tensor(eq, lg, bar, ALU.is_equal))
            link(nc.vector.tensor_reduce(SM[:, 5, :], gt, axis=AX.X, op=ALU.add))
            link(nc.vector.memset(RS[:], 1.0))
            running(E3)
            link(nc.vector.tensor_tensor(run, run, bc(SM[:, 5, :], E3), ALU.add))
            link(nc.vector.scalar_tensor_tensor(run, run, float(TOP_K), eq, ALU.is_le, ALU.mult))
            link(nc.vector.tensor_tensor(run, run, gt, ALU.add))
            nc.vector.tensor_reduce(SC[:, 6, 0:E3], run.rearrange("p t e -> p e t"), axis=AX.X,
                                    op=ALU.add).then_inc(s_cnt3, 1)
            dve.wait_ge(s_cnt3, 1)
            link(nc.vector.tensor_tensor(run, run, pr, ALU.mult))
            link(nc.vector.tensor_reduce(SM[:, 5, :], run, axis=AX.X, op=ALU.add))
            link(nc.vector.tensor_scalar(SM[:, 6, :], SM[:, 5, :], 1e-12, None, ALU.max))
            link(nc.vector.reciprocal(SM[:, 7, :], SM[:, 6, :]))
            link(nc.vector.tensor_tensor(G[:, :, 0:E3], run, bc(SM[:, 7, :], E3), ALU.mult))
            link(nc.vector.memset(G[:, :, E3:E3S], 1.0))
            link(nc.vector.memset(G[:, :, E3S:E3S + 1], 0.0))
            used, place, val = (SC[0:1, 7, 64 * k:64 * k + E3] for k in range(3))
            wl, gl, inuse = (SC[0:1, 7, 192 + 64 * k:192 + 64 * k + E3S] for k in range(3))
            num = SC[0:1, 7, 384:385]
            hit = Z[0:1, 0:5, :].rearrange("p a c -> p (a c)")[:, 0:E3S * E3].rearrange("p (i e) -> p i e", e=E3)
            dve.wait_ge(s_cnt3p, 1)
            link(nc.vector.tensor_single_scalar(used, PS[0:1, 5, 0:E3], 0.0, ALU.is_gt))
            link(nc.vector.tensor_tensor_scan(place, ONE[0:1, 0:E3], used, 0.0, ALU.mult, ALU.add))
            link(nc.vector.tensor_scalar(num, place[:, E3 - 1:E3], 2.0, None, ALU.add))
            link(nc.vector.tensor_tensor(place, place, used, ALU.subtract))
            link(nc.vector.tensor_scalar(place, place, 2.0, None, ALU.add))
            link(nc.vector.tensor_tensor(val, used, IO[0:1, 0:E3], ALU.mult))
            link(nc.vector.tensor_tensor(hit, IO[0:1, 0:E3S].unsqueeze(2).broadcast_to([1, E3S, E3]),
                                         place.unsqueeze(1).broadcast_to([1, E3S, E3]), ALU.is_equal))
            link(nc.vector.tensor_tensor(hit, hit, val.unsqueeze(1).broadcast_to([1, E3S, E3]), ALU.mult))
            link(nc.vector.tensor_reduce(wl, hit, axis=AX.X, op=ALU.add))
            link(nc.vector.tensor_scalar(wl[:, 0:2], IO[0:1, 0:2], float(E3), None, ALU.add))
            link(nc.vector.tensor_scalar(inuse, IO[0:1, 0:E3S], num, float(E3S), ALU.is_ge, ALU.mult))
            link(nc.vector.tensor_tensor(gl, wl, inuse, ALU.max))
            link(nc.vector.tensor_copy(L3W[:, 0:E3S], wl))
            link(nc.vector.tensor_copy(L3G[:, 0:E3S], gl))
            link(nc.vector.tensor_scalar(val[:, 0:STEPS3], IO[0:1, 0:STEPS3], 2.0, None, ALU.mult))
            link(nc.vector.tensor_scalar(val[:, 0:STEPS3], val[:, 0:STEPS3], num, None, ALU.is_lt))
            link(nc.vector.tensor_reduce(num, val[:, 0:STEPS3], axis=AX.X, op=ALU.add))
            nc.vector.tensor_copy(L3G[:, 63:64], num).then_inc(s_list3, 1)
            dve.wait_ge(s_list3, 1)
            ffn3()


def kernel(**inputs):
    import numpy as np
    import concourse.bacc as bacc
    from concourse.bass_utils import run_bass_kernel_spmd

    a = {k: np.asarray(v) for k, v in inputs.items()}
    ins = {n: a[n] for n in (
        "x", "L0_cond_b1", "L0_cond_W1", "L0_cond_W2", "L0_cond_b2", "L0_cond_gamma", "L0_cond_beta", "L0_ffn_Wr", "L0_ffn_br",
        "L0_ffn_b2", "L1_cond_W1", "L1_cond_b1", "L1_cond_v", "L1_ffn_Wr", "L1_ffn_br", "L1_ffn_b2", "L2_cond_W",
        "L2_ffn_w_red", "L2_ffn_wg", "L2_ffn_b2", "L3_cond_weight", "L3_ffn_e_score_bias")}
    ins["ids"] = np.concatenate([a["itok_B_0_8"], a["itok_B_0_2"], a["itok_B_0_30"], a["itok_B_0_15"]]).reshape(1, 8)
    ins["L1_mode"] = a["itok_B_0_2"]
    ins["L3_router_t"] = a["L3_ffn_router_weight"].T
    for L, name in ((2, "L2_cond_b"), (3, "L3_cond_bias")):
        ins[f"L{L}_cond_b"] = a[name].reshape(-1, KD, P).transpose(2, 0, 1)
    for L, (E, F, _) in enumerate(LAYERS):
        w1, w2 = a[f"L{L}_ffn_W1"], a[f"L{L}_ffn_W2"]
        ins[f"L{L}_w1"] = w1.reshape(E, KD, P, F // SUB, SUB).transpose(0, 3, 2, 1, 4).reshape(-1, P, KD * SUB)
        ins[f"L{L}_w2"] = w2.reshape(E, F // SUB, FB, P, D).transpose(0, 1, 3, 2, 4).reshape(-1, P, FB * D)
        ins[f"L{L}_b1_t"] = a[f"L{L}_ffn_b1"].reshape(E * F // P, P).T
    I3 = 128
    gate_up, down = a["L3_ffn_gate_up_proj"], a["L3_ffn_down_proj"]
    sg, su, sd = (a[f"L3_ffn_shared_{n}_w"] for n in ("gate", "up", "down"))
    halves = [np.concatenate([sg[h * I3:(h + 1) * I3], su[h * I3:(h + 1) * I3]]) for h in range(2)]
    gu = np.concatenate([gate_up, np.stack(halves)])
    ins["L3_w1"] = gu.transpose(0, 2, 1).reshape(E3S, KD, P, 2 * I3).transpose(0, 2, 1, 3).reshape(E3S, P, KD * 2 * I3)
    dn = np.concatenate([down, np.stack([sd[:, h * I3:(h + 1) * I3] for h in range(2)])])
    ins["L3_w2"] = dn.transpose(0, 2, 1)

    nc = bacc.Bacc("TRN2", target_bir_lowering=False, num_devices=1)
    arrays, tensors = {}, {}
    for name, v in ins.items():
        arrays[f"in_{name}"] = np.ascontiguousarray(v)
        tensors[name] = nc.dram_tensor(f"in_{name}", v.shape, mybir.dt.from_np(v.dtype), kind="ExternalInput").ap()
    tensors["out"] = nc.dram_tensor("out_x", (B, SEQ, D), F32, kind="ExternalOutput").ap()
    build(nc, tensors)
    r = run_bass_kernel_spmd(nc, [arrays], core_ids=[0])
    return r.results[0]["out_x"]
```

```python
import concourse.bass as bass
from concourse import mybir
from contextlib import ExitStack

F32 = mybir.dt.float32
F32R = mybir.dt.float32r
I32 = mybir.dt.int32
ALU = mybir.AluOpType
ACT = mybir.ActivationFunctionType
AX = mybir.AxisListType

P = 128
B, SEQ, D = 2, 1024, 256
NT = B * SEQ // P
TPB = SEQ // P
CH = 512
NC = B * SEQ // CH
TPC = CH // P
KD = D // P
A0 = 64
GR = 16
SUB = 512
FB = SUB // P
LN_EPS = 1e-5
TOP_P = 0.8
TOP_K = 6
NEG = -1e30
LAYERS = [(8, 1024, ACT.Relu), (8, 1024, ACT.Gelu), (8, 512, ACT.Gelu)]
E3 = 32
E3S = 34
SPARSE = (1, 2)
BT = 256
BTT = BT // P
BLOCKS = B * SEQ // BT + 8
STEPS = BLOCKS // 2
PW = D + 2


def build(nc, t):
    with ExitStack() as ctx:
        def sb(name, shape, dt=F32):
            return ctx.enter_context(nc.sbuf_tensor(name, shape, dt))

        def sem(name):
            return ctx.enter_context(nc.semaphore(name))

        X = sb("x_tok", [P, NT, D])
        Z = sb("z_tok", [P, NT, D])
        TAh = sb("featA_hi", [P, KD, NT * P], F32R)
        TAl = sb("featA_lo", [P, KD, NT * P], F32R)
        TBh = sb("featB_hi", [P, NT * PW], F32R)
        TBl = sb("featB_lo", [P, NT * PW], F32R)
        TBhv = TBh[:, 0:KD * NT * P].rearrange("p (k n) -> p k n", k=KD)
        TBlv = TBl[:, 0:KD * NT * P].rearrange("p (k n) -> p k n", k=KD)
        XRh = TBh[:].rearrange("p (t w) -> p t w", t=NT)
        XRl = TBl[:].rearrange("p (t w) -> p t w", t=NT)
        W1r = sb("w1_raw", [P, KD * SUB])
        W2r = sb("w2_raw", [P, FB * D])
        W1h = sb("w1_hi", [P, 2, KD * SUB], F32R)
        W1l = sb("w1_lo", [P, 2, KD * SUB], F32R)
        W2h = sb("w2_hi", [P, 2, FB * D], F32R)
        W2l = sb("w2_lo", [P, 2, FB * D], F32R)
        HF = sb("hidden_f32", [P, FB, CH])
        HTh = sb("hidden_hi", [P, 2, FB, CH], F32R)
        HTl = sb("hidden_lo", [P, 2, FB, CH], F32R)
        SC = sb("scratch", [P, 8, CH])
        G = sb("gates", [P, NT, E3S + 1])
        IO = sb("iota_f32", [P, 64])
        IOi = sb("iota_int", [P, 64], I32)
        RS16 = sb("reset16", [P, 8 * NT])
        SLOTf = sb("slot_f32", [P, NT])
        SLOT = sb("slot", [P, NT], I32)
        BLK = [sb(f"blocks{L}", [1, 64], I32) for L in SPARSE]
        XS = nc.dram_tensor("x_sorted", [(BLOCKS + 2) * BT, D], F32).ap()
        YS = nc.dram_tensor("y_sorted", [BLOCKS * BT, D], F32).ap()
        Zf = Z[:].rearrange("p t d -> p (t d)")
        ZW = [Zf[:, 0:NT * D // 2], Zf[:, NT * D // 2:]]
        WB1h, WB1l = (x[:, 0:NT * D].rearrange("p (b n) -> p b n", b=2) for x in (TBh, TBl))
        WB2h, WB2l = (x[:].rearrange("p k n -> p (k n)").rearrange("p (b n) -> p b n", b=2) for x in (TAh, TAl))
        XB = W1r[:].rearrange("p (b t d) -> p b t d", b=2, t=BTT)
        YB = W2r[:].rearrange("p (b t d) -> p b t d", b=2, t=BTT)
        L3W = sb("list3_weights", [1, 64], I32)
        L3G = sb("list3_gates", [1, 64], I32)
        ident = sb("ident", [P, P])
        IDS = sb("ids", [1, 8], I32)
        MODEi = sb("mode_int", [P, B], I32)
        B1 = [sb(f"b1_{L}", [P, LAYERS[L][0] * LAYERS[L][1] // P]) for L in range(3)]
        BB = sb("b1_block", [P, 2, 8])
        BS = sb("b1_step", [P, 3 * FB])
        B2 = [sb(f"b2_{L}", [LAYERS[L][0], D]) for L in range(3)]
        BR = [sb("br_0", [P, 8]), sb("br_1", [P, 8]), None, sb("br_3", [P, E3])]
        CB0 = sb("cond0_b1", [A0, B])
        CB1 = sb("cond1_b1", [A0, 1])
        CB3 = sb("cond3_b", [P, B, KD])
        V1 = sb("cond1_v", [A0, 1])
        RW = [GR if L == 2 else 8 if L < 2 else E3 for L in range(4)]
        Rr = [sb(f"router_raw{L}", [P, KD, RW[L]]) for L in range(4)]
        Rh = [sb(f"router_hi{L}", [P, KD, RW[L]], F32R) for L in range(4)]
        Rl = [sb(f"router_lo{L}", [P, KD, RW[L]], F32R) for L in range(4)]
        WG = sb("wg", [8, 3 * GR])
        WGT = sb("wg_t", [GR, 8])
        ST = sb("stats", [P, 6])
        MV = sb("mean_var", [P, NT, 2])
        SM = sb("small", [P, 8, NT])
        JC = sb("j_col", [P, TPB])
        JCi = sb("j_col_int", [P, TPB], I32)
        MD = sb("mode", [P, B, 8])
        TM = sb("tri", [P, 3, P])
        ONE = sb("ones", [P, P])
        PS = ctx.enter_context(nc.psum_tensor("ps", [P, 8, CH], F32))

        RS = SC[:, 7, :]
        DM = W2r[:, 0:B * P].rearrange("p (b j) -> p b j", b=B)
        XTh, XTl = (x[:, 0, :].rearrange("p (b k n) -> p b k n", b=2, k=KD) for x in (W1h, W1l))

        s_x = [sem(f"x_in{c}") for c in range(NC)]
        s_ids = sem("ids_in")
        s_small = sem("small_in")
        N_SMALL = 20
        s_mode = sem("mode_in")
        s_rows = sem("rows_in")
        s_craw = [sem(f"cond_raw{L}") for L in range(4)]
        s_csplit = [sem(f"cond_split{L}") for L in range(4)]
        s_const0 = sem("const_fill")
        s_const = sem("const")
        s_rsplit = sem("router_split")
        s_dve = sem("dve_step")
        s_act = sem("act_step")
        s_pool = sem("pool_step")
        TR = ["x0", "z0", "x1", "z1", "x2", "z2", "x3"]
        TR0 = {n: KD * NC * i for i, n in enumerate(TR)}
        s_tps = sem("tr_ps")
        s_thi = sem("tr_hi")
        s_tlo = sem("tr_lo")
        s_ch = {L: sem(f"cond_h{L}") for L in (0, 1, 3)}
        s_chf = {1: sem("cond_hf1")}
        s_chi = {L: sem(f"cond_hi{L}") for L in (0, 1, 3)}
        s_clo = {L: sem(f"cond_lo{L}") for L in (0, 1, 3)}
        s_cy = sem("cond0_y")
        s_cyf = sem("cond0_y_used")
        s_var = sem("ln_var")
        s_std = sem("ln_std")
        s_norm = sem("ln_norm")
        s_z0 = sem("z0_tile")
        s_sc = sem("score_ps")
        s_sc_sb = sem("score_row")
        s_xr = sem("pool_rhs")
        s_arg = sem("pool_arg")
        s_pf = sem("pool_p")
        s_phi = sem("pool_hi")
        s_plo = sem("pool_lo")
        s_pmm = sem("pool_mm")
        s_den = sem("pool_den")
        s_z1 = sem("z1_tile")
        s_lg = [sem(f"logits{L}") for L in range(4)]
        s_sub = [sem(f"logits_shifted{L}") for L in range(4)]
        s_exp = [sem(f"logits_exp{L}") for L in range(4)]
        s_gate = [sem(f"gates{L}") for L in range(4)]
        s_gt = sem("gates_t_ps")
        s_gts = sem("gates_t")
        s_by = sem("bias_y")
        s_bu = sem("bias_used")
        s_c2y = sem("cond2_y")
        s_z2 = sem("z2_tile")
        s_red = sem("reduced_ps")
        s_reds = sem("reduced")
        s_wgn = sem("wg_norm")
        s_wgt = sem("wg_t_ps")
        s_wgs = sem("wg_t_sb")
        s_ss = sem("wg_sumsq")
        s_sq = sem("wg_root")
        s_wraw = {L: sem(f"w_raw{L}") for L in (0, 3)}
        s_wsplit = {L: sem(f"w_split{L}") for L in (0, 3)}
        s_whi = {L: sem(f"w_hi{L}") for L in (0, 3)}
        s_hps = [sem(f"h_ps{L}") for L in range(4)]
        s_b1 = {L: sem(f"b1_step{L}") for L in (0,)}
        s_hf3 = sem("silu3")
        s_hm3 = sem("hmid3")
        s_hhi = [sem(f"h_hi{L}") for L in range(4)]
        s_hlo = [sem(f"h_lo{L}") for L in range(4)]
        s_y = [sem(f"y_ps{L}") for L in range(4)]
        s_yfree = {L: sem(f"y_free{L}") for L in (0, 3)}
        s_cnt3 = sem("counts3_in")
        s_cnt3p = sem("counts3_ps")
        s_list3 = sem("list3")
        s_done3 = sem("layer3_done")
        s_zero = sem("zeros_filled")
        s_zst = sem("x_sorted_cleared")
        s_oh = sem("onehot")
        s_rank = sem("ranks")
        s_list = sem("block_list")
        s_scat = sem("scattered")
        s_gath = [sem(f"gathered{c}") for c in range(NC)]
        s_add = sem("added")
        s_w1raw = [sem(f"w1_raw{L}") for L in SPARSE]
        s_w1hi = [sem(f"w1_hi{L}") for L in SPARSE]
        s_w1sp = [sem(f"w1_split{L}") for L in SPARSE]
        s_w2raw = [sem(f"w2_raw{L}") for L in SPARSE]
        s_w2hi = [sem(f"w2_hi{L}") for L in SPARSE]
        s_w2sp = [sem(f"w2_split{L}") for L in SPARSE]
        s_bb = [sem(f"b1_block{L}") for L in SPARSE]
        s_xb = [[sem(f"x_block{L}_{k}") for k in range(2)] for L in SPARSE]
        s_xps = [sem(f"xt_ps{L}") for L in SPARSE]
        s_xhi = [sem(f"xt_hi{L}") for L in SPARSE]
        s_xlo = [sem(f"xt_lo{L}") for L in SPARSE]
        s_yev = [sem(f"y_out{L}") for L in SPARSE]
        s_yst = [[sem(f"y_stored{L}_{k}") for k in range(2)] for L in SPARSE]
        s_yb = [sem(f"y_buffer{L}") for L in SPARSE]
        s_blocks = sem("blocks_done")
        s_row = sem("cond2_row")
        s_out = sem("out_stored")

        NSUB = [LAYERS[L][0] * LAYERS[L][1] // SUB for L in range(3)]
        NSUB.append(E3S)
        FEAT = [(TBhv, TBlv), (TAh, TAl), (TAh, TAl), (TAh, TAl)]
        YC = 2 * TPC
        STEPS3 = E3S // 2
        UPI = 2 * NC

        block = ctx.enter_context(nc.Block())

        @block.sync
        def _(sp):
            sp.dma_start(IDS[0:1, 0:8], t["ids"]).then_inc(s_ids, 16)
            for c in range(NC):
                sp.dma_start(X[:, c * TPC:(c + 1) * TPC, :],
                             t["x"].rearrange("b (t p) d -> p (b t) d", p=P)[:, c * TPC:(c + 1) * TPC, :]
                             ).then_inc(s_x[c], 16)
            sp.wait_ge(s_ids, 16)
            lang = [sp.value_load(IDS[0:1, b:b + 1], min_val=0, max_val=9) for b in range(B)]
            for b in range(B):
                sp.dma_start(W1r[:, b * KD * A0:(b + 1) * KD * A0].rearrange("p (k a) -> p k a", k=KD),
                             t["L0_cond_W1"][bass.ds(lang[b], 1), :, :].rearrange("o (k p) a -> p (o k) a", p=P)
                             ).then_inc(s_craw[0], 16)
                sp.dma_start(W1r[0:A0, 256 + b * D:256 + (b + 1) * D],
                             t["L0_cond_W2"][bass.ds(lang[b], 1), :, :].rearrange("o a d -> a (o d)")
                             ).then_inc(s_craw[0], 16)
            for b in range(B):
                for n, name in enumerate(("L0_cond_b2", "L0_cond_gamma", "L0_cond_beta")):
                    sp.dma_start(HF[:, n, b * D:(b + 1) * D],
                                 t[name][bass.ds(lang[b], 1), :].broadcast_to([P, D])).then_inc(s_rows, 16)
                sp.dma_start(CB0[:, b:b + 1], t["L0_cond_b1"][bass.ds(lang[b], 1), :].rearrange("o a -> a o")).then_inc(s_small, 16)
            for L, name in enumerate(("L0_ffn_Wr", "L1_ffn_Wr", "L2_ffn_w_red", "L3_router_t")):
                sp.dma_start(Rr[L][:], t[name].rearrange("(k p) e -> p k e", p=P)).then_inc(s_small, 16)
            sp.dma_start(BR[0][:], t["L0_ffn_br"].unsqueeze(0).broadcast_to([P, 8])).then_inc(s_small, 16)
            sp.dma_start(BR[1][:], t["L1_ffn_br"].unsqueeze(0).broadcast_to([P, 8])).then_inc(s_small, 16)
            sp.dma_start(BR[3][:], t["L3_ffn_e_score_bias"].unsqueeze(0).broadcast_to([P, E3])).then_inc(s_small, 16)
            for L in range(3):
                sp.dma_start(B1[L][:], t[f"L{L}_b1_t"]).then_inc(s_small, 16)
                sp.dma_start(B2[L][:], t[f"L{L}_ffn_b2"]).then_inc(s_small, 16)
            sp.dma_start(CB1[:], t["L1_cond_b1"].unsqueeze(1)).then_inc(s_small, 16)
            sp.dma_start(V1[:], t["L1_cond_v"].unsqueeze(1)).then_inc(s_small, 16)
            sp.dma_start(WG[:, 0:GR], t["L2_ffn_wg"]).then_inc(s_small, 16)
            cat = [sp.value_load(IDS[0:1, 4 + b:5 + b], min_val=0, max_val=31) for b in range(B)]
            emb = [sp.value_load(IDS[0:1, 6 + b:7 + b], min_val=0, max_val=15) for b in range(B)]
            for b in range(B):
                sp.dma_start(CB3[:, b, :], t["L3_cond_b"][:, bass.ds(emb[b], 1), :].rearrange("p o k -> p (o k)")
                             ).then_inc(s_small, 16)

            def sub_weights(L, s):
                if L < 3:
                    sp.dma_start(W1r[:], t[f"L{L}_w1"][bass.ds(s, 1)].rearrange("o p f -> p (o f)")).then_inc(s_wraw[L], 16)
                    sp.dma_start(W2r[:], t[f"L{L}_w2"][bass.ds(s, 1)].rearrange("o p f -> p (o f)")).then_inc(s_wraw[L], 16)
                else:
                    sp.dma_start(W1r[:, 0:KD * D], t["L3_w1"][bass.ds(s, 1)].rearrange("o p f -> p (o f)")
                                 ).then_inc(s_wraw[L], 16)
                    sp.dma_start(W2r[:, 0:D], t["L3_w2"][bass.ds(s, 1)].rearrange("o p f -> p (o f)")
                                 ).then_inc(s_wraw[L], 16)

            def block_weights(L):
                F = LAYERS[SPARSE[L]][1]
                w1, w2 = t[f"L{SPARSE[L]}_w1"], t[f"L{SPARSE[L]}_w2"]

                def load(w, n, raw, done, q, before):
                    e = sp.value_load(BLK[L][0:1, bass.ds(q, 1)] if not isinstance(q, int) else BLK[L][0:1, q:q + 1],
                                      min_val=0, max_val=7)
                    if before is not None:
                        sp.wait_ge(before, q)
                    sp.dma_start(ZW[n][:, 0:KD * F], w[bass.ds(e, 1)].rearrange("o p f -> p (o f)")).then_inc(done, 16)

                sp.wait_ge(s_list, L + 1)
                steps = sp.value_load(BLK[L][0:1, 63:64], min_val=1, max_val=STEPS)
                sp.wait_ge(s_scat, 16 * NT * (L + 1))
                load(w1, 0, ZW, s_w1raw[L], 0, None)
                load(w2, 1, ZW, s_w2raw[L], 0, None)
                load(w1, 0, ZW, s_w1raw[L], 1, s_w1sp[L])
                with sp.Fori(0, STEPS) as i:
                    with sp.If(i < steps):
                        load(w2, 1, ZW, s_w2raw[L], i * 2 + 1, s_w2sp[L])
                    with sp.If(i + 1 < steps):
                        load(w1, 0, ZW, s_w1raw[L], i * 2 + 2, s_w1sp[L])
                        load(w2, 1, ZW, s_w2raw[L], i * 2 + 2, s_w2sp[L])
                        load(w1, 0, ZW, s_w1raw[L], i * 2 + 3, s_w1sp[L])
                sp.wait_ge(s_blocks, L + 1)

            for L in range(4):
                sp.wait_ge(s_csplit[L], 1)
                if L == 3:
                    sub_weights(3, E3)
                    sp.wait_ge(s_list3, 1)
                    steps = sp.value_load(L3G[0:1, 63:64], min_val=1, max_val=STEPS3)
                    with sp.Fori(1, E3S) as s:
                        with sp.If(s < steps * 2):
                            e = sp.value_load(L3W[0:1, bass.ds(s, 1)], min_val=0, max_val=E3S - 1)
                            sp.wait_ge(s_wsplit[3], s)
                            sub_weights(3, e)
                    break
                if L in SPARSE:
                    block_weights(L - 1)
                else:
                    sub_weights(L, 0)
                    with sp.Fori(1, NSUB[L]) as s:
                        sp.wait_ge(s_wsplit[L], s)
                        sub_weights(L, s)
                    sp.wait_ge(s_wsplit[L], NSUB[L])
                if L == 0:
                    sp.dma_start(W1r[:, 0:KD * A0].rearrange("p (k a) -> p k a", k=KD),
                                 t["L1_cond_W1"].rearrange("(k p) a -> p k a", p=P)).then_inc(s_craw[1], 16)
                if L in (1, 2):
                    row = cat if L == 1 else emb
                    for b in range(B):
                        sp.dma_start(W1r[:, b * KD * D:(b + 1) * KD * D].rearrange("p (k d) -> p k d", k=KD),
                                     t["L2_cond_W" if L == 1 else "L3_cond_weight"][bass.ds(row[b], 1), :, :]
                                     .rearrange("o (k p) d -> p (o k) d", p=P)).then_inc(s_craw[L + 1], 16)
                        if L == 1:
                            sp.dma_start(W2r[:, b * D:(b + 1) * D], t["L2_cond_b"][bass.ds(cat[b], 1), :]
                                         .broadcast_to([P, D])).then_inc(s_row, 16)
            sp.wait_ge(s_done3, 1)
            for c in range(NC):
                sp.dma_start(t["out"].rearrange("b (t p) d -> p (b t) d", p=P)[:, c * TPC:(c + 1) * TPC, :],
                             X[:, c * TPC:(c + 1) * TPC, :]).then_inc(s_out, 16)
            sp.wait_ge(s_out, 16 * NC)

        @block.gpsimd
        def _(gp):
            gp.dma_start(MODEi[:], t["L1_mode"].unsqueeze(0).broadcast_to([P, B])).then_inc(s_mode, 16)
            gp.memset(ident[:], 0.0).then_inc(s_const0, 1)
            gp.memset(TM[:], 1.0).then_inc(s_const0, 1)
            gp.memset(ONE[:], 1.0).then_inc(s_const, 1)
            gp.iota(JCi[:], [[P, TPB]], base=0, channel_multiplier=1).then_inc(s_const, 1)
            gp.iota(IOi[:], [[1, 64]], base=0, channel_multiplier=0).then_inc(s_const, 1)
            gp.wait_ge(s_const0, 2)
            gp.affine_select(out=ident[:], in_=ident[:], compare_op=ALU.not_equal, fill=1.0, base=0,
                             pattern=[[-1, P]], channel_multiplier=1).then_inc(s_const, 1)
            gp.affine_select(out=TM[:, 0, :], in_=TM[:, 0, :], compare_op=ALU.is_ge, fill=0.0, base=0,
                             pattern=[[1, P]], channel_multiplier=-1).then_inc(s_const, 1)
            gp.affine_select(out=TM[:, 1, :], in_=TM[:, 1, :], compare_op=ALU.is_ge, fill=0.0, base=0,
                             pattern=[[-1, P]], channel_multiplier=1).then_inc(s_const, 1)
            gp.affine_select(out=TM[:, 2, :], in_=TM[:, 2, :], compare_op=ALU.not_equal, fill=0.0, base=0,
                             pattern=[[-1, P]], channel_multiplier=1).then_inc(s_const, 1)
            zeros = SC[:].rearrange("p a c -> p (a c)")
            gp.memset(zeros, 0.0).then_inc(s_zero, 1)
            gp.wait_ge(s_zero, 1)
            for dst in (XS[0:BLOCKS * BT], YS):
                for k in range(BLOCKS * BT // (P * NT)):
                    gp.dma_start(dst.rearrange("(k p r) d -> k p (r d)", p=P, r=NT)[k], zeros).then_inc(s_zst, 16)
            gp.wait_ge(s_rows, 16 * 3 * B)
            for n in range(NT):
                b = n // TPB
                gp.wait_ge(s_norm, n + 1)
                gp.tensor_tensor(Z[:, n, :], Z[:, n, :], HF[:, 1, b * D:(b + 1) * D], ALU.mult).then_inc(s_pool, 1)
                gp.wait_ge(s_pool, n + 1)
                gp.tensor_tensor(Z[:, n, :], Z[:, n, :], HF[:, 2, b * D:(b + 1) * D], ALU.add).then_inc(s_z0, 1)

            for L in range(2):
                gp.wait_ge(s_list, L + 1)
                steps = gp.value_load(BLK[L][0:1, 63:64], min_val=1, max_val=STEPS)
                if L == 0:
                    gp.wait_ge(s_zst, 16 * 2 * BLOCKS * BT // (P * NT))
                for n in range(NT):
                    gp.indirect_dma_start(XS, bass.IndirectOffsetOnAxis(ap=SLOT[:, n:n + 1], axis=0),
                                          Z[:, n, :], None).then_inc(s_scat, 16)
                gp.wait_ge(s_scat, 16 * NT * (L + 1))

                def load(i, k):
                    src = XS.rearrange("(i k t p) d -> i k p t d", k=2, t=BTT, p=P)
                    gp.dma_start(XB[:, k], src[bass.ds(i, 1), k].rearrange("o p t d -> p (o t) d")
                                 ).then_inc(s_xb[L][k], 16)

                gp.sem_inc(s_yb[L], 2)
                load(0, 0)
                load(0, 1)
                with gp.Fori(0, STEPS) as i:
                    with gp.If(i + 1 < steps):
                        for k in range(2):
                            gp.wait_ge(s_xps[L], i * 2 + k + 1)
                            load(i + 1, k)
                    with gp.If(i < steps):
                        for k in range(2):
                            gp.wait_ge(s_yev[L], BTT * (i * 2 + k + 2))
                            dst = YS.rearrange("(i k t p) d -> i k p t d", k=2, t=BTT, p=P)
                            gp.dma_start(dst[bass.ds(i, 1), k].rearrange("o p t d -> p (o t) d"), YB[:, k]
                                         ).then_inc(s_yst[L][k], 16)
                            gp.wait_ge(s_yst[L][k], i * 16 + 16)
                            gp.sem_inc(s_yb[L], 1)
                gp.sem_inc(s_blocks, 1)
                for n in range(NT):
                    gp.indirect_dma_start(Z[:, n, :], None, YS,
                                          bass.IndirectOffsetOnAxis(ap=SLOT[:, n:n + 1], axis=0)
                                          ).then_inc(s_gath[n // TPC], 16)

        @block.tensor
        def _(pe):
            def mm3(out, lh, ll, rh, rl, first, last):
                nc.tensor.matmul(out, lh, rh, start=first, stop=False)
                nc.tensor.matmul(out, lh, rl, start=False, stop=False)
                return nc.tensor.matmul(out, ll, rh, start=False, stop=last)

            def transposes(n, src, ready):
                for c in range(NC):
                    ready(c)
                    for k in range(KD):
                        g = KD * c + k
                        if g >= 4:
                            pe.wait_ge(s_tlo, TR0[n] + g - 3)
                        for j in range(TPC):
                            last = nc.tensor.transpose(PS[:, g % 4, j * P:(j + 1) * P],
                                                       src[:, c * TPC + j, k * P:(k + 1) * P], ident[:])
                        last.then_inc(s_tps, 1)

            def routing(L, wait_feat):
                fh, fl = FEAT[L]
                E = RW[L]
                for n in range(NT):
                    if n % TPC == 0:
                        wait_feat(n // TPC)
                    for k in range(KD):
                        last = mm3(PS[:, 4, n * E:(n + 1) * E], fh[:, k, n * P:(n + 1) * P],
                                   fl[:, k, n * P:(n + 1) * P], Rh[L][:, k, :], Rl[L][:, k, :], k == 0, k == KD - 1)
                last.then_inc(s_lg[L], 1)

            def bias(L):
                E = LAYERS[L][0]
                pe.wait_ge(s_gate[L], 1)
                for n in range(NT):
                    last = nc.tensor.transpose(PS[0:E, n // TPC, (n % TPC) * P:(n % TPC + 1) * P],
                                               G[:, n, 0:E], ident[:])
                last.then_inc(s_gt, 1)
                pe.wait_ge(s_gts, L + 1)
                if L in SPARSE:
                    pe.wait_ge(s_list, L)
                for n in range(NT):
                    if n >= 4:
                        pe.wait_ge(s_bu, NT * L + n - 3)
                    nc.tensor.matmul(PS[:, 4 + n % 4, 0:D], SC[0:E, 4 + n // TPC, (n % TPC) * P:(n % TPC + 1) * P],
                                     B2[L][:], start=True, stop=True).then_inc(s_by, 1)
                pe.wait_ge(s_bu, NT * L + NT)

            def ffn(L):
                fh, fl = FEAT[L]

                def hidden(q, u):
                    s, c = (u // NC) % 2, u % NC
                    for f in range(FB):
                        if f == 0 and c == 0:
                            pe.wait_ge(s_wsplit[L], (q + NC) // NC if isinstance(q, int) else q[0] * 2 + u // NC + 1)
                        if not (isinstance(q, int) and q == 0):
                            pe.wait_ge(s_hhi[L], FB * (q[0] * UPI + u - 1) + f + 1)
                        for k in range(KD):
                            w = slice(k * SUB + f * P, k * SUB + (f + 1) * P)
                            last = mm3(PS[:, f, :], W1h[:, s, w], W1l[:, s, w],
                                       fh[:, k, c * CH:(c + 1) * CH], fl[:, k, c * CH:(c + 1) * CH],
                                       k == 0, k == KD - 1)
                        last.then_inc(s_hps[L], 1)

                def output(i, u):
                    s, c = u // NC, u % NC
                    pe.wait_ge(s_hlo[L], FB * (i * UPI + u + 1))
                    for j in range(TPC):
                        pe.wait_ge(s_yfree[L], TPC * (i * UPI + u) + j + 1)
                        for f in range(FB):
                            tok = slice(j * P, (j + 1) * P)
                            w = slice(f * D, (f + 1) * D)
                            last = mm3(PS[:, 4 + j, 0:D], HTh[:, u % 2, f, tok], HTl[:, u % 2, f, tok],
                                       W2h[:, s, w], W2l[:, s, w], f == 0, f == FB - 1)
                        last.then_inc(s_y[L], 1)

                def step(i, final):
                    for u in range(UPI):
                        if not (final and u == UPI - 1):
                            hidden((i,), u + 1)
                        output(i, u)

                hidden(0, 0)
                steps = NSUB[L] // 2
                with pe.Fori(0, steps - 1) as i:
                    step(i, False)
                step(steps - 1, True)

            def ranks(L):
                pe.wait_ge(s_oh, L + 1)
                nc.tensor.matmul(PS[:, 5, 0:8 * NT], TM[:, 0, :], SC[:, 3, 0:8 * NT], start=True, stop=True)
                nc.tensor.matmul(PS[:, 5, 8 * NT:16 * NT], ONE[:], SC[:, 3, 0:8 * NT],
                                 start=True, stop=True).then_inc(s_rank, 1)

            def blocks(L):
                NF = LAYERS[SPARSE[L]][1] // P

                def trans(i, k, par=None):
                    first = isinstance(i, int) and i == 0
                    pe.wait_ge(s_xb[L][k], i * 16 + 16)
                    if not first:
                        pe.wait_ge(s_xlo[L], i * 2 + k - 1)
                    for m in range(KD):
                        for tt in range(BTT):
                            last = nc.tensor.transpose(PS[:, 6 + k, m * BT + tt * P:m * BT + (tt + 1) * P],
                                                       XB[:, k, tt, m * P:(m + 1) * P], ident[:])
                    last.then_inc(s_xps[L], 1)

                def hidden(i, k, first=False):
                    q = i * 2 + k
                    pe.wait_ge(s_xlo[L], q + 1)
                    pe.wait_ge(s_w1sp[L], q + 1)
                    for f in range(NF):
                        if not first or f >= 4:
                            pe.wait_ge(s_hhi[SPARSE[L]], NF * q + f - 3)
                        out = PS[:, f % 4, (f // 4) * BT:(f // 4 + 1) * BT]
                        for m in range(KD):
                            w = slice((m * NF + f) * P, (m * NF + f + 1) * P)
                            last = mm3(out, WB1h[:, k, w], WB1l[:, k, w], XTh[:, k, m, :], XTl[:, k, m, :],
                                       m == 0, m == KD - 1)
                        last.then_inc(s_hps[SPARSE[L]], 1)

                def output(i, k):
                    q = i * 2 + k
                    pe.wait_ge(s_w2sp[L], q + 1)
                    pe.wait_ge(s_hlo[SPARSE[L]], NF // 2 * (q + 1))
                    for j in range(BTT):
                        pe.wait_ge(s_yev[L], BTT * q + j + 1)
                        for f in range(NF):
                            tok = slice((f % 2) * BT + j * P, (f % 2) * BT + (j + 1) * P)
                            w = slice(f * D, (f + 1) * D)
                            last = mm3(PS[:, 4 + j, 0:D], HTh[:, k, f // 2, tok], HTl[:, k, f // 2, tok],
                                       WB2h[:, k, w], WB2l[:, k, w], f == 0, f == NF - 1)
                        last.then_inc(s_y[SPARSE[L]], 1)

                steps = pe.value_load(BLK[L][0:1, 63:64], min_val=1, max_val=STEPS)
                trans(0, 0)
                hidden(0, 0, True)
                trans(0, 1)
                with pe.Fori(0, STEPS) as i:
                    with pe.If(i < steps):
                        hidden(i, 1)
                    with pe.If(i + 1 < steps):
                        trans(i + 1, 0)
                    with pe.If(i < steps):
                        output(i, 0)
                    with pe.If(i + 1 < steps):
                        hidden(i + 1, 0)
                        trans(i + 1, 1)
                    with pe.If(i < steps):
                        output(i, 1)

            def ffn3():
                fh, fl = FEAT[3]

                def hidden(i, u, first=False):
                    s, c = (u // NC) % 2, u % NC
                    if c == 0:
                        pe.wait_ge(s_wsplit[3], 1 if first else i * 2 + u // NC + 1)
                    for g in range(2):
                        if not first:
                            pe.wait_ge(s_hm3, i * UPI + u + 1)
                        for k in range(KD):
                            w = slice(k * D + g * P, k * D + (g + 1) * P)
                            last = mm3(PS[:, 2 * (u % 2) + g, :], W1h[:, s, w], W1l[:, s, w],
                                       fh[:, k, c * CH:(c + 1) * CH], fl[:, k, c * CH:(c + 1) * CH],
                                       k == 0, k == KD - 1)
                        last.then_inc(s_hps[3], 1)

                def output(i, u):
                    s = u // NC
                    pe.wait_ge(s_hlo[3], i * UPI + u + 1)
                    for j in range(TPC):
                        pe.wait_ge(s_yfree[3], YC + TPC * (i * UPI + u - 1) + j + 1)
                        tok = slice(j * P, (j + 1) * P)
                        mm3(PS[:, 4 + j, 0:D], HTh[:, u % 2, 0, tok], HTl[:, u % 2, 0, tok],
                            W2h[:, s, 0:D], W2l[:, s, 0:D], True, True).then_inc(s_y[3], 1)

                steps = pe.value_load(L3G[0:1, 63:64], min_val=1, max_val=STEPS3)
                hidden(0, 0, True)
                with pe.Fori(0, STEPS3) as i:
                    with pe.If(i < steps):
                        for u in range(UPI - 1):
                            hidden(i, u + 1)
                            output(i, u)
                        with pe.If(i + 1 < steps):
                            hidden(i, UPI)
                        output(i, UPI - 1)

            pe.wait_ge(s_const, 7)
            transposes("x0", X, lambda c: pe.wait_ge(s_x[c], 16))
            pe.wait_ge(s_csplit[0], 1)
            for c in range(NC):
                b = c // (NC // B)
                pe.wait_ge(s_tlo, TR0["x0"] + KD * (c + 1))
                if c >= 2:
                    pe.wait_ge(s_chi[0], c - 1)
                for k in range(KD):
                    w = slice(b * KD * A0 + k * A0, b * KD * A0 + (k + 1) * A0)
                    last = mm3(PS[0:A0, 4 + c % 2, :], W1h[:, 1, w], W1l[:, 1, w], TAh[:, k, c * CH:(c + 1) * CH],
                               TAl[:, k, c * CH:(c + 1) * CH], k == 0, k == KD - 1)
                last.then_inc(s_ch[0], 1)
                pe.wait_ge(s_clo[0], c + 1)
                for j in range(TPC):
                    n = c * TPC + j
                    if n >= 2:
                        pe.wait_ge(s_cyf, n - 1)
                    w = slice(256 + b * D, 256 + (b + 1) * D)
                    mm3(PS[:, 6 + n % 2, 0:D], HTh[0:A0, c % 2, 0, j * P:(j + 1) * P],
                        HTl[0:A0, c % 2, 0, j * P:(j + 1) * P], W1h[0:A0, 1, w], W1l[0:A0, 1, w],
                        True, True).then_inc(s_cy, 1)
            transposes("z0", Z, lambda c: pe.wait_ge(s_z0, TPC * (c + 1)))
            pe.wait_ge(s_rsplit, 4)
            routing(0, lambda c: pe.wait_ge(s_tlo, TR0["z0"] + KD * (c + 1)))
            bias(0)
            ffn(0)

            def tiles_done(L):
                if L in SPARSE:
                    return lambda c: pe.wait_ge(s_add, NT * (L - 1) + TPC * (c + 1))
                return lambda c: pe.wait_ge(s_yfree[L], 4 + TPC * (NSUB[L] * NC - NC + c + 1))

            transposes("x1", X, tiles_done(0))
            pe.wait_ge(s_csplit[1], 1)
            for c in range(NC):
                pe.wait_ge(s_tlo, TR0["x1"] + KD * (c + 1))
                if c >= 2:
                    pe.wait_ge(s_chf[1], c - 1)
                for k in range(KD):
                    w = slice(k * A0, (k + 1) * A0)
                    last = mm3(PS[0:A0, 4 + c % 2, :], W1h[:, 1, w], W1l[:, 1, w], TAh[:, k, c * CH:(c + 1) * CH],
                               TAl[:, k, c * CH:(c + 1) * CH], k == 0, k == KD - 1)
                last.then_inc(s_ch[1], 1)
            pe.wait_ge(s_chf[1], NC)
            pe.wait_ge(s_tlo, TR0["x1"] + KD * NC)
            pe.wait_ge(s_clo[1], 1)
            for n in range(NT):
                nc.tensor.matmul(PS[:, 6, n:n + 1], HF[0:A0, n // TPC, (n % TPC) * P:(n % TPC + 1) * P], V1[:],
                                 start=True, stop=True)
            for c in range(NC):
                last = nc.tensor.matmul(PS[:, c, :], SC[0:A0, 7, 0:P], HF[0:A0, c, :], start=True, stop=True)
            last.then_inc(s_sc, 1)
            pe.wait_ge(s_sc_sb, 1)
            pe.wait_ge(s_xr, NT + 1)
            for b in range(B):
                if b:
                    pe.wait_ge(s_z1, TPB * b)
                for lb in range(TPB):
                    q = b * TPB + lb
                    pe.wait_ge(s_plo, q + 1)
                    for jt in range(TPB):
                        last = mm3(PS[:, jt, 0:PW], HTh[:, q % 2, jt // 4, (jt % 4) * P:(jt % 4 + 1) * P],
                                   HTl[:, q % 2, jt // 4, (jt % 4) * P:(jt % 4 + 1) * P],
                                   XRh[:, q, :], XRl[:, q, :], lb == 0, lb == TPB - 1)
                    last.then_inc(s_pmm, 1)
            pe.wait_ge(s_z1, NT)
            transposes("z1", Z, lambda c: None)
            routing(1, lambda c: pe.wait_ge(s_tlo, TR0["z1"] + KD * (c + 1)))
            ranks(0)
            bias(1)
            blocks(0)

            def linear_cond(L):
                n = f"x{L}"
                transposes(n, X, tiles_done(L - 1))
                pe.wait_ge(s_csplit[L], 1)
                for c in range(NC):
                    b = c // (NC // B)
                    pe.wait_ge(s_tlo, TR0[n] + KD * (c + 1))
                    for m in range(KD):
                        g = KD * c + m
                        if g >= 4:
                            pe.wait_ge(s_chi[L], g - 3)
                        for k in range(KD):
                            w = slice((b * KD + k) * D + m * P, (b * KD + k) * D + (m + 1) * P)
                            last = mm3(PS[:, 4 + g % 4, :], W1h[:, 1, w], W1l[:, 1, w],
                                       TBhv[:, k, c * CH:(c + 1) * CH], TBlv[:, k, c * CH:(c + 1) * CH],
                                       k == 0, k == KD - 1)
                        last.then_inc(s_ch[L], 1)
                pe.wait_ge(s_clo[L], KD * NC)

            transposes("x2", X, tiles_done(1))
            pe.wait_ge(s_csplit[2], 1)
            for n in range(NT):
                if n % TPC == 0:
                    pe.wait_ge(s_tlo, TR0["x2"] + KD * (n // TPC + 1))
                if n >= 4:
                    pe.wait_ge(s_z2, n - 3)
                for k in range(KD):
                    w = slice((n // TPB * KD + k) * D, (n // TPB * KD + k + 1) * D)
                    last = mm3(PS[:, 4 + n % 4, 0:D], TBhv[:, k, n * P:(n + 1) * P], TBlv[:, k, n * P:(n + 1) * P],
                               W1h[:, 1, w], W1l[:, 1, w], k == 0, k == KD - 1)
                last.then_inc(s_c2y, 1)
            transposes("z2", Z, lambda c: pe.wait_ge(s_z2, TPC * (c + 1)))
            pe.wait_ge(s_tlo, TR0["z2"] + KD * NC)
            for c in range(NC):
                for k in range(KD):
                    last = mm3(PS[0:GR, c, :], Rh[2][:, k, :], Rl[2][:, k, :], TAh[:, k, c * CH:(c + 1) * CH],
                               TAl[:, k, c * CH:(c + 1) * CH], k == 0, k == KD - 1)
            last.then_inc(s_red, 1)
            pe.wait_ge(s_wgn, 1)
            nc.tensor.transpose(PS[0:GR, 5, 0:8], WG[:, 2 * GR:3 * GR], ident[0:8, 0:8]).then_inc(s_wgt, 1)
            pe.wait_ge(s_wgs, 1)
            pe.wait_ge(s_reds, 1)
            for n in range(NT):
                last = nc.tensor.matmul(PS[:, 4, n * 8:(n + 1) * 8], HF[0:GR, n // TPC, (n % TPC) * P:(n % TPC + 1) * P],
                                        WGT[:], start=True, stop=True)
            last.then_inc(s_lg[2], 1)
            ranks(1)
            bias(2)
            blocks(1)

            linear_cond(3)
            routing(3, lambda c: None)
            pe.wait_ge(s_cnt3, 1)
            nc.tensor.matmul(PS[:, 5, 0:E3], ONE[:], SC[:, 6, 0:E3], start=True, stop=True).then_inc(s_cnt3p, 1)
            pe.wait_ge(s_list3, 1)
            ffn3()

        @block.scalar
        def _(act):
            def transposes(n, dst):
                for g in range(KD * NC):
                    c, k = g // KD, g % KD
                    act.wait_ge(s_tps, TR0[n] + g + 1)
                    act.activation(dst[:, k, c * CH:(c + 1) * CH], PS[:, g % 4, :], ACT.Copy).then_inc(s_thi, 1)

            def exps(L, n):
                act.wait_ge(s_sub[L], 1)
                act.activation(SC[:, 1, 0:n], SC[:, 0, 0:n], ACT.Exp).then_inc(s_exp[L], 1)

            def gates_t(L):
                E = LAYERS[L][0]
                act.wait_ge(s_gt, L + 1)
                act.activation(SC[0:E, 4:8, :], PS[0:E, 0:4, :], ACT.Copy).then_inc(s_gts, 1)

            def ffn(L):
                func = LAYERS[L][2]
                BL = B1[L]

                def unit(i, u, first=False):
                    s, c = (u // NC), u % NC
                    for f in range(FB):
                        if first:
                            act.wait_ge(s_hps[L], f + 1)
                            b1 = BL[:, f:f + 1]
                        else:
                            act.wait_ge(s_hps[L], FB * (i * UPI + u) + f + 1)
                            act.wait_ge(s_hlo[L], FB * (i * UPI + u - 1) + f + 1)
                            act.wait_ge(s_yfree[L], TPC * (i * UPI + u))
                            b1 = BS[:, s * FB + f:s * FB + f + 1]
                        act.activation(HF[:, f, :], PS[:, f, :], func, bias=b1)
                        act.activation(HTh[:, u % 2, f, :], PS[:, f, :], func, bias=b1).then_inc(s_hhi[L], 1)

                def step(i, final):
                    n = (2 if final else 3) * FB
                    act.wait_ge(s_hhi[L], FB * (i * UPI + 1))
                    act.activation(BS[:, 0:n], BL[:, bass.ds(i * 2 * FB, n)], ACT.Copy).then_inc(s_b1[L], 1)
                    act.wait_ge(s_b1[L], i + 1)
                    for u in range(1, UPI + 1 - final):
                        unit(i, u)

                unit(0, 0, True)
                steps = NSUB[L] // 2
                with act.Fori(0, steps - 1) as i:
                    step(i, 0)
                step(steps - 1, 1)

            def blocks(L):
                func = LAYERS[SPARSE[L]][2]
                NF = LAYERS[SPARSE[L]][1] // P
                N1 = KD * NF * P
                act.wait_ge(s_list, L + 1)
                steps = act.value_load(BLK[L][0:1, 63:64], min_val=1, max_val=STEPS)

                def weights(i, k):
                    q = i * 2 + k
                    slot = BLK[L][0:1, q:q + 1] if isinstance(q, int) else BLK[L][0:1, bass.ds(q, 1)]
                    e = act.value_load(slot, min_val=0, max_val=7)
                    if not isinstance(q, int):
                        act.wait_ge(s_hhi[SPARSE[L]], NF * (q - 1))
                        act.wait_ge(s_bb[L], q)
                    act.activation(BB[:, k, 0:NF], B1[SPARSE[L]][:, bass.ds(e * NF, NF)], ACT.Copy).then_inc(s_bb[L], 1)
                    if not isinstance(q, int):
                        act.wait_ge(s_hps[SPARSE[L]], NF * (q - 1))
                    act.wait_ge(s_w1raw[L], q * 16 + 16)
                    act.activation(WB1h[:, k, 0:N1], ZW[0][:, 0:N1], ACT.Copy).then_inc(s_w1hi[L], 1)

                def xt(i, k):
                    q = i * 2 + k
                    act.wait_ge(s_xps[L], q + 1)
                    if not isinstance(q, int):
                        act.wait_ge(s_hps[SPARSE[L]], NF * (q - 1))
                    act.activation(XTh[:, k].rearrange("p k n -> p (k n)"), PS[:, 6 + k, :], ACT.Copy).then_inc(s_xhi[L], 1)

                def hidden(i, k, first=False):
                    q = i * 2 + k
                    act.wait_ge(s_bb[L], q + 1)
                    for f in range(NF):
                        act.wait_ge(s_hps[SPARSE[L]], NF * q + f + 1)
                        if not first:
                            act.wait_ge(s_hlo[SPARSE[L]], NF // 2 * (q - 1) + f // 2 + 1)
                            act.wait_ge(s_yev[L], BTT * q)
                        b1 = BB[:, k, f:f + 1]
                        part = slice((f % 2) * BT, (f % 2 + 1) * BT)
                        ps = PS[:, f % 4, (f // 4) * BT:(f // 4 + 1) * BT]
                        act.activation(HF[:, f // 2, part], ps, func, bias=b1)
                        act.activation(HTh[:, k, f // 2, part], ps, func,
                                       bias=b1).then_inc(s_hhi[SPARSE[L]], 1)

                weights(0, 0)
                xt(0, 0)
                hidden(0, 0, True)
                weights(0, 1)
                xt(0, 1)
                with act.Fori(0, STEPS) as i:
                    with act.If(i + 1 < steps):
                        weights(i + 1, 0)
                    with act.If(i < steps):
                        hidden(i, 1)
                    with act.If(i + 1 < steps):
                        xt(i + 1, 0)
                        weights(i + 1, 1)
                        hidden(i + 1, 0)
                        xt(i + 1, 1)

            def ffn3():
                act.wait_ge(s_list3, 1)
                steps = act.value_load(L3G[0:1, 63:64], min_val=1, max_val=STEPS3)

                def unit(i, u):
                    act.wait_ge(s_hps[3], 2 * (i * UPI + u) + 1)
                    act.activation(HF[:, u % 2, :], PS[:, 2 * (u % 2), :], ACT.Silu).then_inc(s_hf3, 1)
                    act.wait_ge(s_hm3, 2 + i * UPI + u + 1)
                    act.wait_ge(s_yfree[3], YC + TPC * (i * UPI + u - 1))
                    act.activation(HTh[:, u % 2, 0, :], HF[:, 2 + u % 2, :], ACT.Copy).then_inc(s_hhi[3], 1)

                with act.Fori(0, STEPS3) as i:
                    with act.If(i < steps):
                        for u in range(UPI):
                            unit(i, u)

            transposes("x0", TAh)
            act.wait_ge(s_small, 16 * N_SMALL)
            for c in range(NC):
                b = c // (NC // B)
                act.wait_ge(s_ch[0], c + 1)
                if c >= 1:
                    act.wait_ge(s_clo[0], c)
                if c >= 2:
                    act.wait_ge(s_cy, TPC * (c - 1))
                act.activation(HF[0:A0, 3, :], PS[0:A0, 4 + c % 2, :], ACT.Relu, bias=CB0[:, b:b + 1])
                act.activation(HTh[0:A0, c % 2, 0, :], PS[0:A0, 4 + c % 2, :], ACT.Relu,
                               bias=CB0[:, b:b + 1]).then_inc(s_chi[0], 1)
            act.wait_ge(s_var, 1)
            act.activation(SM[:, 0, :], SM[:, 0, :], ACT.Sqrt).then_inc(s_std, 1)
            transposes("z0", TBhv)
            exps(0, NT * 8)
            gates_t(0)
            ffn(0)
            transposes("x1", TAh)
            for n in range(NT):
                act.activation(XRh[:, n, 0:D], X[:, n, :], ACT.Copy).then_inc(s_act, 1)
            for c in range(NC):
                act.wait_ge(s_ch[1], c + 1)
                act.activation(HF[0:A0, c, :], PS[0:A0, 4 + c % 2, :], ACT.Tanh, bias=CB1[:, 0:1]).then_inc(s_chf[1], 1)
            act.wait_ge(s_sc, 1)
            act.activation(SM[:, 0, :], PS[:, 6, 0:NT], ACT.Copy)
            act.activation(SC[:, 0:4, :], PS[:, 0:4, :], ACT.Copy).then_inc(s_sc_sb, 1)
            for q in range(NT):
                act.wait_ge(s_arg, q + 1)
                if q >= 2:
                    act.wait_ge(s_pmm, q - 1)
                    act.wait_ge(s_plo, q - 1)
                act.activation(HF[:, 2 * (q % 2):2 * (q % 2) + 2, :], SC[:, 4 + 2 * (q % 2):6 + 2 * (q % 2), :],
                               ACT.Exp).then_inc(s_pf, 1)
                act.activation(HTh[:, q % 2, 0:2, :], SC[:, 4 + 2 * (q % 2):6 + 2 * (q % 2), :],
                               ACT.Exp).then_inc(s_phi, 1)
                if q % TPB == TPB - 1:
                    b = q // TPB
                    act.wait_ge(s_den, b + 1)
                    for jt in range(TPB):
                        n = b * TPB + jt
                        act.activation(Z[:, n, :], PS[:, jt, 0:D], ACT.Copy, scale=SM[:, 2, n:n + 1]).then_inc(s_z1, 1)
            transposes("z1", TAh)
            exps(1, NT * 8)
            gates_t(1)
            blocks(0)

            def linear_cond(L):
                transposes(f"x{L}", TBhv)
                CB = CB3
                for g in range(KD * NC):
                    c, m = g // KD, g % KD
                    act.wait_ge(s_ch[L], g + 1)
                    if g >= 4:
                        act.wait_ge(s_clo[L], g - 3)
                    act.activation(HF[:, g % 4, :], PS[:, 4 + g % 4, :], ACT.Identity, bias=CB[:, c // 2, m:m + 1])
                    act.activation(TAh[:, m, c * CH:(c + 1) * CH], PS[:, 4 + g % 4, :], ACT.Identity,
                                   bias=CB[:, c // 2, m:m + 1]).then_inc(s_chi[L], 1)

            transposes("x2", TBhv)
            transposes("z2", TAh)
            act.wait_ge(s_red, 1)
            act.activation(HF[0:GR, :, :], PS[0:GR, 0:4, :], ACT.Copy).then_inc(s_reds, 1)
            act.wait_ge(s_ss, 1)
            act.activation(SM[0:8, 4, 0:1], SM[0:8, 4, 0:1], ACT.Sqrt).then_inc(s_sq, 1)
            exps(2, NT * 8)
            gates_t(2)
            blocks(1)
            linear_cond(3)
            exps(3, NT * E3)
            ffn3()

        @block.vector
        def _(dve):
            steps_done = [0]

            def link(ins):
                steps_done[0] += 1
                ins.then_inc(s_dve, 1)
                dve.wait_ge(s_dve, steps_done[0])

            def lo(out, full, hi):
                return nc.vector.tensor_tensor(out, full, hi.bitcast(F32), ALU.subtract)

            def transposes(n, dh, dl):
                for g in range(KD * NC):
                    c, k = g // KD, g % KD
                    dve.wait_ge(s_thi, TR0[n] + g + 1)
                    lo(dl[:, k, c * CH:(c + 1) * CH], PS[:, g % 4, :], dh[:, k, c * CH:(c + 1) * CH]).then_inc(s_tlo, 1)

            def cond_split(L, loads, parts):
                dve.wait_ge(s_craw[L], 16 * loads)
                for rows, cols in parts:
                    link(nc.vector.tensor_copy(W1h[0:rows, 1, cols], W1r[0:rows, cols]))
                    last = lo(W1l[0:rows, 1, cols], W1r[0:rows, cols], W1h[0:rows, 1, cols])
                    link(last)
                dve.sem_inc(s_csplit[L], 1)

            def split_into(L, buf, s, after):
                n1, n2 = (KD * SUB, FB * D) if L < 3 else (KD * D, D)
                dve.wait_ge(s_wraw[L], s * 32 + 32)
                if after is not None:
                    dve.wait_ge(s_yfree[L], TPC + after)
                nc.vector.tensor_copy(W1h[:, buf, 0:n1], W1r[:, 0:n1]).then_inc(s_whi[L], 1)
                nc.vector.tensor_copy(W2h[:, buf, 0:n2], W2r[:, 0:n2]).then_inc(s_whi[L], 1)
                dve.wait_ge(s_whi[L], s * 2 + 1)
                lo(W1l[:, buf, 0:n1], W1r[:, 0:n1], W1h[:, buf, 0:n1])
                dve.wait_ge(s_whi[L], s * 2 + 2)
                lo(W2l[:, buf, 0:n2], W2r[:, 0:n2], W2h[:, buf, 0:n2]).then_inc(s_wsplit[L], 1)

            def softmax(L, E):
                lg = SC[:, 0, 0:NT * E].rearrange("p (t e) -> p t e", e=E)
                pr = SC[:, 1, 0:NT * E].rearrange("p (t e) -> p t e", e=E)
                ps = PS[:, 4, 0:NT * E].rearrange("p (t e) -> p t e", e=E)
                dve.wait_ge(s_lg[L], 1)
                if L < 2:
                    link(nc.vector.tensor_tensor(lg, ps, BR[L][:].unsqueeze(1).broadcast_to([P, NT, E]), ALU.add))
                else:
                    link(nc.vector.tensor_copy(lg, ps))
                link(nc.vector.tensor_reduce(SM[:, 5, :], lg, axis=AX.X, op=ALU.max))
                nc.vector.tensor_tensor(lg, lg, SM[:, 5, :].unsqueeze(2).broadcast_to([P, NT, E]),
                                        ALU.subtract).then_inc(s_sub[L], 1)
                dve.wait_ge(s_exp[L], 1)
                link(nc.vector.tensor_reduce(SM[:, 6, :], pr, axis=AX.X, op=ALU.add))
                link(nc.vector.reciprocal(SM[:, 7, :], SM[:, 6, :]))
                return lg, pr

            def bc(col, E):
                return col.unsqueeze(2).broadcast_to([P, NT, E])

            def running(E):
                link(nc.vector.memset(RS, 1.0))
                link(nc.vector.memset(RS.rearrange("p (t e) -> p t e", e=E)[:, :, 0:1], 0.0))
                link(nc.vector.tensor_tensor_scan(SC[:, 3, 0:NT * E], RS[:, 0:NT * E], SC[:, 2, 0:NT * E],
                                                  0.0, ALU.mult, ALU.add))

            def top1(L):
                lg, pr = softmax(L, 8)
                eq = SC[:, 2, 0:NT * 8].rearrange("p (t e) -> p t e", e=8)
                run = SC[:, 3, 0:NT * 8].rearrange("p (t e) -> p t e", e=8)
                link(nc.vector.tensor_single_scalar(eq, lg, 0.0, ALU.is_equal))
                running(8)
                link(nc.vector.scalar_tensor_tensor(run, run, 1.0, eq, ALU.is_equal, ALU.mult))
                dve.sem_inc(s_oh, 1)
                link(nc.vector.tensor_tensor(pr, pr, bc(SM[:, 7, :], 8), ALU.mult))
                nc.vector.tensor_tensor(G[:, :, 0:8], run, pr, ALU.mult).then_inc(s_gate[L], 1)

            def order(L):
                ET = 8 * NT
                pick = SC[:, 3, 0:ET].rearrange("p (t e) -> p t e", e=8)
                tot, cum, off = (SC[:, 0, k * ET:(k + 1) * ET] for k in range(3))
                et = "p (e t) -> p e t"
                tmp = SC[:, 2, 0:ET].rearrange("p (t e) -> p t e", e=8)
                cmp = SC[:, 2, ET:ET + 64].rearrange("p (e k) -> p e k", k=8)
                own, upto, even = (SC[:, 2, 256 + 8 * k:264 + 8 * k] for k in range(3))
                dve.wait_ge(s_rank, L + 1)
                link(nc.vector.tensor_copy(tot.rearrange(et, e=8),
                                           PS[:, 5, ET:2 * ET].rearrange("p (t e) -> p e t", e=8)))
                link(nc.vector.tensor_tensor_scan(cum, RS16[:], tot, 0.0, ALU.mult, ALU.add))
                count = cum.rearrange(et, e=8)[:, :, NT - 1:NT]
                link(nc.vector.tensor_scalar(even, IO[:, 0:8], float(BT), None, ALU.mult))
                link(nc.vector.tensor_tensor(cmp, count.broadcast_to([P, 8, 8]),
                                             even.unsqueeze(1).broadcast_to([P, 8, 8]), ALU.is_gt))
                link(nc.vector.tensor_reduce(own, cmp, axis=AX.X, op=ALU.add))
                link(nc.vector.tensor_tensor_scan(upto, ONE[:, 0:8], own, 0.0, ALU.mult, ALU.add))
                link(nc.vector.tensor_tensor(own, upto, own, ALU.subtract))
                link(nc.vector.tensor_tensor(off, cum, tot, ALU.subtract))
                link(nc.vector.scalar_tensor_tensor(off.rearrange(et, e=8), own.unsqueeze(2).broadcast_to([P, 8, NT]),
                                                    float(BT), off.rearrange(et, e=8), ALU.mult, ALU.add))
                link(nc.vector.tensor_tensor(tmp, PS[:, 5, 0:ET].rearrange("p (t e) -> p t e", e=8),
                                             off.rearrange("p (e t) -> p t e", e=8), ALU.add))
                link(nc.vector.tensor_tensor(tmp, tmp, pick, ALU.mult))
                link(nc.vector.tensor_reduce(SLOTf[:], tmp, axis=AX.X, op=ALU.add))
                link(nc.vector.tensor_scalar(SLOTf[:], SLOTf[:], -1.0, None, ALU.add))
                link(nc.vector.tensor_copy(SLOT[:], SLOTf[:]))
                hit = SC[0:1, 2, 288:288 + BLOCKS * 8].rearrange("p (b e) -> p b e", e=8)
                exp = SC[0:1, 2, 424:424 + BLOCKS]
                link(nc.vector.tensor_tensor(hit, upto[0:1].unsqueeze(1).broadcast_to([1, BLOCKS, 8]),
                                             IO[0:1, 0:BLOCKS].unsqueeze(2).broadcast_to([1, BLOCKS, 8]), ALU.is_le))
                link(nc.vector.tensor_reduce(exp, hit, axis=AX.X, op=ALU.add))
                link(nc.vector.tensor_scalar(exp, exp, 7.0, None, ALU.min))
                link(nc.vector.tensor_copy(BLK[L][:, 0:BLOCKS], exp))
                link(nc.vector.tensor_scalar(even[0:1], IO[0:1, 0:8], 2.0, None, ALU.mult))
                link(nc.vector.tensor_scalar(even[0:1], even[0:1], upto[0:1, 7:8], None, ALU.is_lt))
                link(nc.vector.tensor_reduce(exp[:, 0:1], even[0:1], axis=AX.X, op=ALU.add))
                nc.vector.tensor_copy(BLK[L][:, 63:64], exp[:, 0:1]).then_inc(s_list, 1)
                dve.wait_ge(s_gate[SPARSE[L]], 1)
                link(nc.vector.tensor_reduce(SM[:, 1, :], G[:, :, 0:8], axis=AX.X, op=ALU.add))

            def blocks(L):
                NF = LAYERS[SPARSE[L]][1] // P
                N1, N2 = KD * NF * P, NF * D
                dve.wait_ge(s_list, L + 1)
                steps = dve.value_load(BLK[L][0:1, 63:64], min_val=1, max_val=STEPS)

                def w1_lo(q, k):
                    dve.wait_ge(s_w1hi[L], q + 1)
                    lo(WB1l[:, k, 0:N1], ZW[0][:, 0:N1], WB1h[:, k, 0:N1]).then_inc(s_w1sp[L], 1)

                def w2_split(q, k):
                    dve.wait_ge(s_w2raw[L], q * 16 + 16)
                    nc.vector.tensor_copy(WB2h[:, k, 0:N2], ZW[1][:, 0:N2]).then_inc(s_w2hi[L], 1)
                    dve.wait_ge(s_w2hi[L], q + 1)
                    lo(WB2l[:, k, 0:N2], ZW[1][:, 0:N2], WB2h[:, k, 0:N2]).then_inc(s_w2sp[L], 1)

                def x_lo(q, k):
                    dve.wait_ge(s_xhi[L], q + 1)
                    lo(XTl[:, k].rearrange("p k n -> p (k n)"), PS[:, 6 + k, :],
                       XTh[:, k].rearrange("p k n -> p (k n)")).then_inc(s_xlo[L], 1)

                def lows(q, k, pairs):
                    for f in pairs:
                        dve.wait_ge(s_hhi[SPARSE[L]], NF * q + 2 * f + 2)
                        lo(HTl[:, k, f, :], HF[:, f, :], HTh[:, k, f, :]).then_inc(s_hlo[SPARSE[L]], 1)

                def outputs(q, k):
                    dve.wait_ge(s_yb[L], q + 1)
                    for j in range(BTT):
                        dve.wait_ge(s_y[SPARSE[L]], BTT * q + j + 1)
                        nc.vector.tensor_copy(YB[:, k, j, :], PS[:, 4 + j, 0:D]).then_inc(s_yev[L], 1)

                early, late = range(NF // 4), range(NF // 4, NF // 2)
                dve.sem_inc(s_yev[L], BTT)
                w1_lo(0, 0)
                x_lo(0, 0)
                lows(0, 0, early)
                w2_split(0, 0)
                lows(0, 0, late)
                w1_lo(1, 1)
                x_lo(1, 1)
                with dve.Fori(0, STEPS) as i:
                    with dve.If(i + 1 < steps):
                        w1_lo(i * 2 + 2, 0)
                    with dve.If(i < steps):
                        lows(i * 2 + 1, 1, early)
                        w2_split(i * 2 + 1, 1)
                        lows(i * 2 + 1, 1, late)
                    with dve.If(i + 1 < steps):
                        x_lo(i * 2 + 2, 0)
                    with dve.If(i < steps):
                        outputs(i * 2, 0)
                    with dve.If(i + 1 < steps):
                        w1_lo(i * 2 + 3, 1)
                        lows(i * 2 + 2, 0, early)
                        w2_split(i * 2 + 2, 0)
                        lows(i * 2 + 2, 0, late)
                        x_lo(i * 2 + 3, 1)
                    with dve.If(i < steps):
                        outputs(i * 2 + 1, 1)
                for n in range(NT):
                    if n % TPC == 0:
                        dve.wait_ge(s_gath[n // TPC], 16 * TPC * (L + 1))
                    nc.vector.scalar_tensor_tensor(X[:, n, :], Z[:, n, :], SM[:, 1, n:n + 1], X[:, n, :],
                                                   ALU.mult, ALU.add).then_inc(s_add, 1)

            def bias(L):
                for n in range(NT):
                    dve.wait_ge(s_by, NT * L + n + 1)
                    nc.vector.tensor_tensor(X[:, n, :], PS[:, 4 + n % 4, 0:D], X[:, n, :], ALU.add).then_inc(s_bu, 1)

            def ffn(L):
                def lows(i, u, first=False):
                    for f in range(FB):
                        dve.wait_ge(s_hhi[L], f + 1 if first else FB * (i * UPI + u) + f + 1)
                        lo(HTl[:, u % 2, f, :], HF[:, f, :], HTh[:, u % 2, f, :]).then_inc(s_hlo[L], 1)

                def gated(i, u):
                    c, s = u % NC, u // NC
                    e = (i if L < 2 else i * 2 + s)
                    for j in range(TPC):
                        n = c * TPC + j
                        dve.wait_ge(s_y[L], TPC * (i * UPI + u) + j + 1)
                        nc.vector.scalar_tensor_tensor(X[:, n, :], PS[:, 4 + j, 0:D], G[:, n, bass.ds(e, 1)],
                                                       X[:, n, :], ALU.mult, ALU.add).then_inc(s_yfree[L], 1)

                def step(i, final):
                    for u in range(UPI):
                        if not (final and u == UPI - 1):
                            lows(i, u + 1)
                        gated(i, u)
                        if u == 0:
                            split_into(L, 1, i * 2 + 1, TPC * UPI * i)
                        if u == 4 and not final:
                            split_into(L, 0, i * 2 + 2, TPC * (UPI * i + NC))

                split_into(L, 0, 0, None)
                dve.sem_inc(s_yfree[L], TPC)
                lows(0, 0, True)
                steps = NSUB[L] // 2
                with dve.Fori(0, steps - 1) as i:
                    step(i, False)
                step(steps - 1, True)

            def ffn3():
                def mid(i, u):
                    dve.wait_ge(s_hf3, i * UPI + u + 1)
                    dve.wait_ge(s_hps[3], 2 * (i * UPI + u) + 2)
                    nc.vector.tensor_tensor(HF[:, 2 + u % 2, :], HF[:, u % 2, :], PS[:, 2 * (u % 2) + 1, :],
                                            ALU.mult).then_inc(s_hm3, 1)
                    dve.wait_ge(s_hhi[3], i * UPI + u + 1)
                    lo(HTl[:, u % 2, 0, :], HF[:, 2 + u % 2, :], HTh[:, u % 2, 0, :]).then_inc(s_hlo[3], 1)

                steps = dve.value_load(L3G[0:1, 63:64], min_val=1, max_val=STEPS3)

                def gated(i, u, e):
                    c = u % NC
                    for j in range(TPC):
                        n = c * TPC + j
                        dve.wait_ge(s_y[3], TPC * (i * UPI + u) + j + 1)
                        nc.vector.scalar_tensor_tensor(X[:, n, :], PS[:, 4 + j, 0:D], G[:, n, bass.ds(e, 1)],
                                                       X[:, n, :], ALU.mult, ALU.add).then_inc(s_yfree[3], 1)

                split_into(3, 0, 0, None)
                dve.sem_inc(s_yfree[3], YC)
                dve.sem_inc(s_hm3, 2)
                mid(0, 0)
                with dve.Fori(0, STEPS3) as i:
                    with dve.If(i < steps):
                        for s in range(2):
                            e = dve.value_load(L3G[0:1, bass.ds(i * 2 + s, 1)], min_val=0, max_val=E3S)
                            for u in range(s * NC, (s + 1) * NC):
                                if u < UPI - 1:
                                    mid(i, u + 1)
                                else:
                                    with dve.If(i + 1 < steps):
                                        mid(i, UPI)
                                gated(i, u, e)
                                if u == 0:
                                    split_into(3, 1, i * 2 + 1, YC - TPC + TPC * UPI * i)
                                if u == NC:
                                    with dve.If(i + 1 < steps):
                                        split_into(3, 0, i * 2 + 2, YC - TPC + TPC * (UPI * i + NC))
                dve.drain().then_inc(s_done3, 1)

            dve.wait_ge(s_const, 7)
            link(nc.vector.tensor_copy(IO[:], IOi[:]))
            link(nc.vector.memset(RS16[:], 1.0))
            link(nc.vector.memset(RS16[:].rearrange("p (e t) -> p e t", t=NT)[:, :, 0:1], 0.0))
            dve.wait_ge(s_small, 16 * N_SMALL)
            for L in range(4):
                link(nc.vector.tensor_copy(Rh[L][:], Rr[L][:]))
                lo(Rl[L][:], Rr[L][:], Rh[L][:]).then_inc(s_rsplit, 1)
            cond_split(0, 2 * B, [(P, slice(0, 256)), (A0, slice(256, 256 + B * D))])
            transposes("x0", TAh, TAl)
            for c in range(NC):
                b = c // (NC // B)
                dve.wait_ge(s_chi[0], c + 1)
                lo(HTl[0:A0, c % 2, 0, :], HF[0:A0, 3, :], HTh[0:A0, c % 2, 0, :]).then_inc(s_clo[0], 1)
                for j in range(TPC):
                    n = c * TPC + j
                    dve.wait_ge(s_cy, n + 1)
                    nc.vector.tensor_tensor(Z[:, n, :], PS[:, 6 + n % 2, 0:D], X[:, n, :], ALU.add).then_inc(s_cyf, 1)
                    if n == 0:
                        dve.wait_ge(s_rows, 16 * 3 * B)
                    dve.wait_ge(s_cyf, n + 1)
                    link(nc.vector.tensor_tensor(Z[:, n, :], Z[:, n, :], HF[:, 0, b * D:(b + 1) * D], ALU.add))
                    link(nc.vector.bn_stats(ST[:], Z[:, n, :]))
                    link(nc.vector.bn_aggr(MV[:, n, :], ST[:]))
            nc.vector.tensor_scalar(SM[:, 0, :], MV[:, :, 1], LN_EPS, None, ALU.add).then_inc(s_var, 1)
            dve.wait_ge(s_std, 1)
            link(nc.vector.reciprocal(SM[:, 1, :], SM[:, 0, :]))
            for n in range(NT):
                nc.vector.tensor_scalar(Z[:, n, :], Z[:, n, :], MV[:, n, 0:1], SM[:, 1, n:n + 1],
                                        ALU.subtract, ALU.mult).then_inc(s_norm, 1)
            transposes("z0", TBhv, TBlv)
            dve.wait_ge(s_zst, 16 * 2 * BLOCKS * BT // (P * NT))
            lg, pr = softmax(0, 8)
            link(nc.vector.tensor_tensor(pr, pr, bc(SM[:, 7, :], 8), ALU.mult))
            before = SC[:, 2, 0:NT * 8].rearrange("p (t e) -> p t e", e=8)
            term = SC[:, 3, 0:NT * 8].rearrange("p (t e) -> p t e", e=8)
            link(nc.vector.memset(before, 0.0))
            for j in range(8):
                pj = pr[:, :, j:j + 1]
                if j:
                    nc.vector.tensor_tensor(term[:, :, 0:j], pr[:, :, 0:j], pj.broadcast_to([P, NT, j]), ALU.is_lt)
                if j < 7:
                    nc.vector.tensor_tensor(term[:, :, j + 1:8], pr[:, :, j + 1:8],
                                            pj.broadcast_to([P, NT, 7 - j]), ALU.is_le)
                link(nc.vector.memset(term[:, :, j:j + 1], 0.0))
                link(nc.vector.tensor_tensor(term, term, pj.broadcast_to([P, NT, 8]), ALU.mult))
                link(nc.vector.tensor_tensor(before, before, term, ALU.add))
            link(nc.vector.tensor_tensor(term, before, pr, ALU.add))
            link(nc.vector.tensor_single_scalar(term, term, TOP_P, ALU.is_lt))
            link(nc.vector.scalar_tensor_tensor(term, before, 0.0, term, ALU.is_equal, ALU.max))
            nc.vector.tensor_tensor(G[:, :, 0:8], term, pr, ALU.mult).then_inc(s_gate[0], 1)
            bias(0)
            ffn(0)
            cond_split(1, 1, [(P, slice(0, KD * A0))])
            link(nc.vector.tensor_copy(SC[0:A0, 7, 0:P], V1[:].broadcast_to([A0, P])))
            dve.sem_inc(s_clo[1], 1)
            transposes("x1", TAh, TAl)
            for n in range(NT):
                dve.wait_ge(s_act, n + 1)
                lo(XRl[:, n, 0:D], X[:, n, :], XRh[:, n, 0:D]).then_inc(s_xr, 1)
            nc.vector.tensor_copy(XRh[:, :, D:D + 2], ONE[:, 0:2].unsqueeze(1).broadcast_to([P, NT, 2]))
            link(nc.vector.tensor_scalar(XRl[:, :, D:D + 2], ONE[:, 0:2].unsqueeze(1).broadcast_to([P, NT, 2]),
                                         0.0, None, ALU.mult))
            dve.sem_inc(s_xr, 1)
            dve.wait_ge(s_mode, 16)
            link(nc.vector.tensor_copy(MD[:, :, 7], MODEi[:]))
            nc.vector.tensor_single_scalar(MD[:, :, 0], MD[:, :, 7], 0.0, ALU.is_equal)
            link(nc.vector.tensor_single_scalar(MD[:, :, 1], MD[:, :, 7], 1.0, ALU.is_equal))
            link(nc.vector.tensor_tensor(MD[:, :, 6], MD[:, :, 0], MD[:, :, 1], ALU.add))
            link(nc.vector.tensor_scalar(MD[:, :, 2], MD[:, :, 6], -1.0, 1.0, ALU.mult, ALU.add))
            nc.vector.tensor_scalar(MD[:, :, 3], MD[:, :, 0], NEG, None, ALU.mult)
            link(nc.vector.tensor_scalar(MD[:, :, 4], MD[:, :, 1], NEG, None, ALU.mult))
            link(nc.vector.tensor_copy(JC[:], JCi[:]))
            for b in range(B):
                m = [MD[:, b, k:k + 1] for k in range(8)]
                link(nc.vector.tensor_scalar(DM[:, b, :], TM[:, 0, :], m[0], None, ALU.mult))
                link(nc.vector.scalar_tensor_tensor(DM[:, b, :], TM[:, 1, :], m[1], DM[:, b, :], ALU.mult, ALU.add))
                link(nc.vector.scalar_tensor_tensor(DM[:, b, :], TM[:, 2, :], m[2], DM[:, b, :], ALU.mult, ALU.add))
                link(nc.vector.tensor_scalar(DM[:, b, :], DM[:, b, :], -NEG, NEG, ALU.mult, ALU.add))
                cnt = SM[:, 3, b * TPB:(b + 1) * TPB]
                tmp = SM[:, 4, b * TPB:(b + 1) * TPB]
                link(nc.vector.tensor_scalar(tmp, JC[:], 1.0, None, ALU.add))
                link(nc.vector.tensor_scalar(cnt, tmp, m[0], None, ALU.mult))
                link(nc.vector.tensor_scalar(tmp, JC[:], -1.0, float(SEQ), ALU.mult, ALU.add))
                link(nc.vector.scalar_tensor_tensor(cnt, tmp, m[1], cnt, ALU.mult, ALU.add))
                link(nc.vector.memset(tmp, float(SEQ - 1)))
                link(nc.vector.scalar_tensor_tensor(cnt, tmp, m[2], cnt, ALU.mult, ALU.add))
            dve.wait_ge(s_sc_sb, 1)
            for b in range(B):
                m = [MD[:, b, k:k + 1] for k in range(8)]
                cols = SM[:, 0, b * TPB:(b + 1) * TPB]
                sl = SM[:, 5, b * TPB:(b + 1) * TPB]
                su = SM[:, 6, b * TPB:(b + 1) * TPB]
                nc.vector.tensor_scalar(sl, cols, m[3], None, ALU.add)
                nc.vector.tensor_scalar(su, cols, m[4], None, ALU.add)
                row = SC[:, 2 * b:2 * b + 2, :].rearrange("p a c -> p (a c)")
                pre, suf, oth = (Z[:, 4 * k:4 * k + 4, :].rearrange("p a c -> p (a c)") for k in range(3))
                link(nc.vector.tensor_tensor_scan(pre, row, row, -3e38, ALU.max, ALU.max))
                link(nc.vector.tensor_tensor_scan(suf[:, ::-1], row[:, ::-1], row[:, ::-1], -3e38, ALU.max, ALU.max))
                nc.vector.tensor_tensor(oth[:, 1:SEQ - 1], pre[:, 0:SEQ - 2], suf[:, 2:SEQ], ALU.max)
                nc.vector.tensor_copy(oth[:, 0:1], suf[:, 1:2])
                link(nc.vector.tensor_copy(oth[:, SEQ - 1:SEQ], pre[:, SEQ - 2:SEQ - 1]))
                link(nc.vector.tensor_scalar(row, pre, m[0], -1.0, ALU.mult, ALU.mult))
                link(nc.vector.tensor_scalar(pre, suf, m[1], -1.0, ALU.mult, ALU.mult))
                link(nc.vector.tensor_tensor(row, row, pre, ALU.add))
                link(nc.vector.tensor_scalar(pre, oth, m[2], -1.0, ALU.mult, ALU.mult))
                link(nc.vector.tensor_tensor(row, row, pre, ALU.add))
            for b in range(B):
                cols = SM[:, 0, b * TPB:(b + 1) * TPB]
                sl = SM[:, 5, b * TPB:(b + 1) * TPB]
                su = SM[:, 6, b * TPB:(b + 1) * TPB]
                row = SC[:, 2 * b:2 * b + 2, :].rearrange("p a c -> p (a c)")
                for lb in range(TPB):
                    q = b * TPB + lb
                    if q >= 2:
                        dve.wait_ge(s_phi, q - 1)
                    arg = SC[:, 4 + 2 * (q % 2):6 + 2 * (q % 2), :].rearrange("p a c -> p (a c)")
                    diag = slice(lb * P, (lb + 1) * P)
                    if lb:
                        nc.vector.tensor_scalar(arg[:, 0:lb * P], row[:, 0:lb * P], sl[:, lb:lb + 1], 0.0,
                                                ALU.add, ALU.min)
                    if lb < TPB - 1:
                        nc.vector.tensor_scalar(arg[:, (lb + 1) * P:], row[:, (lb + 1) * P:], su[:, lb:lb + 1], 0.0,
                                                ALU.add, ALU.min)
                    link(nc.vector.tensor_scalar(arg[:, diag], row[:, diag], cols[:, lb:lb + 1], 0.0,
                                                 ALU.add, ALU.min))
                    nc.vector.tensor_tensor(arg[:, diag], arg[:, diag], DM[:, b, :], ALU.add).then_inc(s_arg, 1)
                    if lb:
                        pooled_lo = q - 1
                        dve.wait_ge(s_phi, pooled_lo + 1)
                        lo(HTl[:, pooled_lo % 2, 0:2, :], HF[:, 2 * (pooled_lo % 2):2 * (pooled_lo % 2) + 2, :],
                           HTh[:, pooled_lo % 2, 0:2, :]).then_inc(s_plo, 1)
                q = b * TPB + TPB - 1
                dve.wait_ge(s_phi, q + 1)
                lo(HTl[:, q % 2, 0:2, :], HF[:, 2 * (q % 2):2 * (q % 2) + 2, :], HTh[:, q % 2, 0:2, :]).then_inc(s_plo, 1)
                dve.wait_ge(s_pmm, q + 1)
                bs = slice(b * TPB, (b + 1) * TPB)
                link(nc.vector.tensor_tensor(SM[:, 4, bs], PS[:, :, D], SM[:, 3, bs], ALU.mult))
                nc.vector.reciprocal(SM[:, 2, bs], SM[:, 4, bs]).then_inc(s_den, 1)
            transposes("z1", TAh, TAl)
            top1(1)
            order(0)
            bias(1)
            blocks(0)

            def linear_cond(L):
                cond_split(L, B, [(P, slice(0, B * KD * D))])
                transposes(f"x{L}", TBhv, TBlv)
                for g in range(KD * NC):
                    c, m = g // KD, g % KD
                    dve.wait_ge(s_chi[L], g + 1)
                    lo(TAl[:, m, c * CH:(c + 1) * CH], HF[:, g % 4, :], TAh[:, m, c * CH:(c + 1) * CH]).then_inc(s_clo[L], 1)

            link(nc.vector.tensor_tensor(WG[:, GR:2 * GR], WG[:, 0:GR], WG[:, 0:GR], ALU.mult))
            nc.vector.tensor_reduce(SM[0:8, 4, 0:1], WG[:, GR:2 * GR], axis=AX.X, op=ALU.add).then_inc(s_ss, 1)
            cond_split(2, B, [(P, slice(0, B * KD * D))])
            transposes("x2", TBhv, TBlv)
            dve.wait_ge(s_row, 16 * B)
            for n in range(NT):
                dve.wait_ge(s_c2y, n + 1)
                b = n // TPB
                nc.vector.tensor_tensor(Z[:, n, :], PS[:, 4 + n % 4, 0:D], W2r[:, b * D:(b + 1) * D],
                                        ALU.add).then_inc(s_z2, 1)
            transposes("z2", TAh, TAl)
            dve.wait_ge(s_sq, 1)
            link(nc.vector.tensor_scalar(SM[0:8, 4, 1:2], SM[0:8, 4, 0:1], 1e-4, None, ALU.max))
            link(nc.vector.reciprocal(SM[0:8, 4, 2:3], SM[0:8, 4, 1:2]))
            nc.vector.tensor_scalar(WG[:, 2 * GR:3 * GR], WG[:, 0:GR], SM[0:8, 4, 2:3], None, ALU.mult).then_inc(s_wgn, 1)
            dve.wait_ge(s_wgt, 1)
            nc.vector.tensor_copy(WGT[:], PS[0:GR, 5, 0:8]).then_inc(s_wgs, 1)
            top1(2)
            order(1)
            bias(2)
            blocks(1)
            linear_cond(3)
            lg, pr = softmax(3, E3)
            link(nc.vector.tensor_tensor(pr, pr, bc(SM[:, 7, :], E3), ALU.mult))
            link(nc.vector.tensor_tensor(lg, pr, BR[3][:].unsqueeze(1).broadcast_to([P, NT, E3]), ALU.add))
            for n in range(NT):
                last = nc.vector.max(SC[:, 4, n * 8:(n + 1) * 8], lg[:, n, :])
            link(last)
            bar = SC[:, 4, 0:NT * 8].rearrange("p (t e) -> p t e", e=8)[:, :, TOP_K - 1:TOP_K].broadcast_to([P, NT, E3])
            eq = SC[:, 2, :].rearrange("p (t e) -> p t e", e=E3)
            run = SC[:, 3, :].rearrange("p (t e) -> p t e", e=E3)
            gt = SC[:, 5, :].rearrange("p (t e) -> p t e", e=E3)
            nc.vector.tensor_tensor(gt, lg, bar, ALU.is_gt)
            link(nc.vector.tensor_tensor(eq, lg, bar, ALU.is_equal))
            link(nc.vector.tensor_reduce(SM[:, 5, :], gt, axis=AX.X, op=ALU.add))
            running(E3)
            link(nc.vector.tensor_tensor(run, run, bc(SM[:, 5, :], E3), ALU.add))
            link(nc.vector.scalar_tensor_tensor(run, run, float(TOP_K), eq, ALU.is_le, ALU.mult))
            link(nc.vector.tensor_tensor(run, run, gt, ALU.add))
            nc.vector.tensor_reduce(SC[:, 6, 0:E3], run.rearrange("p t e -> p e t"), axis=AX.X,
                                    op=ALU.add).then_inc(s_cnt3, 1)
            dve.wait_ge(s_cnt3, 1)
            link(nc.vector.tensor_tensor(run, run, pr, ALU.mult))
            link(nc.vector.tensor_reduce(SM[:, 5, :], run, axis=AX.X, op=ALU.add))
            link(nc.vector.tensor_scalar(SM[:, 6, :], SM[:, 5, :], 1e-12, None, ALU.max))
            link(nc.vector.reciprocal(SM[:, 7, :], SM[:, 6, :]))
            link(nc.vector.tensor_tensor(G[:, :, 0:E3], run, bc(SM[:, 7, :], E3), ALU.mult))
            link(nc.vector.memset(G[:, :, E3:E3S], 1.0))
            link(nc.vector.memset(G[:, :, E3S:E3S + 1], 0.0))
            used, place, val = (SC[0:1, 7, 64 * k:64 * k + E3] for k in range(3))
            wl, gl, inuse = (SC[0:1, 7, 192 + 64 * k:192 + 64 * k + E3S] for k in range(3))
            num = SC[0:1, 7, 384:385]
            hit = Z[0:1, 0:5, :].rearrange("p a c -> p (a c)")[:, 0:E3S * E3].rearrange("p (i e) -> p i e", e=E3)
            dve.wait_ge(s_cnt3p, 1)
            link(nc.vector.tensor_single_scalar(used, PS[0:1, 5, 0:E3], 0.0, ALU.is_gt))
            link(nc.vector.tensor_tensor_scan(place, ONE[0:1, 0:E3], used, 0.0, ALU.mult, ALU.add))
            link(nc.vector.tensor_scalar(num, place[:, E3 - 1:E3], 2.0, None, ALU.add))
            link(nc.vector.tensor_tensor(place, place, used, ALU.subtract))
            link(nc.vector.tensor_scalar(place, place, 2.0, None, ALU.add))
            link(nc.vector.tensor_tensor(val, used, IO[0:1, 0:E3], ALU.mult))
            link(nc.vector.tensor_tensor(hit, IO[0:1, 0:E3S].unsqueeze(2).broadcast_to([1, E3S, E3]),
                                         place.unsqueeze(1).broadcast_to([1, E3S, E3]), ALU.is_equal))
            link(nc.vector.tensor_tensor(hit, hit, val.unsqueeze(1).broadcast_to([1, E3S, E3]), ALU.mult))
            link(nc.vector.tensor_reduce(wl, hit, axis=AX.X, op=ALU.add))
            link(nc.vector.tensor_scalar(wl[:, 0:2], IO[0:1, 0:2], float(E3), None, ALU.add))
            link(nc.vector.tensor_scalar(inuse, IO[0:1, 0:E3S], num, float(E3S), ALU.is_ge, ALU.mult))
            link(nc.vector.tensor_tensor(gl, wl, inuse, ALU.max))
            link(nc.vector.tensor_copy(L3W[:, 0:E3S], wl))
            link(nc.vector.tensor_copy(L3G[:, 0:E3S], gl))
            link(nc.vector.tensor_scalar(val[:, 0:STEPS3], IO[0:1, 0:STEPS3], 2.0, None, ALU.mult))
            link(nc.vector.tensor_scalar(val[:, 0:STEPS3], val[:, 0:STEPS3], num, None, ALU.is_lt))
            link(nc.vector.tensor_reduce(num, val[:, 0:STEPS3], axis=AX.X, op=ALU.add))
            nc.vector.tensor_copy(L3G[:, 63:64], num).then_inc(s_list3, 1)
            dve.wait_ge(s_list3, 1)
            ffn3()


def kernel(**inputs):
    import numpy as np
    import concourse.bacc as bacc
    from concourse.bass_utils import run_bass_kernel_spmd

    a = {k: np.asarray(v) for k, v in inputs.items()}
    ins = {n: a[n] for n in (
        "x", "L0_cond_b1", "L0_cond_W1", "L0_cond_W2", "L0_cond_b2", "L0_cond_gamma", "L0_cond_beta", "L0_ffn_Wr", "L0_ffn_br",
        "L0_ffn_b2", "L1_cond_W1", "L1_cond_b1", "L1_cond_v", "L1_ffn_Wr", "L1_ffn_br", "L1_ffn_b2", "L2_cond_W", "L2_cond_b",
        "L2_ffn_w_red", "L2_ffn_wg", "L2_ffn_b2", "L3_cond_weight", "L3_ffn_e_score_bias")}
    ins["ids"] = np.concatenate([a["itok_B_0_8"], a["itok_B_0_2"], a["itok_B_0_30"], a["itok_B_0_15"]]).reshape(1, 8)
    ins["L1_mode"] = a["itok_B_0_2"]
    ins["L3_router_t"] = a["L3_ffn_router_weight"].T
    ins["L3_cond_b"] = a["L3_cond_bias"].reshape(-1, KD, P).transpose(2, 0, 1)
    for L, (E, F, _) in enumerate(LAYERS):
        w1, w2 = a[f"L{L}_ffn_W1"], a[f"L{L}_ffn_W2"]
        if L in SPARSE:
            ins[f"L{L}_w1"] = w1.reshape(E, KD, P, F).transpose(0, 2, 1, 3).reshape(E, P, KD * F)
            ins[f"L{L}_w2"] = w2.reshape(E, F // P, P, D).transpose(0, 2, 1, 3).reshape(E, P, F // P * D)
            ins[f"L{L}_b1_t"] = a[f"L{L}_ffn_b1"].reshape(E * F // P, P).T
            continue
        ins[f"L{L}_w1"] = w1.reshape(E, KD, P, F // SUB, SUB).transpose(0, 3, 2, 1, 4).reshape(-1, P, KD * SUB)
        ins[f"L{L}_w2"] = w2.reshape(E, F // SUB, FB, P, D).transpose(0, 1, 3, 2, 4).reshape(-1, P, FB * D)
        ins[f"L{L}_b1_t"] = a[f"L{L}_ffn_b1"].reshape(E * F // P, P).T
    I3 = 128
    gate_up, down = a["L3_ffn_gate_up_proj"], a["L3_ffn_down_proj"]
    sg, su, sd = (a[f"L3_ffn_shared_{n}_w"] for n in ("gate", "up", "down"))
    halves = [np.concatenate([sg[h * I3:(h + 1) * I3], su[h * I3:(h + 1) * I3]]) for h in range(2)]
    gu = np.concatenate([gate_up, np.stack(halves)])
    ins["L3_w1"] = gu.transpose(0, 2, 1).reshape(E3S, KD, P, 2 * I3).transpose(0, 2, 1, 3).reshape(E3S, P, KD * 2 * I3)
    dn = np.concatenate([down, np.stack([sd[:, h * I3:(h + 1) * I3] for h in range(2)])])
    ins["L3_w2"] = dn.transpose(0, 2, 1)

    nc = bacc.Bacc("TRN2", target_bir_lowering=False, num_devices=1)
    arrays, tensors = {}, {}
    for name, v in ins.items():
        arrays[f"in_{name}"] = np.ascontiguousarray(v)
        tensors[name] = nc.dram_tensor(f"in_{name}", v.shape, mybir.dt.from_np(v.dtype), kind="ExternalInput").ap()
    tensors["out"] = nc.dram_tensor("out_x", (B, SEQ, D), F32, kind="ExternalOutput").ap()
    build(nc, tensors)
    r = run_bass_kernel_spmd(nc, [arrays], core_ids=[0])
    return r.results[0]["out_x"]
```

```python
import concourse.bass as bass
from concourse import mybir
from contextlib import ExitStack

F32 = mybir.dt.float32
F32R = mybir.dt.float32r
I32 = mybir.dt.int32
ALU = mybir.AluOpType
ACT = mybir.ActivationFunctionType
AX = mybir.AxisListType

P = 128
B, SEQ, D = 2, 1024, 256
NT = B * SEQ // P
TPB = SEQ // P
CH = 512
NC = B * SEQ // CH
TPC = CH // P
KD = D // P
A0 = 64
GR = 16
SUB = 512
FB = SUB // P
LN_EPS = 1e-5
TOP_P = 0.8
TOP_K = 6
NEG = -1e30
LAYERS = [(8, 1024, ACT.Relu), (8, 1024, ACT.Gelu), (8, 512, ACT.Gelu)]
E3 = 32
E3S = 34
SPARSE = (1, 2)
BT = 256
BTT = BT // P
BLOCKS = B * SEQ // BT + 8
STEPS = BLOCKS // 2
PW = D + 2


def build(nc, t):
    with ExitStack() as ctx:
        def sb(name, shape, dt=F32):
            return ctx.enter_context(nc.sbuf_tensor(name, shape, dt))

        def sem(name):
            return ctx.enter_context(nc.semaphore(name))

        X = sb("x_tok", [P, NT, D])
        Z = sb("z_tok", [P, NT, D])
        TAh = sb("featA_hi", [P, KD, NT * P], F32R)
        TAl = sb("featA_lo", [P, KD, NT * P], F32R)
        TBh = sb("featB_hi", [P, NT * PW], F32R)
        TBl = sb("featB_lo", [P, NT * PW], F32R)
        TBhv = TBh[:, 0:KD * NT * P].rearrange("p (k n) -> p k n", k=KD)
        TBlv = TBl[:, 0:KD * NT * P].rearrange("p (k n) -> p k n", k=KD)
        XRh = TBh[:].rearrange("p (t w) -> p t w", t=NT)
        XRl = TBl[:].rearrange("p (t w) -> p t w", t=NT)
        W1r = sb("w1_raw", [P, KD * SUB])
        W2r = sb("w2_raw", [P, FB * D])
        W1h = sb("w1_hi", [P, 2, KD * SUB], F32R)
        W1l = sb("w1_lo", [P, 2, KD * SUB], F32R)
        W2h = sb("w2_hi", [P, 2, FB * D], F32R)
        W2l = sb("w2_lo", [P, 2, FB * D], F32R)
        HF = sb("hidden_f32", [P, FB, CH])
        HTh = sb("hidden_hi", [P, 2, FB, CH], F32R)
        HTl = sb("hidden_lo", [P, 2, FB, CH], F32R)
        SC = sb("scratch", [P, 8, CH])
        G = sb("gates", [P, NT, E3S + 1])
        IO = sb("iota_f32", [P, 64])
        IOi = sb("iota_int", [P, 64], I32)
        RS16 = sb("reset16", [P, 8 * NT])
        SLOTf = sb("slot_f32", [P, NT])
        SLOT = sb("slot", [P, NT], I32)
        BLK = [sb(f"blocks{L}", [1, 64], I32) for L in SPARSE]
        XS = nc.dram_tensor("x_sorted", [(BLOCKS + 2) * BT, D], F32).ap()
        YS = nc.dram_tensor("y_sorted", [BLOCKS * BT, D], F32).ap()
        Zf = Z[:].rearrange("p t d -> p (t d)")
        SCf = SC[:].rearrange("p a c -> p (a c)")
        ZW = [[x[:, 0:NT * D // 2], x[:, NT * D // 2:]] for x in (Zf, SCf)]
        WB1h, WB1l = (x[:, 0:NT * D].rearrange("p (b n) -> p b n", b=2) for x in (TBh, TBl))
        WB2h, WB2l = (x[:].rearrange("p k n -> p (k n)").rearrange("p (b n) -> p b n", b=2) for x in (TAh, TAl))
        XB = W1r[:].rearrange("p (b t d) -> p b t d", b=2, t=BTT)
        YB = W2r[:].rearrange("p (b t d) -> p b t d", b=2, t=BTT)
        L3W = sb("list3_weights", [1, 64], I32)
        L3G = sb("list3_gates", [1, 64], I32)
        ident = sb("ident", [P, P])
        IDS = sb("ids", [1, 8], I32)
        MODEi = sb("mode_int", [P, B], I32)
        B1 = [sb(f"b1_{L}", [P, LAYERS[L][0] * LAYERS[L][1] // P]) for L in range(3)]
        BB = sb("b1_block", [P, 2, 8])
        BS = sb("b1_step", [P, 3 * FB])
        B2 = [sb(f"b2_{L}", [LAYERS[L][0], D]) for L in range(3)]
        BR = [sb("br_0", [P, 8]), sb("br_1", [P, 8]), None, sb("br_3", [P, E3])]
        CB0 = sb("cond0_b1", [A0, B])
        CB1 = sb("cond1_b1", [A0, 1])
        CB3 = sb("cond3_b", [P, B, KD])
        V1 = sb("cond1_v", [A0, 1])
        RW = [GR if L == 2 else 8 if L < 2 else E3 for L in range(4)]
        Rr = [sb(f"router_raw{L}", [P, KD, RW[L]]) for L in range(4)]
        Rh = [sb(f"router_hi{L}", [P, KD, RW[L]], F32R) for L in range(4)]
        Rl = [sb(f"router_lo{L}", [P, KD, RW[L]], F32R) for L in range(4)]
        WG = sb("wg", [8, 3 * GR])
        WGT = sb("wg_t", [GR, 8])
        ST = sb("stats", [P, 2, 6])
        MV = sb("mean_var", [P, NT, 2])
        SM = sb("small", [P, 8, NT])
        JC = sb("j_col", [P, TPB])
        JCi = sb("j_col_int", [P, TPB], I32)
        MD = sb("mode", [P, B, 12])
        TM = sb("tri", [P, 3, P])
        ONE = sb("ones", [P, P])
        PS = ctx.enter_context(nc.psum_tensor("ps", [P, 8, CH], F32))

        RS = SC[:, 7, :]
        MX3 = W1r[:].rearrange("p (a c) -> p a c", c=D)
        DM = W2r[:, 0:B * P].rearrange("p (b j) -> p b j", b=B)
        XTh, XTl = (x[:, 0, :].rearrange("p (b k n) -> p b k n", b=2, k=KD) for x in (W1h, W1l))

        s_x = [sem(f"x_in{c}") for c in range(NC)]
        s_ids = sem("ids_in")
        s_small = sem("small_in")
        N_SMALL = 18
        s_cb0 = sem("cond0_b1_in")
        s_mode = sem("mode_in")
        s_rows = sem("rows_in")
        s_craw = [sem(f"cond_raw{L}") for L in range(4)]
        s_csplit = [sem(f"cond_split{L}") for L in range(4)]
        s_const0 = sem("const_fill")
        s_const = sem("const")
        s_rsplit = sem("router_split")
        s_dve = sem("dve_step")
        s_act = sem("act_step")
        s_pool = sem("pool_step")
        TR = ["x0", "z0", "x1", "z1", "x2", "z2", "x3"]
        TR0 = {n: KD * NC * i for i, n in enumerate(TR)}
        s_tps = sem("tr_ps")
        s_thi = sem("tr_hi")
        s_tlo = sem("tr_lo")
        s_ch = {L: sem(f"cond_h{L}") for L in (0, 1, 3)}
        s_chf = {1: sem("cond_hf1")}
        s_chi = {L: sem(f"cond_hi{L}") for L in (0, 1, 3)}
        s_clo = {L: sem(f"cond_lo{L}") for L in (0, 1, 3)}
        s_cy = sem("cond0_y")
        s_cyf = sem("cond0_y_used")
        s_xb2 = sem("x_plus_b2")
        s_stat = sem("ln_stats")
        s_aggr = sem("ln_mean_var")
        s_var = sem("ln_var")
        s_std = sem("ln_std")
        s_norm = sem("ln_norm")
        s_z0 = sem("z0_tile")
        s_sc = sem("score_ps")
        s_sc_sb = sem("score_row")
        s_xr = sem("pool_rhs")
        s_arg = sem("pool_arg")
        s_pf = sem("pool_p")
        s_phi = sem("pool_hi")
        s_plo = sem("pool_lo")
        s_pmm = sem("pool_mm")
        s_den = sem("pool_den")
        s_z1 = sem("z1_tile")
        s_lg = sem("logits")
        s_sub = sem("logits_shifted")
        s_exp = sem("logits_exp")
        s_gate = sem("gates")
        s_gt = sem("gates_t_ps")
        s_gts = sem("gates_t")
        s_by = sem("bias_y")
        s_bu = sem("bias_used")
        s_c2y = sem("cond2_y")
        s_z2 = sem("z2_tile")
        s_red = sem("reduced_ps")
        s_reds = sem("reduced")
        s_wgn = sem("wg_norm")
        s_wgt = sem("wg_t_ps")
        s_wgs = sem("wg_t_sb")
        s_ss = sem("wg_sumsq")
        s_sq = sem("wg_root")
        s_wraw = {L: sem(f"w_raw{L}") for L in (0, 3)}
        s_wsplit = {L: sem(f"w_split{L}") for L in (0, 3)}
        s_whi = {L: sem(f"w_hi{L}") for L in (0, 3)}
        s_hps = [sem(f"h_ps{L}") for L in range(4)]
        s_b1 = {L: sem(f"b1_step{L}") for L in (0,)}
        s_hf3 = sem("silu3")
        s_hm3 = sem("hmid3")
        s_hhi = [sem(f"h_hi{L}") for L in range(4)]
        s_hlo = [sem(f"h_lo{L}") for L in range(4)]
        s_y = [sem(f"y_ps{L}") for L in range(4)]
        s_yfree = {L: sem(f"y_free{L}") for L in (0, 3)}
        s_cnt3 = sem("counts3_in")
        s_used3 = sem("counts3_read")
        s_cnt3p = sem("counts3_ps")
        s_list3 = sem("list3")
        s_zero = sem("zeros_filled")
        s_zst = sem("x_sorted_cleared")
        s_oh = sem("onehot")
        s_rank = sem("ranks")
        s_slot = sem("slots")
        s_list = sem("block_list")
        s_scat = sem("scattered")
        s_gath = [sem(f"gathered{c}") for c in range(NC)]
        s_add = sem("added")
        s_w1raw = [[sem(f"w1_raw{L}_{k}") for k in range(2)] for L in SPARSE]
        s_w1hi = [sem(f"w1_hi{L}") for L in SPARSE]
        s_w1sp = [sem(f"w1_split{L}") for L in SPARSE]
        s_w2raw = [[sem(f"w2_raw{L}_{k}") for k in range(2)] for L in SPARSE]
        s_w2hi = [sem(f"w2_hi{L}") for L in SPARSE]
        s_w2sp = [sem(f"w2_split{L}") for L in SPARSE]
        s_bb = [sem(f"b1_block{L}") for L in SPARSE]
        s_xb = [[sem(f"x_block{L}_{k}") for k in range(2)] for L in SPARSE]
        s_xps = [sem(f"xt_ps{L}") for L in SPARSE]
        s_xhi = [sem(f"xt_hi{L}") for L in SPARSE]
        s_xlo = [sem(f"xt_lo{L}") for L in SPARSE]
        s_yev = [sem(f"y_out{L}") for L in SPARSE]
        s_yst = [[sem(f"y_stored{L}_{k}") for k in range(2)] for L in SPARSE]
        s_yb = [sem(f"y_buffer{L}") for L in SPARSE]
        s_blocks = sem("blocks_done")
        s_row = sem("cond2_row")
        s_out = sem("out_stored")

        NSUB = [LAYERS[L][0] * LAYERS[L][1] // SUB for L in range(3)]
        NSUB.append(E3S)
        GTB = [4, 0, 0]
        FEAT = [(TBhv, TBlv), (TAh, TAl), (TAh, TAl), (TAh, TAl)]
        YC = 2 * TPC
        STEPS3 = E3S // 2
        UPI = 2 * NC

        block = ctx.enter_context(nc.Block())

        @block.sync
        def _(sp):
            sp.dma_start(IDS[0:1, 0:8], t["ids"]).then_inc(s_ids, 16)
            for c in range(NC):
                sp.dma_start(X[:, c * TPC:(c + 1) * TPC, :],
                             t["x"].rearrange("b (t p) d -> p (b t) d", p=P)[:, c * TPC:(c + 1) * TPC, :]
                             ).then_inc(s_x[c], 16)
            sp.wait_ge(s_ids, 16)
            lang = [sp.value_load(IDS[0:1, b:b + 1], min_val=0, max_val=9) for b in range(B)]
            for b in range(B):
                sp.dma_start(W1r[:, b * KD * A0:(b + 1) * KD * A0].rearrange("p (k a) -> p k a", k=KD),
                             t["L0_cond_W1"][bass.ds(lang[b], 1), :, :].rearrange("o (k p) a -> p (o k) a", p=P)
                             ).then_inc(s_craw[0], 16)
                sp.dma_start(W1r[0:A0, 256 + b * D:256 + (b + 1) * D],
                             t["L0_cond_W2"][bass.ds(lang[b], 1), :, :].rearrange("o a d -> a (o d)")
                             ).then_inc(s_craw[0], 16)
            for b in range(B):
                sp.dma_start(CB0[:, b:b + 1], t["L0_cond_b1"][bass.ds(lang[b], 1), :].rearrange("o a -> a o")
                             ).then_inc(s_cb0, 16)
            for b in range(B):
                for n, name in enumerate(("L0_cond_b2", "L0_cond_gamma", "L0_cond_beta")):
                    sp.dma_start(HF[:, n, b * D:(b + 1) * D],
                                 t[name][bass.ds(lang[b], 1), :].broadcast_to([P, D])).then_inc(s_rows, 16)
            for L, name in enumerate(("L0_ffn_Wr", "L1_ffn_Wr", "L2_ffn_w_red", "L3_router_t")):
                sp.dma_start(Rr[L][:], t[name].rearrange("(k p) e -> p k e", p=P)).then_inc(s_small, 16)
            sp.dma_start(BR[0][:], t["L0_ffn_br"].unsqueeze(0).broadcast_to([P, 8])).then_inc(s_small, 16)
            sp.dma_start(BR[1][:], t["L1_ffn_br"].unsqueeze(0).broadcast_to([P, 8])).then_inc(s_small, 16)
            sp.dma_start(BR[3][:], t["L3_ffn_e_score_bias"].unsqueeze(0).broadcast_to([P, E3])).then_inc(s_small, 16)
            for L in range(3):
                sp.dma_start(B1[L][:], t[f"L{L}_b1_t"]).then_inc(s_small, 16)
                sp.dma_start(B2[L][:], t[f"L{L}_ffn_b2"]).then_inc(s_small, 16)
            sp.dma_start(CB1[:], t["L1_cond_b1"].unsqueeze(1)).then_inc(s_small, 16)
            sp.dma_start(V1[:], t["L1_cond_v"].unsqueeze(1)).then_inc(s_small, 16)
            sp.dma_start(WG[:, 0:GR], t["L2_ffn_wg"]).then_inc(s_small, 16)
            cat = [sp.value_load(IDS[0:1, 4 + b:5 + b], min_val=0, max_val=31) for b in range(B)]
            emb = [sp.value_load(IDS[0:1, 6 + b:7 + b], min_val=0, max_val=15) for b in range(B)]
            for b in range(B):
                sp.dma_start(CB3[:, b, :], t["L3_cond_b"][:, bass.ds(emb[b], 1), :].rearrange("p o k -> p (o k)")
                             ).then_inc(s_small, 16)

            def sub_weights(L, s):
                if L < 3:
                    sp.dma_start(W1r[:], t[f"L{L}_w1"][bass.ds(s, 1)].rearrange("o p f -> p (o f)")).then_inc(s_wraw[L], 16)
                    sp.dma_start(W2r[:], t[f"L{L}_w2"][bass.ds(s, 1)].rearrange("o p f -> p (o f)")).then_inc(s_wraw[L], 16)
                else:
                    sp.dma_start(W1r[:, 0:KD * D], t["L3_w1"][bass.ds(s, 1)].rearrange("o p f -> p (o f)")
                                 ).then_inc(s_wraw[L], 16)
                    sp.dma_start(W2r[:, 0:D], t["L3_w2"][bass.ds(s, 1)].rearrange("o p f -> p (o f)")
                                 ).then_inc(s_wraw[L], 16)

            def block_weights(L):
                F = LAYERS[SPARSE[L]][1]
                w1, w2 = t[f"L{SPARSE[L]}_w1"], t[f"L{SPARSE[L]}_w2"]

                src = XS.rearrange("(i k t p) d -> i k p t d", k=2, t=BTT, p=P)

                def load(i, k):
                    q = i * 2 + k
                    first = isinstance(i, int)
                    e = sp.value_load(BLK[L][0:1, q:q + 1] if first else BLK[L][0:1, bass.ds(q, 1)],
                                      min_val=0, max_val=7)
                    if not first:
                        sp.wait_ge(s_xps[L], q - 1)
                    sp.dma_start(XB[:, k], src[bass.ds(i, 1), k].rearrange("o p t d -> p (o t) d")
                                 ).then_inc(s_xb[L][k], 16)
                    if not first:
                        sp.wait_ge(s_w1sp[L], q - 1)
                    sp.dma_start(ZW[k][0][:, 0:KD * F], w1[bass.ds(e, 1)].rearrange("o p f -> p (o f)")
                                 ).then_inc(s_w1raw[L][k], 16)
                    if not first:
                        sp.wait_ge(s_w2sp[L], q - 1)
                    sp.dma_start(ZW[k][1][:, 0:KD * F], w2[bass.ds(e, 1)].rearrange("o p f -> p (o f)")
                                 ).then_inc(s_w2raw[L][k], 16)

                sp.wait_ge(s_list, L + 1)
                steps = sp.value_load(BLK[L][0:1, 63:64], min_val=1, max_val=STEPS)
                sp.wait_ge(s_scat, 16 * NT * (L + 1))
                load(0, 0)
                sp.wait_ge(s_bu, NT * (L + 2))
                load(0, 1)
                with sp.Fori(0, STEPS) as i:
                    with sp.If(i + 1 < steps):
                        for k in range(2):
                            load(i + 1, k)
                sp.wait_ge(s_blocks, L + 1)

            for L in range(4):
                sp.wait_ge(s_csplit[L], 1)
                if L == 3:
                    sub_weights(3, E3)
                    sp.wait_ge(s_wsplit[3], 1)
                    sub_weights(3, E3 + 1)
                    sp.wait_ge(s_list3, 1)
                    steps = sp.value_load(L3G[0:1, 63:64], min_val=1, max_val=STEPS3)
                    with sp.Fori(2, E3S) as s:
                        with sp.If(s < steps * 2):
                            e = sp.value_load(L3W[0:1, bass.ds(s, 1)], min_val=0, max_val=E3S - 1)
                            sp.wait_ge(s_wsplit[3], s)
                            sub_weights(3, e)
                    break
                if L in SPARSE:
                    block_weights(L - 1)
                else:
                    sub_weights(L, 0)
                    with sp.Fori(1, NSUB[L]) as s:
                        sp.wait_ge(s_wsplit[L], s)
                        sub_weights(L, s)
                    sp.wait_ge(s_wsplit[L], NSUB[L])
                if L == 0:
                    sp.dma_start(W1r[:, 0:KD * A0].rearrange("p (k a) -> p k a", k=KD),
                                 t["L1_cond_W1"].rearrange("(k p) a -> p k a", p=P)).then_inc(s_craw[1], 16)
                if L in (1, 2):
                    row = cat if L == 1 else emb
                    for b in range(B):
                        sp.dma_start(W1r[:, b * KD * D:(b + 1) * KD * D].rearrange("p (k d) -> p k d", k=KD),
                                     t["L2_cond_W" if L == 1 else "L3_cond_weight"][bass.ds(row[b], 1), :, :]
                                     .rearrange("o (k p) d -> p (o k) d", p=P)).then_inc(s_craw[L + 1], 16)
                        if L == 1:
                            sp.dma_start(W2r[:, b * D:(b + 1) * D], t["L2_cond_b"][bass.ds(cat[b], 1), :]
                                         .broadcast_to([P, D])).then_inc(s_row, 16)
            for c in range(NC):
                sp.wait_ge(s_yfree[3], steps * (TPC * UPI) + max(0, YC - TPC * (NC - c - 1)))
                sp.dma_start(t["out"].rearrange("b (t p) d -> p (b t) d", p=P)[:, c * TPC:(c + 1) * TPC, :],
                             X[:, c * TPC:(c + 1) * TPC, :]).then_inc(s_out, 16)
            sp.wait_ge(s_out, 16 * NC)

        @block.gpsimd
        def _(gp):
            gp.dma_start(MODEi[:], t["L1_mode"].unsqueeze(0).broadcast_to([P, B])).then_inc(s_mode, 16)
            gp.memset(ident[:], 0.0).then_inc(s_const0, 1)
            gp.memset(TM[:], 1.0).then_inc(s_const0, 1)
            gp.memset(ONE[:], 1.0).then_inc(s_const, 1)
            gp.iota(JCi[:], [[P, TPB]], base=0, channel_multiplier=1).then_inc(s_const, 1)
            gp.iota(IOi[:], [[1, 64]], base=0, channel_multiplier=0).then_inc(s_const, 1)
            gp.wait_ge(s_const0, 2)
            gp.affine_select(out=ident[:], in_=ident[:], compare_op=ALU.not_equal, fill=1.0, base=0,
                             pattern=[[-1, P]], channel_multiplier=1).then_inc(s_const, 1)
            gp.affine_select(out=TM[:, 0, :], in_=TM[:, 0, :], compare_op=ALU.is_ge, fill=0.0, base=0,
                             pattern=[[1, P]], channel_multiplier=-1).then_inc(s_const, 1)
            gp.affine_select(out=TM[:, 1, :], in_=TM[:, 1, :], compare_op=ALU.is_ge, fill=0.0, base=0,
                             pattern=[[-1, P]], channel_multiplier=1).then_inc(s_const, 1)
            gp.affine_select(out=TM[:, 2, :], in_=TM[:, 2, :], compare_op=ALU.not_equal, fill=0.0, base=0,
                             pattern=[[-1, P]], channel_multiplier=1).then_inc(s_const, 1)
            gp.wait_ge(s_rows, 16 * 3 * B)
            for n in range(NT):
                if n % TPC == 0:
                    gp.wait_ge(s_x[n // TPC], 16)
                gp.tensor_tensor(Z[:, n, :], X[:, n, :], HF[:, 0, n // TPB * D:(n // TPB + 1) * D], ALU.add).then_inc(s_xb2, 1)
            zeros = SC[:].rearrange("p a c -> p (a c)")
            gp.memset(zeros, 0.0).then_inc(s_zero, 1)
            gp.wait_ge(s_small, 16 * N_SMALL)
            gp.wait_ge(s_zero, 1)
            for dst in (XS[0:BLOCKS * BT], YS):
                for k in range(BLOCKS * BT // (P * NT)):
                    gp.dma_start(dst.rearrange("(k p r) d -> k p (r d)", p=P, r=NT)[k], zeros).then_inc(s_zst, 16)
            for n in range(NT):
                b = n // TPB
                gp.wait_ge(s_norm, n + 1)
                gp.tensor_tensor(Z[:, n, :], Z[:, n, :], HF[:, 1, b * D:(b + 1) * D], ALU.mult).then_inc(s_pool, 1)
                gp.wait_ge(s_pool, n + 1)
                gp.tensor_tensor(Z[:, n, :], Z[:, n, :], HF[:, 2, b * D:(b + 1) * D], ALU.add).then_inc(s_z0, 1)

            for L in range(2):
                gp.wait_ge(s_slot, L + 1)
                if L == 0:
                    gp.wait_ge(s_zst, 16 * 2 * BLOCKS * BT // (P * NT))
                for n in range(NT):
                    gp.indirect_dma_start(XS, bass.IndirectOffsetOnAxis(ap=SLOT[:, n:n + 1], axis=0),
                                          Z[:, n, :], None).then_inc(s_scat, 16)
                gp.wait_ge(s_scat, 16 * NT * (L + 1))

                gp.wait_ge(s_list, L + 1)
                steps = gp.value_load(BLK[L][0:1, 63:64], min_val=1, max_val=STEPS)
                gp.sem_inc(s_yb[L], 2)
                with gp.Fori(0, STEPS) as i:
                    with gp.If(i < steps):
                        for k in range(2):
                            gp.wait_ge(s_yev[L], BTT * (i * 2 + k + 2))
                            dst = YS.rearrange("(i k t p) d -> i k p t d", k=2, t=BTT, p=P)
                            gp.dma_start(dst[bass.ds(i, 1), k].rearrange("o p t d -> p (o t) d"), YB[:, k]
                                         ).then_inc(s_yst[L][k], 16)
                            gp.wait_ge(s_yst[L][k], i * 16 + 16)
                            gp.sem_inc(s_yb[L], 1)
                gp.sem_inc(s_blocks, 1)
                for n in range(NT):
                    gp.indirect_dma_start(Z[:, n, :], None, YS,
                                          bass.IndirectOffsetOnAxis(ap=SLOT[:, n:n + 1], axis=0)
                                          ).then_inc(s_gath[n // TPC], 16)

        @block.tensor
        def _(pe):
            def mm3(out, lh, ll, rh, rl, first, last):
                nc.tensor.matmul(out, lh, rh, start=first, stop=False)
                nc.tensor.matmul(out, lh, rl, start=False, stop=False)
                return nc.tensor.matmul(out, ll, rh, start=False, stop=last)

            def transposes(n, src, ready):
                for c in range(NC):
                    ready(c)
                    for k in range(KD):
                        g = KD * c + k
                        if g >= 4:
                            pe.wait_ge(s_tlo, TR0[n] + g - 3)
                        for j in range(TPC):
                            last = nc.tensor.transpose(PS[:, g % 4, j * P:(j + 1) * P],
                                                       src[:, c * TPC + j, k * P:(k + 1) * P], ident[:])
                        last.then_inc(s_tps, 1)

            def routing(L, wait_feat):
                fh, fl = FEAT[L]
                E = RW[L]
                for n in range(NT):
                    if n % TPC == 0:
                        wait_feat(n // TPC)
                    for k in range(KD):
                        last = mm3(PS[:, 4, n * E:(n + 1) * E], fh[:, k, n * P:(n + 1) * P],
                                   fl[:, k, n * P:(n + 1) * P], Rh[L][:, k, :], Rl[L][:, k, :], k == 0, k == KD - 1)
                last.then_inc(s_lg, 1)

            def bias(L):
                E = LAYERS[L][0]
                pe.wait_ge(s_gate, L + 1)
                for n in range(NT):
                    last = nc.tensor.transpose(PS[0:E, GTB[L] + n // TPC, (n % TPC) * P:(n % TPC + 1) * P],
                                               G[:, n, 0:E], ident[:])
                last.then_inc(s_gt, 1)
                pe.wait_ge(s_gts, L + 1)
                if L in SPARSE:
                    pe.wait_ge(s_list, L)
                for n in range(NT):
                    if n >= 4:
                        pe.wait_ge(s_bu, NT * L + n - 3)
                    nc.tensor.matmul(PS[:, 4 + n % 4, 0:D], SC[0:E, 4 + n // TPC, (n % TPC) * P:(n % TPC + 1) * P],
                                     B2[L][:], start=True, stop=True).then_inc(s_by, 1)
                pe.wait_ge(s_bu, NT * L + NT)

            def ffn(L, gates):
                fh, fl = FEAT[L]

                def hidden(q, u):
                    s, c = (u // NC) % 2, u % NC
                    for f in range(FB):
                        if f == 0 and c == 0:
                            pe.wait_ge(s_wsplit[L], (q + NC) // NC if isinstance(q, int) else q[0] * 2 + u // NC + 1)
                        if not (isinstance(q, int) and q == 0):
                            pe.wait_ge(s_hhi[L], FB * (q[0] * UPI + u - 1) + f + 1)
                        for k in range(KD):
                            w = slice(k * SUB + f * P, k * SUB + (f + 1) * P)
                            last = mm3(PS[:, f, :], W1h[:, s, w], W1l[:, s, w],
                                       fh[:, k, c * CH:(c + 1) * CH], fl[:, k, c * CH:(c + 1) * CH],
                                       k == 0, k == KD - 1)
                        last.then_inc(s_hps[L], 1)

                def output(i, u):
                    s, c = u // NC, u % NC
                    pe.wait_ge(s_hlo[L], FB * (i * UPI + u + 1))
                    for j in range(TPC):
                        pe.wait_ge(s_yfree[L], TPC * (i * UPI + u) + j + 1)
                        for f in range(FB):
                            tok = slice(j * P, (j + 1) * P)
                            w = slice(f * D, (f + 1) * D)
                            last = mm3(PS[:, 4 + j, 0:D], HTh[:, u % 2, f, tok], HTl[:, u % 2, f, tok],
                                       W2h[:, s, w], W2l[:, s, w], f == 0, f == FB - 1)
                        last.then_inc(s_y[L], 1)

                def step(i, final, begun=False):
                    for u in range(UPI):
                        if not (final and u == UPI - 1) and not (begun and u == 0):
                            hidden((i,), u + 1)
                        output(i, u)

                hidden(0, 0)
                hidden((0,), 1)
                gates()
                steps = NSUB[L] // 2
                step(0, False, True)
                with pe.Fori(1, steps - 1) as i:
                    step(i, False)
                step(steps - 1, True)

            def ranks(L):
                pe.wait_ge(s_oh, L + 1)
                nc.tensor.matmul(PS[:, 5, 0:8 * NT], TM[:, 0, :], SC[:, 3, 0:8 * NT], start=True, stop=True)
                nc.tensor.matmul(PS[:, 5, 8 * NT:16 * NT], ONE[:], SC[:, 3, 0:8 * NT],
                                 start=True, stop=True).then_inc(s_rank, 1)

            def blocks(L):
                NF = LAYERS[SPARSE[L]][1] // P

                def trans(i, k):
                    first = isinstance(i, int) and i == 0
                    pe.wait_ge(s_xb[L][k], i * 16 + 16)
                    if not first:
                        pe.wait_ge(s_xlo[L], i * 2 + k - 1)
                    for m in range(KD):
                        for tt in range(BTT):
                            last = nc.tensor.transpose(PS[:, 6 + k, m * BT + tt * P:m * BT + (tt + 1) * P],
                                                       XB[:, k, tt, m * P:(m + 1) * P], ident[:])
                    last.then_inc(s_xps[L], 1)

                def hidden(i, k, first=False):
                    q = i * 2 + k
                    pe.wait_ge(s_xlo[L], q + 1)
                    pe.wait_ge(s_w1sp[L], q + 1)
                    for f in range(NF):
                        if not first or f >= 4:
                            pe.wait_ge(s_hhi[SPARSE[L]], NF * q + f - 3)
                        out = PS[:, f % 4, (f // 4) * BT:(f // 4 + 1) * BT]
                        for m in range(KD):
                            w = slice((m * NF + f) * P, (m * NF + f + 1) * P)
                            last = mm3(out, WB1h[:, k, w], WB1l[:, k, w], XTh[:, k, m, :], XTl[:, k, m, :],
                                       m == 0, m == KD - 1)
                        last.then_inc(s_hps[SPARSE[L]], 1)

                def output(i, k):
                    q = i * 2 + k
                    pe.wait_ge(s_w2sp[L], q + 1)
                    pe.wait_ge(s_hlo[SPARSE[L]], NF // 2 * (q + 1))
                    for j in range(BTT):
                        pe.wait_ge(s_yev[L], BTT * q + j + 1)
                        for f in range(NF):
                            tok = slice((f % 2) * BT + j * P, (f % 2) * BT + (j + 1) * P)
                            w = slice(f * D, (f + 1) * D)
                            last = mm3(PS[:, 4 + j, 0:D], HTh[:, k, f // 2, tok], HTl[:, k, f // 2, tok],
                                       WB2h[:, k, w], WB2l[:, k, w], f == 0, f == NF - 1)
                        last.then_inc(s_y[SPARSE[L]], 1)

                steps = pe.value_load(BLK[L][0:1, 63:64], min_val=1, max_val=STEPS)
                trans(0, 0)
                hidden(0, 0, True)
                trans(0, 1)
                with pe.Fori(0, STEPS) as i:
                    with pe.If(i < steps):
                        hidden(i, 1)
                    with pe.If(i + 1 < steps):
                        trans(i + 1, 0)
                    with pe.If(i < steps):
                        output(i, 0)
                    with pe.If(i + 1 < steps):
                        hidden(i + 1, 0)
                        trans(i + 1, 1)
                    with pe.If(i < steps):
                        output(i, 1)

            def ffn3():
                fh, fl = FEAT[3]

                def hidden(i, u, first=False):
                    s, c = (u // NC) % 2, u % NC
                    if c == 0:
                        pe.wait_ge(s_wsplit[3], 1 if first else i * 2 + u // NC + 1)
                    for g in range(2):
                        if not first:
                            pe.wait_ge(s_hm3, i * UPI + u + 1)
                        for k in range(KD):
                            w = slice(k * D + g * P, k * D + (g + 1) * P)
                            last = mm3(PS[:, 2 * (u % 2) + g, :], W1h[:, s, w], W1l[:, s, w],
                                       fh[:, k, c * CH:(c + 1) * CH], fl[:, k, c * CH:(c + 1) * CH],
                                       k == 0, k == KD - 1)
                        last.then_inc(s_hps[3], 1)

                def output(i, u):
                    s = u // NC
                    pe.wait_ge(s_hlo[3], i * UPI + u + 1)
                    for j in range(TPC):
                        pe.wait_ge(s_yfree[3], YC + TPC * (i * UPI + u - 1) + j + 1)
                        if isinstance(i, int) and (u, j) == (0, 0):
                            pe.wait_ge(s_sub, 4)
                        if isinstance(i, int) and (u, j) == (NC, 1):
                            pe.wait_ge(s_used3, 1)
                        tok = slice(j * P, (j + 1) * P)
                        mm3(PS[:, 4 + j, 0:D], HTh[:, u % 2, 0, tok], HTl[:, u % 2, 0, tok],
                            W2h[:, s, 0:D], W2l[:, s, 0:D], True, True).then_inc(s_y[3], 1)

                hidden(0, 0, True)
                for u in range(UPI):
                    if u < UPI - 1:
                        hidden(0, u + 1)
                    output(0, u)
                    if u == NC - 1:
                        pe.wait_ge(s_cnt3, 1)
                        pe.wait_ge(s_yfree[3], YC + TPC * u + 2)
                        nc.tensor.matmul(PS[:, 5, 0:E3], ONE[:], SC[:, 6, 0:E3],
                                         start=True, stop=True).then_inc(s_cnt3p, 1)
                pe.wait_ge(s_list3, 1)
                steps = pe.value_load(L3G[0:1, 63:64], min_val=1, max_val=STEPS3)
                hidden(0, UPI)
                with pe.Fori(1, STEPS3) as i:
                    with pe.If(i < steps):
                        for u in range(UPI - 1):
                            hidden(i, u + 1)
                            output(i, u)
                        with pe.If(i + 1 < steps):
                            hidden(i, UPI)
                        output(i, UPI - 1)

            pe.wait_ge(s_const, 7)
            transposes("x0", X, lambda c: pe.wait_ge(s_x[c], 16))
            pe.wait_ge(s_csplit[0], 1)

            def adapter_hidden(c):
                b = c // (NC // B)
                pe.wait_ge(s_tlo, TR0["x0"] + KD * (c + 1))
                if c >= 2:
                    pe.wait_ge(s_chi[0], c - 1)
                for k in range(KD):
                    w = slice(b * KD * A0 + k * A0, b * KD * A0 + (k + 1) * A0)
                    last = mm3(PS[0:A0, 4 + c % 2, :], W1h[:, 1, w], W1l[:, 1, w], TAh[:, k, c * CH:(c + 1) * CH],
                               TAl[:, k, c * CH:(c + 1) * CH], k == 0, k == KD - 1)
                last.then_inc(s_ch[0], 1)

            adapter_hidden(0)
            for c in range(NC):
                b = c // (NC // B)
                if c + 1 < NC:
                    adapter_hidden(c + 1)
                pe.wait_ge(s_clo[0], c + 1)
                for j in range(TPC):
                    n = c * TPC + j
                    if n >= 2:
                        pe.wait_ge(s_cyf, n - 1)
                    w = slice(256 + b * D, 256 + (b + 1) * D)
                    mm3(PS[:, 6 + n % 2, 0:D], HTh[0:A0, c % 2, 0, j * P:(j + 1) * P],
                        HTl[0:A0, c % 2, 0, j * P:(j + 1) * P], W1h[0:A0, 1, w], W1l[0:A0, 1, w],
                        True, True).then_inc(s_cy, 1)
            transposes("z0", Z, lambda c: pe.wait_ge(s_z0, TPC * (c + 1)))
            pe.wait_ge(s_rsplit, 4)
            routing(0, lambda c: pe.wait_ge(s_tlo, TR0["z0"] + KD * (c + 1)))
            ffn(0, lambda: bias(0))

            def tiles_done(L):
                if L in SPARSE:
                    return lambda c: pe.wait_ge(s_add, NT * (L - 1) + TPC * (c + 1))
                return lambda c: pe.wait_ge(s_yfree[L], 4 + TPC * (NSUB[L] * NC - NC + c + 1))

            transposes("x1", X, tiles_done(0))
            pe.wait_ge(s_csplit[1], 1)
            for c in range(NC):
                pe.wait_ge(s_tlo, TR0["x1"] + KD * (c + 1))
                if c >= 2:
                    pe.wait_ge(s_chf[1], c - 1)
                for k in range(KD):
                    w = slice(k * A0, (k + 1) * A0)
                    last = mm3(PS[0:A0, 4 + c % 2, :], W1h[:, 1, w], W1l[:, 1, w], TAh[:, k, c * CH:(c + 1) * CH],
                               TAl[:, k, c * CH:(c + 1) * CH], k == 0, k == KD - 1)
                last.then_inc(s_ch[1], 1)
            pe.wait_ge(s_tlo, TR0["x1"] + KD * NC)
            pe.wait_ge(s_clo[1], 1)
            for c in range(NC):
                pe.wait_ge(s_chf[1], c + 1)
                for j in range(TPC):
                    nc.tensor.matmul(PS[:, 6, c * TPC + j:c * TPC + j + 1], HF[0:A0, c, j * P:(j + 1) * P], V1[:],
                                     start=True, stop=True)
                last = nc.tensor.matmul(PS[:, c, :], SC[0:A0, 7, 0:P], HF[0:A0, c, :], start=True, stop=True)
            last.then_inc(s_sc, 1)
            pe.wait_ge(s_sc_sb, 1)
            for b in range(B):
                pe.wait_ge(s_xr, 1 + TPB * (b + 1))
                if b:
                    pe.wait_ge(s_z1, TPB * b)
                for lb in range(TPB):
                    q = b * TPB + lb
                    pe.wait_ge(s_plo, q + 1)
                    for jt in range(TPB):
                        last = mm3(PS[:, jt, 0:PW], HTh[:, q % 2, jt // 4, (jt % 4) * P:(jt % 4 + 1) * P],
                                   HTl[:, q % 2, jt // 4, (jt % 4) * P:(jt % 4 + 1) * P],
                                   XRh[:, q, :], XRl[:, q, :], lb == 0, lb == TPB - 1)
                    last.then_inc(s_pmm, 1)
            pe.wait_ge(s_z1, NT)
            transposes("z1", Z, lambda c: None)
            routing(1, lambda c: pe.wait_ge(s_tlo, TR0["z1"] + KD * (c + 1)))
            ranks(0)
            bias(1)
            blocks(0)

            def linear_cond(L):
                n = f"x{L}"
                transposes(n, X, tiles_done(L - 1))
                pe.wait_ge(s_csplit[L], 1)
                for c in range(NC):
                    b = c // (NC // B)
                    pe.wait_ge(s_tlo, TR0[n] + KD * (c + 1))
                    for m in range(KD):
                        g = KD * c + m
                        if g >= 4:
                            pe.wait_ge(s_chi[L], g - 3)
                        for k in range(KD):
                            w = slice((b * KD + k) * D + m * P, (b * KD + k) * D + (m + 1) * P)
                            last = mm3(PS[:, 4 + g % 4, :], W1h[:, 1, w], W1l[:, 1, w],
                                       TBhv[:, k, c * CH:(c + 1) * CH], TBlv[:, k, c * CH:(c + 1) * CH],
                                       k == 0, k == KD - 1)
                        last.then_inc(s_ch[L], 1)
                pe.wait_ge(s_clo[L], KD * NC)

            transposes("x2", X, tiles_done(1))
            pe.wait_ge(s_csplit[2], 1)
            for n in range(NT):
                if n % TPC == 0:
                    pe.wait_ge(s_tlo, TR0["x2"] + KD * (n // TPC + 1))
                if n >= 4:
                    pe.wait_ge(s_z2, n - 3)
                for k in range(KD):
                    w = slice((n // TPB * KD + k) * D, (n // TPB * KD + k + 1) * D)
                    last = mm3(PS[:, 4 + n % 4, 0:D], TBhv[:, k, n * P:(n + 1) * P], TBlv[:, k, n * P:(n + 1) * P],
                               W1h[:, 1, w], W1l[:, 1, w], k == 0, k == KD - 1)
                last.then_inc(s_c2y, 1)
            transposes("z2", Z, lambda c: pe.wait_ge(s_z2, TPC * (c + 1)))
            pe.wait_ge(s_tlo, TR0["z2"] + KD * NC)
            for c in range(NC):
                for k in range(KD):
                    last = mm3(PS[0:GR, c, :], Rh[2][:, k, :], Rl[2][:, k, :], TAh[:, k, c * CH:(c + 1) * CH],
                               TAl[:, k, c * CH:(c + 1) * CH], k == 0, k == KD - 1)
            last.then_inc(s_red, 1)
            pe.wait_ge(s_wgn, 1)
            nc.tensor.transpose(PS[0:GR, 5, 0:8], WG[:, 2 * GR:3 * GR], ident[0:8, 0:8]).then_inc(s_wgt, 1)
            pe.wait_ge(s_wgs, 1)
            pe.wait_ge(s_reds, 1)
            for n in range(NT):
                last = nc.tensor.matmul(PS[:, 4, n * 8:(n + 1) * 8], HF[0:GR, n // TPC, (n % TPC) * P:(n % TPC + 1) * P],
                                        WGT[:], start=True, stop=True)
            last.then_inc(s_lg, 1)
            ranks(1)
            bias(2)
            blocks(1)

            linear_cond(3)
            routing(3, lambda c: None)
            ffn3()

        @block.scalar
        def _(act):
            def transposes(n, dst):
                for g in range(KD * NC):
                    c, k = g // KD, g % KD
                    act.wait_ge(s_tps, TR0[n] + g + 1)
                    act.activation(dst[:, k, c * CH:(c + 1) * CH], PS[:, g % 4, :], ACT.Copy).then_inc(s_thi, 1)

            def exps(L, n):
                act.wait_ge(s_sub, L + 1)
                act.activation(SC[:, 1, 0:n], SC[:, 0, 0:n], ACT.Exp).then_inc(s_exp, 1)

            def gates_t(L):
                E = LAYERS[L][0]
                act.wait_ge(s_gt, L + 1)
                act.activation(SC[0:E, 4:8, :], PS[0:E, GTB[L]:GTB[L] + 4, :], ACT.Copy).then_inc(s_gts, 1)

            def ffn(L, gates):
                func = LAYERS[L][2]
                BL = B1[L]

                def unit(i, u, first=False):
                    s, c = (u // NC), u % NC
                    for f in range(FB):
                        if first:
                            act.wait_ge(s_hps[L], f + 1)
                            b1 = BL[:, f:f + 1]
                        else:
                            act.wait_ge(s_hps[L], FB * (i * UPI + u) + f + 1)
                            act.wait_ge(s_hlo[L], FB * (i * UPI + u - 1) + f + 1)
                            act.wait_ge(s_yfree[L], TPC * (i * UPI + u))
                            b1 = BS[:, s * FB + f:s * FB + f + 1]
                        act.activation(HF[:, f, :], PS[:, f, :], func, bias=b1)
                        act.activation(HTh[:, u % 2, f, :], PS[:, f, :], func, bias=b1).then_inc(s_hhi[L], 1)

                def step(i, final):
                    n = (2 if final else 3) * FB
                    act.wait_ge(s_hhi[L], FB * (i * UPI + 1))
                    act.activation(BS[:, 0:n], BL[:, bass.ds(i * 2 * FB, n)], ACT.Copy).then_inc(s_b1[L], 1)
                    act.wait_ge(s_b1[L], i + 1)
                    for u in range(1, UPI + 1 - final):
                        unit(i, u)

                unit(0, 0, True)
                gates()
                steps = NSUB[L] // 2
                with act.Fori(0, steps - 1) as i:
                    step(i, 0)
                step(steps - 1, 1)

            def blocks(L):
                func = LAYERS[SPARSE[L]][2]
                NF = LAYERS[SPARSE[L]][1] // P
                N1 = KD * NF * P
                act.wait_ge(s_list, L + 1)
                steps = act.value_load(BLK[L][0:1, 63:64], min_val=1, max_val=STEPS)

                def weights(i, k):
                    q = i * 2 + k
                    slot = BLK[L][0:1, q:q + 1] if isinstance(q, int) else BLK[L][0:1, bass.ds(q, 1)]
                    e = act.value_load(slot, min_val=0, max_val=7)
                    if not isinstance(q, int):
                        act.wait_ge(s_hhi[SPARSE[L]], NF * (q - 1))
                        act.wait_ge(s_bb[L], q)
                    act.activation(BB[:, k, 0:NF], B1[SPARSE[L]][:, bass.ds(e * NF, NF)], ACT.Copy).then_inc(s_bb[L], 1)
                    if not isinstance(q, int):
                        act.wait_ge(s_hps[SPARSE[L]], NF * (q - 1))
                    act.wait_ge(s_w1raw[L][k], i * 16 + 16)
                    act.activation(WB1h[:, k, 0:N1], ZW[k][0][:, 0:N1], ACT.Copy).then_inc(s_w1hi[L], 1)

                def xt(i, k):
                    q = i * 2 + k
                    act.wait_ge(s_xps[L], q + 1)
                    if not isinstance(q, int):
                        act.wait_ge(s_hps[SPARSE[L]], NF * (q - 1))
                    act.activation(XTh[:, k].rearrange("p k n -> p (k n)"), PS[:, 6 + k, :], ACT.Copy).then_inc(s_xhi[L], 1)

                def hidden(i, k, first=False):
                    q = i * 2 + k
                    act.wait_ge(s_bb[L], q + 1)
                    for f in range(NF):
                        act.wait_ge(s_hps[SPARSE[L]], NF * q + f + 1)
                        if not first:
                            act.wait_ge(s_hlo[SPARSE[L]], NF // 2 * (q - 1) + f // 2 + 1)
                            act.wait_ge(s_yev[L], BTT * q)
                        b1 = BB[:, k, f:f + 1]
                        part = slice((f % 2) * BT, (f % 2 + 1) * BT)
                        ps = PS[:, f % 4, (f // 4) * BT:(f // 4 + 1) * BT]
                        act.activation(HF[:, f // 2, part], ps, func, bias=b1)
                        act.activation(HTh[:, k, f // 2, part], ps, func,
                                       bias=b1).then_inc(s_hhi[SPARSE[L]], 1)

                weights(0, 0)
                xt(0, 0)
                hidden(0, 0, True)
                weights(0, 1)
                xt(0, 1)
                with act.Fori(0, STEPS) as i:
                    with act.If(i + 1 < steps):
                        weights(i + 1, 0)
                    with act.If(i < steps):
                        hidden(i, 1)
                    with act.If(i + 1 < steps):
                        xt(i + 1, 0)
                        weights(i + 1, 1)
                        hidden(i + 1, 0)
                        xt(i + 1, 1)

            def ffn3():
                def unit(i, u):
                    act.wait_ge(s_hps[3], 2 * (i * UPI + u) + 1)
                    act.activation(HF[:, u % 2, :], PS[:, 2 * (u % 2), :], ACT.Silu).then_inc(s_hf3, 1)
                    act.wait_ge(s_hm3, 2 + i * UPI + u + 1)
                    act.wait_ge(s_yfree[3], YC + TPC * (i * UPI + u - 1))
                    act.activation(HTh[:, u % 2, 0, :], HF[:, 2 + u % 2, :], ACT.Copy).then_inc(s_hhi[3], 1)

                for u in range(UPI):
                    unit(0, u)
                act.wait_ge(s_list3, 1)
                steps = act.value_load(L3G[0:1, 63:64], min_val=1, max_val=STEPS3)
                with act.Fori(1, STEPS3) as i:
                    with act.If(i < steps):
                        for u in range(UPI):
                            unit(i, u)

            transposes("x0", TAh)
            act.wait_ge(s_cb0, 16 * B)
            for c in range(NC):
                b = c // (NC // B)
                act.wait_ge(s_ch[0], c + 1)
                if c >= 1:
                    act.wait_ge(s_clo[0], c)
                if c >= 2:
                    act.wait_ge(s_cy, TPC * (c - 1))
                act.activation(HF[0:A0, 3, :], PS[0:A0, 4 + c % 2, :], ACT.Relu, bias=CB0[:, b:b + 1])
                act.activation(HTh[0:A0, c % 2, 0, :], PS[0:A0, 4 + c % 2, :], ACT.Relu,
                               bias=CB0[:, b:b + 1]).then_inc(s_chi[0], 1)
                if c >= 2:
                    act.wait_ge(s_var, c - 1)
                    half = slice((c - 2) * TPB, (c - 1) * TPB)
                    act.activation(SM[:, 0, half], SM[:, 0, half], ACT.Sqrt).then_inc(s_std, 1)
            transposes("z0", TBhv)
            exps(0, NT * 8)
            ffn(0, lambda: gates_t(0))
            transposes("x1", TAh)

            def pool_rhs(b):
                for n in range(b * TPB, (b + 1) * TPB):
                    act.activation(XRh[:, n, 0:D], X[:, n, :], ACT.Copy).then_inc(s_act, 1)

            for c in range(NC):
                act.wait_ge(s_ch[1], c + 1)
                act.activation(HF[0:A0, c, :], PS[0:A0, 4 + c % 2, :], ACT.Tanh, bias=CB1[:, 0:1]).then_inc(s_chf[1], 1)
            pool_rhs(0)
            act.wait_ge(s_sc, 1)
            act.activation(SM[:, 0, :], PS[:, 6, 0:NT], ACT.Copy)
            act.activation(SC[:, 0:4, :], PS[:, 0:4, :], ACT.Copy).then_inc(s_sc_sb, 1)
            pool_rhs(1)
            for q in range(NT):
                act.wait_ge(s_arg, q + 1)
                if q >= 2:
                    act.wait_ge(s_pmm, q - 1)
                    act.wait_ge(s_plo, q - 1)
                act.activation(HF[:, 2 * (q % 2):2 * (q % 2) + 2, :], SC[:, 4 + 2 * (q % 2):6 + 2 * (q % 2), :],
                               ACT.Exp).then_inc(s_pf, 1)
                act.activation(HTh[:, q % 2, 0:2, :], SC[:, 4 + 2 * (q % 2):6 + 2 * (q % 2), :],
                               ACT.Exp).then_inc(s_phi, 1)
                if q % TPB == TPB - 1:
                    b = q // TPB
                    act.wait_ge(s_den, b + 1)
                    for jt in range(TPB):
                        n = b * TPB + jt
                        act.activation(Z[:, n, :], PS[:, jt, 0:D], ACT.Copy, scale=SM[:, 2, n:n + 1]).then_inc(s_z1, 1)
            transposes("z1", TAh)
            exps(1, NT * 8)
            gates_t(1)
            blocks(0)

            def linear_cond(L):
                transposes(f"x{L}", TBhv)
                CB = CB3
                for g in range(KD * NC):
                    c, m = g // KD, g % KD
                    act.wait_ge(s_ch[L], g + 1)
                    if g >= 4:
                        act.wait_ge(s_clo[L], g - 3)
                    act.activation(HF[:, g % 4, :], PS[:, 4 + g % 4, :], ACT.Identity, bias=CB[:, c // 2, m:m + 1])
                    act.activation(TAh[:, m, c * CH:(c + 1) * CH], PS[:, 4 + g % 4, :], ACT.Identity,
                                   bias=CB[:, c // 2, m:m + 1]).then_inc(s_chi[L], 1)

            transposes("x2", TBhv)
            transposes("z2", TAh)
            act.wait_ge(s_red, 1)
            act.activation(HF[0:GR, :, :], PS[0:GR, 0:4, :], ACT.Copy).then_inc(s_reds, 1)
            act.wait_ge(s_ss, 1)
            act.activation(SM[0:8, 4, 0:1], SM[0:8, 4, 0:1], ACT.Sqrt).then_inc(s_sq, 1)
            exps(2, NT * 8)
            gates_t(2)
            blocks(1)
            linear_cond(3)
            exps(3, NT * E3)
            ffn3()

        @block.vector
        def _(dve):
            steps_done = [0]

            def link(ins):
                steps_done[0] += 1
                ins.then_inc(s_dve, 1)
                dve.wait_ge(s_dve, steps_done[0])

            def lo(out, full, hi):
                return nc.vector.tensor_tensor(out, full, hi.bitcast(F32), ALU.subtract)

            def transposes(n, dh, dl, chunk=None):
                for g in range(KD * NC) if chunk is None else range(KD * chunk, KD * chunk + KD):
                    c, k = g // KD, g % KD
                    dve.wait_ge(s_thi, TR0[n] + g + 1)
                    lo(dl[:, k, c * CH:(c + 1) * CH], PS[:, g % 4, :], dh[:, k, c * CH:(c + 1) * CH]).then_inc(s_tlo, 1)

            def cond_split(L, loads, parts):
                dve.wait_ge(s_craw[L], 16 * loads)
                for rows, cols in parts:
                    link(nc.vector.tensor_copy(W1h[0:rows, 1, cols], W1r[0:rows, cols]))
                    last = lo(W1l[0:rows, 1, cols], W1r[0:rows, cols], W1h[0:rows, 1, cols])
                    link(last)
                dve.sem_inc(s_csplit[L], 1)

            def split_into(L, buf, s, after):
                n1, n2 = (KD * SUB, FB * D) if L < 3 else (KD * D, D)
                dve.wait_ge(s_wraw[L], s * 32 + 32)
                if after is not None:
                    dve.wait_ge(s_yfree[L], TPC + after)
                nc.vector.tensor_copy(W1h[:, buf, 0:n1], W1r[:, 0:n1]).then_inc(s_whi[L], 1)
                nc.vector.tensor_copy(W2h[:, buf, 0:n2], W2r[:, 0:n2]).then_inc(s_whi[L], 1)
                dve.wait_ge(s_whi[L], s * 2 + 1)
                lo(W1l[:, buf, 0:n1], W1r[:, 0:n1], W1h[:, buf, 0:n1])
                dve.wait_ge(s_whi[L], s * 2 + 2)
                lo(W2l[:, buf, 0:n2], W2r[:, 0:n2], W2h[:, buf, 0:n2]).then_inc(s_wsplit[L], 1)

            def softmax(L, E, meanwhile=None):
                lg = SC[:, 0, 0:NT * E].rearrange("p (t e) -> p t e", e=E)
                pr = SC[:, 1, 0:NT * E].rearrange("p (t e) -> p t e", e=E)
                ps = PS[:, 4, 0:NT * E].rearrange("p (t e) -> p t e", e=E)
                dve.wait_ge(s_lg, L + 1)
                if L < 2:
                    link(nc.vector.tensor_tensor(lg, ps, BR[L][:].unsqueeze(1).broadcast_to([P, NT, E]), ALU.add))
                else:
                    link(nc.vector.tensor_copy(lg, ps))
                link(nc.vector.tensor_reduce(SM[:, 5, :], lg, axis=AX.X, op=ALU.max))
                nc.vector.tensor_tensor(lg, lg, SM[:, 5, :].unsqueeze(2).broadcast_to([P, NT, E]),
                                        ALU.subtract).then_inc(s_sub, 1)
                if meanwhile:
                    dve.wait_ge(s_sub, L + 1)
                    meanwhile(lg)
                dve.wait_ge(s_exp, L + 1)
                link(nc.vector.tensor_reduce(SM[:, 6, :], pr, axis=AX.X, op=ALU.add))
                link(nc.vector.reciprocal(SM[:, 7, :], SM[:, 6, :]))
                return lg, pr

            def bc(col, E):
                return col.unsqueeze(2).broadcast_to([P, NT, E])

            def running(E):
                link(nc.vector.memset(RS, 1.0))
                link(nc.vector.memset(RS.rearrange("p (t e) -> p t e", e=E)[:, :, 0:1], 0.0))
                link(nc.vector.tensor_tensor_scan(SC[:, 3, 0:NT * E], RS[:, 0:NT * E], SC[:, 2, 0:NT * E],
                                                  0.0, ALU.mult, ALU.add))

            def top1(L):
                eq = SC[:, 2, 0:NT * 8].rearrange("p (t e) -> p t e", e=8)
                run = SC[:, 3, 0:NT * 8].rearrange("p (t e) -> p t e", e=8)

                def choose(lg):
                    link(nc.vector.tensor_single_scalar(eq, lg, 0.0, ALU.is_equal))
                    running(8)
                    link(nc.vector.scalar_tensor_tensor(run, run, 1.0, eq, ALU.is_equal, ALU.mult))
                    dve.sem_inc(s_oh, 1)

                lg, pr = softmax(L, 8, choose)
                link(nc.vector.tensor_tensor(pr, pr, bc(SM[:, 7, :], 8), ALU.mult))
                nc.vector.tensor_tensor(G[:, :, 0:8], run, pr, ALU.mult).then_inc(s_gate, 1)

            def order(L):
                ET = 8 * NT
                pick = SC[:, 3, 0:ET].rearrange("p (t e) -> p t e", e=8)
                tot, cum, off = (SC[:, 0, k * ET:(k + 1) * ET] for k in range(3))
                et = "p (e t) -> p e t"
                tmp = SC[:, 2, 0:ET].rearrange("p (t e) -> p t e", e=8)
                cmp = SC[:, 2, ET:ET + 64].rearrange("p (e k) -> p e k", k=8)
                own, upto, even = (SC[:, 2, 256 + 8 * k:264 + 8 * k] for k in range(3))
                dve.wait_ge(s_rank, L + 1)
                link(nc.vector.tensor_copy(tot.rearrange(et, e=8),
                                           PS[:, 5, ET:2 * ET].rearrange("p (t e) -> p e t", e=8)))
                link(nc.vector.tensor_tensor_scan(cum, RS16[:], tot, 0.0, ALU.mult, ALU.add))
                count = cum.rearrange(et, e=8)[:, :, NT - 1:NT]
                link(nc.vector.tensor_scalar(even, IO[:, 0:8], float(BT), None, ALU.mult))
                link(nc.vector.tensor_tensor(cmp, count.broadcast_to([P, 8, 8]),
                                             even.unsqueeze(1).broadcast_to([P, 8, 8]), ALU.is_gt))
                link(nc.vector.tensor_reduce(own, cmp, axis=AX.X, op=ALU.add))
                link(nc.vector.tensor_tensor_scan(upto, ONE[:, 0:8], own, 0.0, ALU.mult, ALU.add))
                link(nc.vector.tensor_tensor(own, upto, own, ALU.subtract))
                link(nc.vector.tensor_tensor(off, cum, tot, ALU.subtract))
                link(nc.vector.scalar_tensor_tensor(off.rearrange(et, e=8), own.unsqueeze(2).broadcast_to([P, 8, NT]),
                                                    float(BT), off.rearrange(et, e=8), ALU.mult, ALU.add))
                link(nc.vector.tensor_tensor(tmp, PS[:, 5, 0:ET].rearrange("p (t e) -> p t e", e=8),
                                             off.rearrange("p (e t) -> p t e", e=8), ALU.add))
                link(nc.vector.tensor_tensor(tmp, tmp, pick, ALU.mult))
                link(nc.vector.tensor_reduce(SLOTf[:], tmp, axis=AX.X, op=ALU.add))
                link(nc.vector.tensor_scalar(SLOTf[:], SLOTf[:], -1.0, None, ALU.add))
                link(nc.vector.tensor_copy(SLOT[:], SLOTf[:]))
                dve.sem_inc(s_slot, 1)
                hit = SC[0:1, 2, 288:288 + BLOCKS * 8].rearrange("p (b e) -> p b e", e=8)
                exp = SC[0:1, 2, 424:424 + BLOCKS]
                link(nc.vector.tensor_tensor(hit, upto[0:1].unsqueeze(1).broadcast_to([1, BLOCKS, 8]),
                                             IO[0:1, 0:BLOCKS].unsqueeze(2).broadcast_to([1, BLOCKS, 8]), ALU.is_le))
                link(nc.vector.tensor_reduce(exp, hit, axis=AX.X, op=ALU.add))
                link(nc.vector.tensor_scalar(exp, exp, 7.0, None, ALU.min))
                link(nc.vector.tensor_copy(BLK[L][:, 0:BLOCKS], exp))
                link(nc.vector.tensor_scalar(even[0:1], IO[0:1, 0:8], 2.0, None, ALU.mult))
                link(nc.vector.tensor_scalar(even[0:1], even[0:1], upto[0:1, 7:8], None, ALU.is_lt))
                link(nc.vector.tensor_reduce(exp[:, 0:1], even[0:1], axis=AX.X, op=ALU.add))
                nc.vector.tensor_copy(BLK[L][:, 63:64], exp[:, 0:1]).then_inc(s_list, 1)
                dve.wait_ge(s_gate, SPARSE[L] + 1)
                link(nc.vector.tensor_reduce(SM[:, 1, :], G[:, :, 0:8], axis=AX.X, op=ALU.add))

            def blocks(L):
                NF = LAYERS[SPARSE[L]][1] // P
                N1, N2 = KD * NF * P, NF * D
                dve.wait_ge(s_list, L + 1)
                steps = dve.value_load(BLK[L][0:1, 63:64], min_val=1, max_val=STEPS)

                def w1_lo(q, k):
                    dve.wait_ge(s_w1hi[L], q + 1)
                    lo(WB1l[:, k, 0:N1], ZW[k][0][:, 0:N1], WB1h[:, k, 0:N1]).then_inc(s_w1sp[L], 1)

                def w2_split(i, k):
                    q = i * 2 + k
                    dve.wait_ge(s_w2raw[L][k], i * 16 + 16)
                    nc.vector.tensor_copy(WB2h[:, k, 0:N2], ZW[k][1][:, 0:N2]).then_inc(s_w2hi[L], 1)
                    dve.wait_ge(s_w2hi[L], q + 1)
                    lo(WB2l[:, k, 0:N2], ZW[k][1][:, 0:N2], WB2h[:, k, 0:N2]).then_inc(s_w2sp[L], 1)

                def x_lo(q, k):
                    dve.wait_ge(s_xhi[L], q + 1)
                    lo(XTl[:, k].rearrange("p k n -> p (k n)"), PS[:, 6 + k, :],
                       XTh[:, k].rearrange("p k n -> p (k n)")).then_inc(s_xlo[L], 1)

                def lows(q, k):
                    for f in range(NF // 2):
                        dve.wait_ge(s_hhi[SPARSE[L]], NF * q + 2 * f + 2)
                        lo(HTl[:, k, f, :], HF[:, f, :], HTh[:, k, f, :]).then_inc(s_hlo[SPARSE[L]], 1)

                def outputs(q, k):
                    dve.wait_ge(s_yb[L], q + 1)
                    for j in range(BTT):
                        dve.wait_ge(s_y[SPARSE[L]], BTT * q + j + 1)
                        nc.vector.tensor_copy(YB[:, k, j, :], PS[:, 4 + j, 0:D]).then_inc(s_yev[L], 1)

                dve.sem_inc(s_yev[L], BTT)
                w1_lo(0, 0)
                x_lo(0, 0)
                w2_split(0, 0)
                lows(0, 0)
                w1_lo(1, 1)
                x_lo(1, 1)
                with dve.Fori(0, STEPS) as i:
                    with dve.If(i + 1 < steps):
                        w1_lo(i * 2 + 2, 0)
                    with dve.If(i < steps):
                        w2_split(i, 1)
                        lows(i * 2 + 1, 1)
                    with dve.If(i + 1 < steps):
                        x_lo(i * 2 + 2, 0)
                    with dve.If(i < steps):
                        outputs(i * 2, 0)
                    with dve.If(i + 1 < steps):
                        w1_lo(i * 2 + 3, 1)
                        w2_split(i + 1, 0)
                        lows(i * 2 + 2, 0)
                        x_lo(i * 2 + 3, 1)
                    with dve.If(i < steps):
                        outputs(i * 2 + 1, 1)
            def add_back(L, n0, dh, dl):
                for c in range(NC + 1):
                    if c < NC:
                        dve.wait_ge(s_gath[c], 16 * TPC * (L + 1))
                        for n in range(c * TPC, (c + 1) * TPC):
                            nc.vector.scalar_tensor_tensor(X[:, n, :], Z[:, n, :], SM[:, 1, n:n + 1], X[:, n, :],
                                                           ALU.mult, ALU.add).then_inc(s_add, 1)
                    if c:
                        transposes(n0, dh, dl, c - 1)

            def bias(L):
                for n in range(NT):
                    dve.wait_ge(s_by, NT * L + n + 1)
                    nc.vector.tensor_tensor(X[:, n, :], PS[:, 4 + n % 4, 0:D], X[:, n, :], ALU.add).then_inc(s_bu, 1)

            def ffn(L, gates):
                def lows(i, u, first=False):
                    for f in range(FB):
                        dve.wait_ge(s_hhi[L], f + 1 if first else FB * (i * UPI + u) + f + 1)
                        lo(HTl[:, u % 2, f, :], HF[:, f, :], HTh[:, u % 2, f, :]).then_inc(s_hlo[L], 1)

                def gated(i, u):
                    c = u % NC
                    e = i
                    for j in range(TPC):
                        n = c * TPC + j
                        dve.wait_ge(s_y[L], TPC * (i * UPI + u) + j + 1)
                        nc.vector.scalar_tensor_tensor(X[:, n, :], PS[:, 4 + j, 0:D], G[:, n, bass.ds(e, 1)],
                                                       X[:, n, :], ALU.mult, ALU.add).then_inc(s_yfree[L], 1)

                def step(i, final):
                    for u in range(UPI):
                        if not (final and u == UPI - 1):
                            lows(i, u + 1)
                        gated(i, u)
                        if u == 0:
                            split_into(L, 1, i * 2 + 1, TPC * UPI * i)
                        if u == 4 and not final:
                            split_into(L, 0, i * 2 + 2, TPC * (UPI * i + NC))

                dve.sem_inc(s_yfree[L], TPC)
                lows(0, 0, True)
                gates()
                steps = NSUB[L] // 2
                with dve.Fori(0, steps - 1) as i:
                    step(i, False)
                step(steps - 1, True)

            def ffn3():
                def mid(i, u):
                    dve.wait_ge(s_hf3, i * UPI + u + 1)
                    dve.wait_ge(s_hps[3], 2 * (i * UPI + u) + 2)
                    nc.vector.tensor_tensor(HF[:, 2 + u % 2, :], HF[:, u % 2, :], PS[:, 2 * (u % 2) + 1, :],
                                            ALU.mult).then_inc(s_hm3, 1)
                    dve.wait_ge(s_hhi[3], i * UPI + u + 1)
                    lo(HTl[:, u % 2, 0, :], HF[:, 2 + u % 2, :], HTh[:, u % 2, 0, :]).then_inc(s_hlo[3], 1)

                def gated(i, u, e):
                    c = u % NC
                    for j in range(TPC):
                        n = c * TPC + j
                        dve.wait_ge(s_y[3], TPC * (i * UPI + u) + j + 1)
                        nc.vector.scalar_tensor_tensor(X[:, n, :], PS[:, 4 + j, 0:D], G[:, n, bass.ds(e, 1)],
                                                       X[:, n, :], ALU.mult, ALU.add).then_inc(s_yfree[3], 1)

                split_into(3, 0, 0, None)
                dve.sem_inc(s_yfree[3], YC)
                dve.sem_inc(s_hm3, 2)
                link(nc.vector.memset(G[:, :, E3:E3S], 1.0))
                link(nc.vector.memset(G[:, :, E3S:E3S + 1], 0.0))
                lg, pr = softmax(3, E3)
                link(nc.vector.tensor_tensor(pr, pr, bc(SM[:, 7, :], E3), ALU.mult))
                link(nc.vector.tensor_tensor(lg, pr, BR[3][:].unsqueeze(1).broadcast_to([P, NT, E3]), ALU.add))
                mid(0, 0)
                for n in range(NT):
                    last = nc.vector.max(SC[:, 4, n * 8:(n + 1) * 8], lg[:, n, :])
                link(last)
                mid(0, 1)
                gated(0, 0, E3)
                split_into(3, 1, 1, YC - TPC)
                bar = SC[:, 4, 0:NT * 8].rearrange("p (t e) -> p t e", e=8)[:, :, TOP_K - 1:TOP_K].broadcast_to([P, NT, E3])
                eq = SC[:, 2, :].rearrange("p (t e) -> p t e", e=E3)
                run = SC[:, 3, :].rearrange("p (t e) -> p t e", e=E3)
                gt = SC[:, 5, :].rearrange("p (t e) -> p t e", e=E3)
                nc.vector.tensor_tensor(gt, lg, bar, ALU.is_gt)
                link(nc.vector.tensor_tensor(eq, lg, bar, ALU.is_equal))
                link(nc.vector.tensor_reduce(SM[:, 5, :], gt, axis=AX.X, op=ALU.add))
                running(E3)
                link(nc.vector.tensor_tensor(run, run, bc(SM[:, 5, :], E3), ALU.add))
                link(nc.vector.scalar_tensor_tensor(run, run, float(TOP_K), eq, ALU.is_le, ALU.mult))
                link(nc.vector.tensor_tensor(run, run, gt, ALU.add))
                nc.vector.tensor_reduce(SC[:, 6, 0:E3], run.rearrange("p t e -> p e t"), axis=AX.X,
                                        op=ALU.add).then_inc(s_cnt3, 1)
                dve.wait_ge(s_cnt3, 1)
                mid(0, 2)
                gated(0, 1, E3)
                link(nc.vector.tensor_tensor(run, run, pr, ALU.mult))
                link(nc.vector.tensor_reduce(SM[:, 5, :], run, axis=AX.X, op=ALU.add))
                link(nc.vector.tensor_scalar(SM[:, 6, :], SM[:, 5, :], 1e-12, None, ALU.max))
                link(nc.vector.reciprocal(SM[:, 7, :], SM[:, 6, :]))
                link(nc.vector.tensor_tensor(G[:, :, 0:E3], run, bc(SM[:, 7, :], E3), ALU.mult))
                mid(0, 3)
                gated(0, 2, E3)
                mid(0, 4)
                gated(0, 3, E3)
                used, place, val = (SC[0:1, 7, 64 * k:64 * k + E3] for k in range(3))
                wl, gl, inuse = (SC[0:1, 7, 192 + 64 * k:192 + 64 * k + E3S] for k in range(3))
                num = SC[0:1, 7, 384:385]
                hit = Z[0:1, 0:5, :].rearrange("p a c -> p (a c)")[:, 0:E3S * E3].rearrange("p (i e) -> p i e", e=E3)
                dve.wait_ge(s_cnt3p, 1)
                link(nc.vector.tensor_single_scalar(used, PS[0:1, 5, 0:E3], 0.0, ALU.is_gt))
                dve.sem_inc(s_used3, 1)
                link(nc.vector.tensor_tensor_scan(place, ONE[0:1, 0:E3], used, 0.0, ALU.mult, ALU.add))
                link(nc.vector.tensor_scalar(num, place[:, E3 - 1:E3], 2.0, None, ALU.add))
                link(nc.vector.tensor_tensor(place, place, used, ALU.subtract))
                link(nc.vector.tensor_scalar(place, place, 2.0, None, ALU.add))
                link(nc.vector.tensor_tensor(val, used, IO[0:1, 0:E3], ALU.mult))
                link(nc.vector.tensor_tensor(hit, IO[0:1, 0:E3S].unsqueeze(2).broadcast_to([1, E3S, E3]),
                                             place.unsqueeze(1).broadcast_to([1, E3S, E3]), ALU.is_equal))
                link(nc.vector.tensor_tensor(hit, hit, val.unsqueeze(1).broadcast_to([1, E3S, E3]), ALU.mult))
                link(nc.vector.tensor_reduce(wl, hit, axis=AX.X, op=ALU.add))
                link(nc.vector.tensor_scalar(wl[:, 0:2], IO[0:1, 0:2], float(E3), None, ALU.add))
                mid(0, 5)
                gated(0, 4, E3 + 1)
                link(nc.vector.tensor_scalar(inuse, IO[0:1, 0:E3S], num, float(E3S), ALU.is_ge, ALU.mult))
                link(nc.vector.tensor_tensor(gl, wl, inuse, ALU.max))
                link(nc.vector.tensor_copy(L3W[:, 0:E3S], wl))
                link(nc.vector.tensor_copy(L3G[:, 0:E3S], gl))
                link(nc.vector.tensor_scalar(val[:, 0:STEPS3], IO[0:1, 0:STEPS3], 2.0, None, ALU.mult))
                link(nc.vector.tensor_scalar(val[:, 0:STEPS3], val[:, 0:STEPS3], num, None, ALU.is_lt))
                link(nc.vector.tensor_reduce(num, val[:, 0:STEPS3], axis=AX.X, op=ALU.add))
                nc.vector.tensor_copy(L3G[:, 63:64], num).then_inc(s_list3, 1)
                mid(0, 6)
                gated(0, 5, E3 + 1)
                mid(0, 7)
                split_into(3, 0, 2, YC - TPC + TPC * NC)
                gated(0, 6, E3 + 1)
                gated(0, 7, E3 + 1)
                mid(0, UPI)
                dve.wait_ge(s_list3, 1)
                steps = dve.value_load(L3G[0:1, 63:64], min_val=1, max_val=STEPS3)
                with dve.Fori(1, STEPS3) as i:
                    with dve.If(i < steps):
                        for s in range(2):
                            e = dve.value_load(L3G[0:1, bass.ds(i * 2 + s, 1)], min_val=0, max_val=E3S)
                            for u in range(s * NC, (s + 1) * NC):
                                if u < UPI - 1:
                                    mid(i, u + 1)
                                else:
                                    with dve.If(i + 1 < steps):
                                        mid(i, UPI)
                                gated(i, u, e)
                                if u == 0:
                                    split_into(3, 1, i * 2 + 1, YC - TPC + TPC * UPI * i)
                                if u == NC:
                                    with dve.If(i + 1 < steps):
                                        split_into(3, 0, i * 2 + 2, YC - TPC + TPC * (UPI * i + NC))

            dve.wait_ge(s_const, 7)
            link(nc.vector.tensor_copy(IO[:], IOi[:]))
            link(nc.vector.memset(RS16[:], 1.0))
            link(nc.vector.memset(RS16[:].rearrange("p (e t) -> p e t", t=NT)[:, :, 0:1], 0.0))
            cond_split(0, 2 * B, [(P, slice(0, 256)), (A0, slice(256, 256 + B * D))])
            transposes("x0", TAh, TAl)

            def adapter_lo(c):
                dve.wait_ge(s_chi[0], c + 1)
                lo(HTl[0:A0, c % 2, 0, :], HF[0:A0, 3, :], HTh[0:A0, c % 2, 0, :]).then_inc(s_clo[0], 1)

            def variances(b):
                bs = slice(b * TPB, (b + 1) * TPB)
                dve.wait_ge(s_aggr, (b + 1) * TPB)
                nc.vector.tensor_scalar(SM[:, 0, bs], MV[:, bs, 1], LN_EPS, None, ALU.add).then_inc(s_var, 1)

            def norm(b):
                bs = slice(b * TPB, (b + 1) * TPB)
                dve.wait_ge(s_std, b + 1)
                link(nc.vector.reciprocal(SM[:, 1, bs], SM[:, 0, bs]))
                for n in range(b * TPB, (b + 1) * TPB):
                    nc.vector.tensor_scalar(Z[:, n, :], Z[:, n, :], MV[:, n, 0:1], SM[:, 1, n:n + 1],
                                            ALU.subtract, ALU.mult).then_inc(s_norm, 1)

            adapter_lo(0)
            for n in range(NT + 2):
                if n < NT:
                    dve.wait_ge(s_cy, n + 1)
                    dve.wait_ge(s_xb2, n + 1)
                    nc.vector.tensor_tensor(Z[:, n, :], PS[:, 6 + n % 2, 0:D], Z[:, n, :], ALU.add).then_inc(s_cyf, 1)
                if 1 <= n <= NT:
                    dve.wait_ge(s_cyf, n)
                    if n >= 3:
                        dve.wait_ge(s_aggr, n - 2)
                    nc.vector.bn_stats(ST[:, (n - 1) % 2, :], Z[:, n - 1, :]).then_inc(s_stat, 1)
                if n >= 2:
                    dve.wait_ge(s_stat, n - 1)
                    nc.vector.bn_aggr(MV[:, n - 2, :], ST[:, n % 2, :]).then_inc(s_aggr, 1)
                if n == TPB + 1:
                    variances(0)
                if n % TPC == 1 and n // TPC + 1 < NC:
                    adapter_lo(n // TPC + 1)
                if n == TPB + TPC:
                    norm(0)
            variances(1)
            dve.wait_ge(s_small, 16 * N_SMALL)
            for L in range(4):
                link(nc.vector.tensor_copy(Rh[L][:], Rr[L][:]))
                lo(Rl[L][:], Rr[L][:], Rh[L][:]).then_inc(s_rsplit, 1)
            split_into(0, 0, 0, None)
            norm(1)
            transposes("z0", TBhv, TBlv)
            dve.wait_ge(s_zst, 16 * 2 * BLOCKS * BT // (P * NT))
            lg, pr = softmax(0, 8)
            link(nc.vector.tensor_tensor(pr, pr, bc(SM[:, 7, :], 8), ALU.mult))
            before = SC[:, 2, 0:NT * 8].rearrange("p (t e) -> p t e", e=8)
            term = SC[:, 3, 0:NT * 8].rearrange("p (t e) -> p t e", e=8)
            link(nc.vector.memset(before, 0.0))
            for j in range(8):
                pj = pr[:, :, j:j + 1]
                if j:
                    nc.vector.tensor_tensor(term[:, :, 0:j], pr[:, :, 0:j], pj.broadcast_to([P, NT, j]), ALU.is_lt)
                if j < 7:
                    nc.vector.tensor_tensor(term[:, :, j + 1:8], pr[:, :, j + 1:8],
                                            pj.broadcast_to([P, NT, 7 - j]), ALU.is_le)
                link(nc.vector.memset(term[:, :, j:j + 1], 0.0))
                link(nc.vector.tensor_tensor(term, term, pj.broadcast_to([P, NT, 8]), ALU.mult))
                link(nc.vector.tensor_tensor(before, before, term, ALU.add))
            link(nc.vector.tensor_tensor(term, before, pr, ALU.add))
            link(nc.vector.tensor_single_scalar(term, term, TOP_P, ALU.is_lt))
            link(nc.vector.scalar_tensor_tensor(term, before, 0.0, term, ALU.is_equal, ALU.max))
            nc.vector.tensor_tensor(G[:, :, 0:8], term, pr, ALU.mult).then_inc(s_gate, 1)
            ffn(0, lambda: bias(0))
            cond_split(1, 1, [(P, slice(0, KD * A0))])
            link(nc.vector.tensor_copy(SC[0:A0, 7, 0:P], V1[:].broadcast_to([A0, P])))
            dve.sem_inc(s_clo[1], 1)
            transposes("x1", TAh, TAl)
            nc.vector.tensor_copy(XRh[:, :, D:D + 2], ONE[:, 0:2].unsqueeze(1).broadcast_to([P, NT, 2]))
            link(nc.vector.tensor_scalar(XRl[:, :, D:D + 2], ONE[:, 0:2].unsqueeze(1).broadcast_to([P, NT, 2]),
                                         0.0, None, ALU.mult))
            dve.sem_inc(s_xr, 1)

            def pool_rhs(n):
                dve.wait_ge(s_act, n + 1)
                lo(XRl[:, n, 0:D], X[:, n, :], XRh[:, n, 0:D]).then_inc(s_xr, 1)

            for n in range(TPB):
                pool_rhs(n)
            dve.wait_ge(s_mode, 16)
            link(nc.vector.tensor_copy(MD[:, :, 7], MODEi[:]))
            nc.vector.tensor_single_scalar(MD[:, :, 0], MD[:, :, 7], 0.0, ALU.is_equal)
            link(nc.vector.tensor_single_scalar(MD[:, :, 1], MD[:, :, 7], 1.0, ALU.is_equal))
            link(nc.vector.tensor_tensor(MD[:, :, 6], MD[:, :, 0], MD[:, :, 1], ALU.add))
            link(nc.vector.tensor_scalar(MD[:, :, 2], MD[:, :, 6], -1.0, 1.0, ALU.mult, ALU.add))
            link(nc.vector.tensor_scalar(MD[:, :, 8:11], MD[:, :, 0:3], -1.0, None, ALU.mult))
            nc.vector.tensor_scalar(MD[:, :, 3], MD[:, :, 0], NEG, None, ALU.mult)
            link(nc.vector.tensor_scalar(MD[:, :, 4], MD[:, :, 1], NEG, None, ALU.mult))
            link(nc.vector.tensor_copy(JC[:], JCi[:]))
            for b in range(B):
                m = [MD[:, b, k:k + 1] for k in range(8)]
                link(nc.vector.tensor_scalar(DM[:, b, :], TM[:, 0, :], m[0], None, ALU.mult))
                link(nc.vector.scalar_tensor_tensor(DM[:, b, :], TM[:, 1, :], m[1], DM[:, b, :], ALU.mult, ALU.add))
                link(nc.vector.scalar_tensor_tensor(DM[:, b, :], TM[:, 2, :], m[2], DM[:, b, :], ALU.mult, ALU.add))
                link(nc.vector.tensor_scalar(DM[:, b, :], DM[:, b, :], -NEG, NEG, ALU.mult, ALU.add))
                cnt = SM[:, 3, b * TPB:(b + 1) * TPB]
                tmp = SM[:, 4, b * TPB:(b + 1) * TPB]
                link(nc.vector.tensor_scalar(tmp, JC[:], 1.0, None, ALU.add))
                link(nc.vector.tensor_scalar(cnt, tmp, m[0], None, ALU.mult))
                link(nc.vector.tensor_scalar(tmp, JC[:], -1.0, float(SEQ), ALU.mult, ALU.add))
                link(nc.vector.scalar_tensor_tensor(cnt, tmp, m[1], cnt, ALU.mult, ALU.add))
                link(nc.vector.memset(tmp, float(SEQ - 1)))
                link(nc.vector.scalar_tensor_tensor(cnt, tmp, m[2], cnt, ALU.mult, ALU.add))
            dve.wait_ge(s_sc_sb, 1)

            def row_maxima(b, part):
                m = [MD[:, b, k:k + 1] for k in range(11)]
                cols = SM[:, 0, b * TPB:(b + 1) * TPB]
                row = SC[:, 2 * b:2 * b + 2, :].rearrange("p a c -> p (a c)")
                pre, suf, oth = (t[:].rearrange("p a c -> p (a c)") for t in
                                 (Z[:, 8:12], Z[:, 12:16], Z[:, 0:4] if b == 0 else MX3))
                if part == 0:
                    nc.vector.tensor_scalar(SM[:, 5, b * TPB:(b + 1) * TPB], cols, m[3], None, ALU.add)
                    nc.vector.tensor_scalar(SM[:, 6, b * TPB:(b + 1) * TPB], cols, m[4], None, ALU.add)
                    link(nc.vector.tensor_tensor_scan(pre, row, row, -3e38, ALU.max, ALU.max))
                if part == 1:
                    link(nc.vector.tensor_tensor_scan(suf[:, ::-1], row[:, ::-1], row[:, ::-1], -3e38, ALU.max, ALU.max))
                if part == 2:
                    nc.vector.tensor_tensor(oth[:, 1:SEQ - 1], pre[:, 0:SEQ - 2], suf[:, 2:SEQ], ALU.max)
                    nc.vector.tensor_copy(oth[:, 0:1], suf[:, 1:2])
                    nc.vector.tensor_copy(oth[:, SEQ - 1:SEQ], pre[:, SEQ - 2:SEQ - 1])
                if part == 3:
                    link(nc.vector.tensor_scalar(row, pre, m[8], None, ALU.mult))
                    link(nc.vector.scalar_tensor_tensor(row, suf, m[9], row, ALU.mult, ALU.add))
                if part == 4:
                    link(nc.vector.scalar_tensor_tensor(row, oth, m[10], row, ALU.mult, ALU.add))

            for part in range(5):
                row_maxima(0, part)
            for b in range(B):
                cols = SM[:, 0, b * TPB:(b + 1) * TPB]
                sl = SM[:, 5, b * TPB:(b + 1) * TPB]
                su = SM[:, 6, b * TPB:(b + 1) * TPB]
                row = SC[:, 2 * b:2 * b + 2, :].rearrange("p a c -> p (a c)")
                for lb in range(TPB):
                    q = b * TPB + lb
                    if q >= 2:
                        dve.wait_ge(s_phi, q - 1)
                    arg = SC[:, 4 + 2 * (q % 2):6 + 2 * (q % 2), :].rearrange("p a c -> p (a c)")
                    diag = slice(lb * P, (lb + 1) * P)
                    if lb:
                        nc.vector.tensor_scalar(arg[:, 0:lb * P], row[:, 0:lb * P], sl[:, lb:lb + 1], 0.0,
                                                ALU.add, ALU.min)
                    if lb < TPB - 1:
                        nc.vector.tensor_scalar(arg[:, (lb + 1) * P:], row[:, (lb + 1) * P:], su[:, lb:lb + 1], 0.0,
                                                ALU.add, ALU.min)
                    link(nc.vector.tensor_scalar(arg[:, diag], row[:, diag], cols[:, lb:lb + 1], 0.0,
                                                 ALU.add, ALU.min))
                    nc.vector.tensor_tensor(arg[:, diag], arg[:, diag], DM[:, b, :], ALU.add).then_inc(s_arg, 1)
                    if b == 0:
                        pool_rhs(TPB + lb)
                        if lb < 5:
                            row_maxima(1, lb)
                    if lb:
                        pooled_lo = q - 1
                        dve.wait_ge(s_phi, pooled_lo + 1)
                        lo(HTl[:, pooled_lo % 2, 0:2, :], HF[:, 2 * (pooled_lo % 2):2 * (pooled_lo % 2) + 2, :],
                           HTh[:, pooled_lo % 2, 0:2, :]).then_inc(s_plo, 1)
                q = b * TPB + TPB - 1
                dve.wait_ge(s_phi, q + 1)
                lo(HTl[:, q % 2, 0:2, :], HF[:, 2 * (q % 2):2 * (q % 2) + 2, :], HTh[:, q % 2, 0:2, :]).then_inc(s_plo, 1)
                dve.wait_ge(s_pmm, q + 1)
                bs = slice(b * TPB, (b + 1) * TPB)
                link(nc.vector.tensor_tensor(SM[:, 4, bs], PS[:, :, D], SM[:, 3, bs], ALU.mult))
                nc.vector.reciprocal(SM[:, 2, bs], SM[:, 4, bs]).then_inc(s_den, 1)
            transposes("z1", TAh, TAl)
            top1(1)
            order(0)
            bias(1)
            blocks(0)

            def linear_cond(L):
                cond_split(L, B, [(P, slice(0, B * KD * D))])
                add_back(1, f"x{L}", TBhv, TBlv)
                for g in range(KD * NC):
                    c, m = g // KD, g % KD
                    dve.wait_ge(s_chi[L], g + 1)
                    lo(TAl[:, m, c * CH:(c + 1) * CH], HF[:, g % 4, :], TAh[:, m, c * CH:(c + 1) * CH]).then_inc(s_clo[L], 1)

            link(nc.vector.tensor_tensor(WG[:, GR:2 * GR], WG[:, 0:GR], WG[:, 0:GR], ALU.mult))
            nc.vector.tensor_reduce(SM[0:8, 4, 0:1], WG[:, GR:2 * GR], axis=AX.X, op=ALU.add).then_inc(s_ss, 1)
            cond_split(2, B, [(P, slice(0, B * KD * D))])
            add_back(0, "x2", TBhv, TBlv)
            dve.wait_ge(s_row, 16 * B)
            for n in range(NT):
                dve.wait_ge(s_c2y, n + 1)
                b = n // TPB
                nc.vector.tensor_tensor(Z[:, n, :], PS[:, 4 + n % 4, 0:D], W2r[:, b * D:(b + 1) * D],
                                        ALU.add).then_inc(s_z2, 1)
            transposes("z2", TAh, TAl)
            dve.wait_ge(s_sq, 1)
            link(nc.vector.tensor_scalar(SM[0:8, 4, 1:2], SM[0:8, 4, 0:1], 1e-4, None, ALU.max))
            link(nc.vector.reciprocal(SM[0:8, 4, 2:3], SM[0:8, 4, 1:2]))
            nc.vector.tensor_scalar(WG[:, 2 * GR:3 * GR], WG[:, 0:GR], SM[0:8, 4, 2:3], None, ALU.mult).then_inc(s_wgn, 1)
            dve.wait_ge(s_wgt, 1)
            nc.vector.tensor_copy(WGT[:], PS[0:GR, 5, 0:8]).then_inc(s_wgs, 1)
            top1(2)
            order(1)
            bias(2)
            blocks(1)
            linear_cond(3)
            ffn3()


def kernel(**inputs):
    import numpy as np
    import concourse.bacc as bacc
    from concourse.bass_utils import run_bass_kernel_spmd

    a = {k: np.asarray(v) for k, v in inputs.items()}
    ins = {n: a[n] for n in (
        "x", "L0_cond_b1", "L0_cond_W1", "L0_cond_W2", "L0_cond_b2", "L0_cond_gamma", "L0_cond_beta", "L0_ffn_Wr", "L0_ffn_br",
        "L0_ffn_b2", "L1_cond_W1", "L1_cond_b1", "L1_cond_v", "L1_ffn_Wr", "L1_ffn_br", "L1_ffn_b2", "L2_cond_W", "L2_cond_b",
        "L2_ffn_w_red", "L2_ffn_wg", "L2_ffn_b2", "L3_cond_weight", "L3_ffn_e_score_bias")}
    ins["ids"] = np.concatenate([a["itok_B_0_8"], a["itok_B_0_2"], a["itok_B_0_30"], a["itok_B_0_15"]]).reshape(1, 8)
    ins["L1_mode"] = a["itok_B_0_2"]
    ins["L3_router_t"] = a["L3_ffn_router_weight"].T
    ins["L3_cond_b"] = a["L3_cond_bias"].reshape(-1, KD, P).transpose(2, 0, 1)
    for L, (E, F, _) in enumerate(LAYERS):
        w1, w2 = a[f"L{L}_ffn_W1"], a[f"L{L}_ffn_W2"]
        if L in SPARSE:
            ins[f"L{L}_w1"] = w1.reshape(E, KD, P, F).transpose(0, 2, 1, 3).reshape(E, P, KD * F)
            ins[f"L{L}_w2"] = w2.reshape(E, F // P, P, D).transpose(0, 2, 1, 3).reshape(E, P, F // P * D)
            ins[f"L{L}_b1_t"] = a[f"L{L}_ffn_b1"].reshape(E * F // P, P).T
            continue
        ins[f"L{L}_w1"] = w1.reshape(E, KD, P, F // SUB, SUB).transpose(0, 3, 2, 1, 4).reshape(-1, P, KD * SUB)
        ins[f"L{L}_w2"] = w2.reshape(E, F // SUB, FB, P, D).transpose(0, 1, 3, 2, 4).reshape(-1, P, FB * D)
        ins[f"L{L}_b1_t"] = a[f"L{L}_ffn_b1"].reshape(E * F // P, P).T
    I3 = 128
    gate_up, down = a["L3_ffn_gate_up_proj"], a["L3_ffn_down_proj"]
    sg, su, sd = (a[f"L3_ffn_shared_{n}_w"] for n in ("gate", "up", "down"))
    halves = [np.concatenate([sg[h * I3:(h + 1) * I3], su[h * I3:(h + 1) * I3]]) for h in range(2)]
    gu = np.concatenate([gate_up, np.stack(halves)])
    ins["L3_w1"] = gu.transpose(0, 2, 1).reshape(E3S, KD, P, 2 * I3).transpose(0, 2, 1, 3).reshape(E3S, P, KD * 2 * I3)
    dn = np.concatenate([down, np.stack([sd[:, h * I3:(h + 1) * I3] for h in range(2)])])
    ins["L3_w2"] = dn.transpose(0, 2, 1)

    nc = bacc.Bacc("TRN2", target_bir_lowering=False, num_devices=1)
    arrays, tensors = {}, {}
    for name, v in ins.items():
        arrays[f"in_{name}"] = np.ascontiguousarray(v)
        tensors[name] = nc.dram_tensor(f"in_{name}", v.shape, mybir.dt.from_np(v.dtype), kind="ExternalInput").ap()
    tensors["out"] = nc.dram_tensor("out_x", (B, SEQ, D), F32, kind="ExternalOutput").ap()
    build(nc, tensors)
    r = run_bass_kernel_spmd(nc, [arrays], core_ids=[0])
    return r.results[0]["out_x"]
```
